# Optimizing a Trainium2 kernel written in Bass

```python
import numpy as np
import jax
import jax.numpy as jnp

def _softmax(x, axis=-1):
    return jax.nn.softmax(x, axis=axis)

def _gelu(x):
    return jax.nn.gelu(x, approximate=True)

def _silu(x):
    return jax.nn.silu(x)

def _sigmoid(x):
    return jax.nn.sigmoid(x)

def _layernorm(x, axis=-1, eps=1e-05):
    m = jnp.mean(x, axis=axis, keepdims=True)
    v = jnp.var(x, axis=axis, keepdims=True)
    return (x - m) / jnp.sqrt(v + eps)

def _scatter_add(tgt, idx, src, axis=0):
    return tgt.at[idx].add(src)

def _segment_sum(src, seg, n):
    return jax.ops.segment_sum(src, seg, n)
kernel_name = 'mk_decoder_preln_d1_seqx_r4_0e3eb2'

def setup_inputs(seed: int=0):
    np.random.seed(seed)
    _w = jnp.asarray

    def _rec_inputs():
        import jax
        import jax.numpy as jnp
        _rk = jax.random.key(seed)
        x = 2.818e-05 + 1 * jax.random.normal(jax.random.fold_in(_rk, 1), (32, 128, 256), jnp.float32)
        _lenS = 128 - jax.random.randint(jax.random.fold_in(_rk, 7), (32,), 0, max(1, 128 // 4) + 1, jnp.int32)
        _lenS2 = 128 - jax.random.randint(jax.random.fold_in(_rk, 8), (32,), 0, max(1, 128 // 4) + 1, jnp.int32)
        _ctx_2048P = jax.random.normal(jax.random.fold_in(_rk, 11), (32, 16, 512), jnp.float32)
        _ctx_2048c = jax.random.dirichlet(jax.random.fold_in(_rk, 511), 0.3 * jnp.ones((16,), jnp.float32), (32, 128))
        _ctx_2048t = jnp.einsum('bsk,bkd->bsd', _ctx_2048c, _ctx_2048P)
        _ctx_2048t = _ctx_2048t * jax.lax.rsqrt(jnp.mean(jnp.square(_ctx_2048t)) + 1e-12) * 0.953939
        ctx_2048 = -0.000125008 + 0.999885 * (_ctx_2048t + 0.3 * jax.random.normal(jax.random.fold_in(_rk, 611), (32, 128, 512), jnp.float32))
        _validS = jnp.arange(128)[None, :] < _lenS[:, None]
        _validS2 = jnp.arange(128)[None, :] < _lenS2[:, None]
        _causal = jnp.tril(jnp.ones((128, 128), dtype=bool))
        mask_BxS2_fk1 = jnp.where(jnp.broadcast_to(_validS2[:, :], (32, 128)), 1.0, 0.0).astype(jnp.float32)
        return (x, ctx_2048, mask_BxS2_fk1)
    x, ctx_2048, mask_BxS2_fk1 = _rec_inputs()

    def _L0_attn_setup():
        import jax, jax.numpy as jnp
        import numpy as np
        from jax import lax
        D_MODEL = 256
        D_INNER = 2 * D_MODEL
        D_STATE = 16
        D_CONV = 4
        DT_RANK = 64
        DT_MIN = 0.001
        DT_MAX = 0.1
        BATCH = 4
        SEQ = 512
        key = jax.random.key(seed)
        ks = jax.random.split(key, 8)
        s = lambda fan_in: 1.0 / np.sqrt(fan_in)
        x = jax.random.normal(ks[0], (BATCH, SEQ, D_MODEL), dtype=jnp.float32)
        W_in = jax.random.uniform(ks[1], (D_MODEL, 2 * D_INNER), jnp.float32, -s(D_MODEL), s(D_MODEL))
        conv_w = jax.random.uniform(ks[2], (D_INNER, 1, D_CONV), jnp.float32, -s(D_CONV), s(D_CONV))
        conv_b = jax.random.uniform(ks[3], (D_INNER,), jnp.float32, -s(D_CONV), s(D_CONV))
        W_x = jax.random.uniform(ks[4], (D_INNER, DT_RANK + 2 * D_STATE), jnp.float32, -s(D_INNER), s(D_INNER))
        W_dt = jax.random.uniform(ks[5], (DT_RANK, D_INNER), jnp.float32, -s(DT_RANK), s(DT_RANK))
        b_dt = jax.random.uniform(ks[6], (D_INNER,), jnp.float32, -s(DT_RANK), s(DT_RANK))
        A_log = jnp.log(jnp.broadcast_to(jnp.arange(1, D_STATE + 1, dtype=jnp.float32), (D_INNER, D_STATE)))
        D_param = jnp.ones((D_INNER,), dtype=jnp.float32)
        W_out = jax.random.uniform(ks[7], (D_INNER, D_MODEL), jnp.float32, -s(D_INNER), s(D_INNER))
        return {'x': x, 'W_in': W_in, 'conv_w': conv_w, 'conv_b': conv_b, 'W_x': W_x, 'W_dt': W_dt, 'b_dt': b_dt, 'A_log': A_log, 'D_param': D_param, 'W_out': W_out}
    _L0_attn_all = _L0_attn_setup()
    _L0_attn_in = {k: v for k, v in _L0_attn_all.items() if k in ('W_in', 'conv_w', 'conv_b', 'W_x', 'W_dt', 'b_dt', 'A_log', 'D_param', 'W_out')}
    del _L0_attn_all

    def _L0_xattn_setup():
        import jax, jax.numpy as jnp
        import numpy as np
        B, S, T = (32, 128, 128)
        SRC_SIZE, TGT_SIZE, OUT_SIZE, NUM_HEAD = (512, 256, 256, 8)
        HEAD_DIM = OUT_SIZE // NUM_HEAD
        key = jax.random.key(seed)
        ks = jax.random.split(key, 12)
        src = jax.random.normal(ks[0], (B, S, SRC_SIZE), dtype=jnp.float32)
        tgt = jax.random.normal(ks[1], (B, T, TGT_SIZE), dtype=jnp.float32)
        src_mask = (jax.random.uniform(ks[2], (B, S)) > 0.3).astype(jnp.float32)
        src_mask = src_mask.at[:, 0].set(1.0)
        tgt_mask = (jax.random.uniform(ks[3], (B, T)) > 0.3).astype(jnp.float32)
        tgt_mask = tgt_mask.at[:, 0].set(1.0)

        def lin(k, out_f, in_f):
            return jax.random.normal(k, (out_f, in_f), dtype=jnp.float32) / np.sqrt(in_f)
        W_src = lin(ks[4], 2 * OUT_SIZE, SRC_SIZE)
        b_src = jnp.zeros((2 * OUT_SIZE,), jnp.float32)
        W_tgt = lin(ks[5], OUT_SIZE, TGT_SIZE)
        b_tgt = jnp.zeros((OUT_SIZE,), jnp.float32)
        W_out = lin(ks[6], OUT_SIZE, OUT_SIZE + TGT_SIZE)
        b_out = jnp.zeros((OUT_SIZE,), jnp.float32)
        return {'src': src, 'tgt': tgt, 'src_mask': src_mask, 'tgt_mask': tgt_mask, 'W_src': W_src, 'b_src': b_src, 'W_tgt': W_tgt, 'b_tgt': b_tgt, 'W_out': W_out, 'b_out': b_out}
    _L0_xattn_all = _L0_xattn_setup()
    _L0_xattn_in = {k: v for k, v in _L0_xattn_all.items() if k in ('W_src', 'b_src', 'W_tgt', 'b_tgt', 'W_out', 'b_out')}
    del _L0_xattn_all

    def _L0_ffn_setup():
        import jax, jax.numpy as jnp
        import numpy as np
        H = 256
        I = 512
        E = 8
        B, S = (2, 256)

        def _swiglu(x, wg, wu, wd):
            return jax.nn.silu(x @ wg) * (x @ wu) @ wd
        key = jax.random.key(seed)
        ks = jax.random.split(key, 8)
        sc_h = 1.0 / np.sqrt(H)
        sc_i = 1.0 / np.sqrt(I)
        return {'hidden_states': jax.random.normal(ks[0], (B, S, H), jnp.float32), 'gate_w': jax.random.normal(ks[1], (H, E), jnp.float32) * sc_h, 'sh_gate': jax.random.normal(ks[2], (H, I), jnp.float32) * sc_h, 'sh_up': jax.random.normal(ks[3], (H, I), jnp.float32) * sc_h, 'sh_down': jax.random.normal(ks[4], (I, H), jnp.float32) * sc_i, 'rt_gate': jax.random.normal(ks[5], (E, H, I), jnp.float32) * sc_h, 'rt_up': jax.random.normal(ks[6], (E, H, I), jnp.float32) * sc_h, 'rt_down': jax.random.normal(ks[7], (E, I, H), jnp.float32) * sc_i}
    _L0_ffn_all = _L0_ffn_setup()
    _L0_ffn_in = {k: v for k, v in _L0_ffn_all.items() if k in ('gate_w', 'sh_gate', 'sh_up', 'sh_down', 'rt_gate', 'rt_up', 'rt_down')}
    del _L0_ffn_all
    return {'x': x, 'ctx_2048': ctx_2048, 'mask_BxS2_fk1': mask_BxS2_fk1, 'L0_attn_W_in': _L0_attn_in['W_in'], 'L0_attn_conv_w': _L0_attn_in['conv_w'], 'L0_attn_conv_b': _L0_attn_in['conv_b'], 'L0_attn_W_x': _L0_attn_in['W_x'], 'L0_attn_W_dt': _L0_attn_in['W_dt'], 'L0_attn_b_dt': _L0_attn_in['b_dt'], 'L0_attn_A_log': _L0_attn_in['A_log'], 'L0_attn_D_param': _L0_attn_in['D_param'], 'L0_attn_W_out': _L0_attn_in['W_out'], 'L0_xattn_W_src': _L0_xattn_in['W_src'], 'L0_xattn_b_src': _L0_xattn_in['b_src'], 'L0_xattn_W_tgt': _L0_xattn_in['W_tgt'], 'L0_xattn_b_tgt': _L0_xattn_in['b_tgt'], 'L0_xattn_W_out': _L0_xattn_in['W_out'], 'L0_xattn_b_out': _L0_xattn_in['b_out'], 'L0_ffn_gate_w': _L0_ffn_in['gate_w'], 'L0_ffn_sh_gate': _L0_ffn_in['sh_gate'], 'L0_ffn_sh_up': _L0_ffn_in['sh_up'], 'L0_ffn_sh_down': _L0_ffn_in['sh_down'], 'L0_ffn_rt_gate': _L0_ffn_in['rt_gate'], 'L0_ffn_rt_up': _L0_ffn_in['rt_up'], 'L0_ffn_rt_down': _L0_ffn_in['rt_down']}

def reference(x, ctx_2048, mask_BxS2_fk1, L0_attn_W_in, L0_attn_conv_w, L0_attn_conv_b, L0_attn_W_x, L0_attn_W_dt, L0_attn_b_dt, L0_attn_A_log, L0_attn_D_param, L0_attn_W_out, L0_xattn_W_src, L0_xattn_b_src, L0_xattn_W_tgt, L0_xattn_b_tgt, L0_xattn_W_out, L0_xattn_b_out, L0_ffn_gate_w, L0_ffn_sh_gate, L0_ffn_sh_up, L0_ffn_sh_down, L0_ffn_rt_gate, L0_ffn_rt_up, L0_ffn_rt_down):
    import jax
    import jax.numpy as jnp

    def _L0_attn_ref(x, W_in, conv_w, conv_b, W_x, W_dt, b_dt, A_log, D_param, W_out):
        import jax, jax.numpy as jnp
        import numpy as np
        from jax import lax
        D_MODEL = 256
        D_INNER = 2 * D_MODEL
        D_STATE = 16
        D_CONV = 4
        DT_RANK = 64
        DT_MIN = 0.001
        DT_MAX = 0.1
        BATCH = 4
        SEQ = 512
        xz = x @ W_in
        x_branch, z_branch = jnp.split(xz, 2, axis=-1)
        xc = jnp.pad(x_branch.transpose(0, 2, 1), ((0, 0), (0, 0), (D_CONV - 1, 0)))
        xc = lax.conv_general_dilated(xc, conv_w, (1,), 'VALID', dimension_numbers=('NCH', 'OIH', 'NCH'), feature_group_count=D_INNER)
        xc = xc + conv_b[None, :, None]
        x_conv = jax.nn.silu(xc.transpose(0, 2, 1))
        x_dbl = x_conv @ W_x
        dt_low = x_dbl[..., :DT_RANK]
        Bm = x_dbl[..., DT_RANK:DT_RANK + D_STATE]
        Cm = x_dbl[..., DT_RANK + D_STATE:]
        dt = jax.nn.sigmoid(dt_low @ W_dt + b_dt) * (DT_MAX - DT_MIN) + DT_MIN
        dt = jnp.maximum(dt, 0.0001)
        A = -jnp.exp(A_log)

        def step(h, inp):
            dt_t, B_t, C_t, x_t = inp
            dA = jnp.exp(dt_t[:, :, None] * A[None])
            h = dA * h + (dt_t * x_t)[:, :, None] * B_t[:, None, :]
            y_t = jnp.sum(h * C_t[:, None, :], axis=-1)
            return (h, y_t)
        h0 = jnp.zeros((x.shape[0], D_INNER, D_STATE), dtype=x.dtype)
        _, ys = lax.scan(step, h0, (dt.swapaxes(0, 1), Bm.swapaxes(0, 1), Cm.swapaxes(0, 1), x_conv.swapaxes(0, 1)))
        y = ys.swapaxes(0, 1)
        y = y + x_conv * D_param
        y = y * jax.nn.silu(z_branch)
        return y @ W_out

    def _L0_xattn_ref(src, tgt, src_mask, tgt_mask, W_src, b_src, W_tgt, b_tgt, W_out, b_out):
        import jax, jax.numpy as jnp
        import numpy as np
        B, S, T = (32, 128, 128)
        SRC_SIZE, TGT_SIZE, OUT_SIZE, NUM_HEAD = (512, 256, 256, 8)
        HEAD_DIM = OUT_SIZE // NUM_HEAD
        b, s, _ = src.shape
        t = tgt.shape[1]
        src_trans = jnp.einsum('bsf,of->bso', src, W_src) + b_src
        tgt_trans = jnp.einsum('btf,of->bto', tgt, W_tgt) + b_tgt
        src_trans = src_trans * src_mask[:, :, None]
        tgt_trans = tgt_trans * tgt_mask[:, :, None]
        src_key, src_val = jnp.split(src_trans, 2, axis=2)
        k = src_key.reshape(b, s, NUM_HEAD, HEAD_DIM)
        v = src_val.reshape(b, s, NUM_HEAD, HEAD_DIM)
        q = tgt_trans.reshape(b, t, NUM_HEAD, HEAD_DIM)
        scores = jnp.einsum('bthd,bshd->bhts', q, k) / np.sqrt(HEAD_DIM)
        scores = jnp.where(src_mask[:, None, None, :] == 0, -jnp.inf, scores)
        attn = jax.nn.softmax(scores, axis=-1)
        tgt_update = jnp.einsum('bhts,bshd->bthd', attn, v).reshape(b, t, OUT_SIZE)
        cat_tgt = jnp.concatenate([tgt, tgt_update], axis=2)
        return jnp.einsum('btf,of->bto', cat_tgt, W_out) + b_out

    def _L0_ffn_ref(hidden_states, gate_w, sh_gate, sh_up, sh_down, rt_gate, rt_up, rt_down):
        import jax, jax.numpy as jnp
        import numpy as np
        H = 256
        I = 512
        E = 8
        B, S = (2, 256)

        def _swiglu(x, wg, wu, wd):
            return jax.nn.silu(x @ wg) * (x @ wu) @ wd
        b, s, h = hidden_states.shape
        x = hidden_states.reshape(-1, h)
        logits = x @ gate_w
        top_val = jnp.max(logits, axis=-1, keepdims=True)
        top_id = jnp.argmax(logits, axis=-1)
        score = jax.nn.sigmoid(top_val)
        xs = x * score
        g = jnp.einsum('th,ehi->eti', xs, rt_gate)
        u = jnp.einsum('th,ehi->eti', xs, rt_up)
        act = jax.nn.silu(g) * u
        y = jnp.einsum('eti,eih->eth', act, rt_down)
        onehot = jax.nn.one_hot(top_id, E, dtype=x.dtype)
        routed = jnp.einsum('eth,te->th', y, onehot)
        shared = _swiglu(x, sh_gate, sh_up, sh_down)
        return (shared + routed).reshape(b, s, h)
    x = x + _L0_attn_ref(_layernorm(x, axis=-1), L0_attn_W_in, L0_attn_conv_w, L0_attn_conv_b, L0_attn_W_x, L0_attn_W_dt, L0_attn_b_dt, L0_attn_A_log, L0_attn_D_param, L0_attn_W_out)
    x = x + _L0_xattn_ref(ctx_2048, _layernorm(x, axis=-1), mask_BxS2_fk1, mask_BxS2_fk1, L0_xattn_W_src, L0_xattn_b_src, L0_xattn_W_tgt, L0_xattn_b_tgt, L0_xattn_W_out, L0_xattn_b_out)
    x = x + _L0_ffn_ref(_layernorm(x, axis=-1), L0_ffn_gate_w, L0_ffn_sh_gate, L0_ffn_sh_up, L0_ffn_sh_down, L0_ffn_rt_gate, L0_ffn_rt_up, L0_ffn_rt_down)
    return x

_drawn_inputs = setup_inputs


def setup_inputs(seed=0):
    import zlib

    import numpy as np

    out = dict(_drawn_inputs(seed))
    spreads = {'L0_attn_D_param': (1.0, 0.6),
     'L0_xattn_b_src': (0.0, 0.1),
     'L0_xattn_b_tgt': (0.0, 0.267),
     'L0_xattn_b_out': (0.0, 0.1)}
    factors = {'L0_attn_W_x': 8.0, 'L0_attn_W_dt': 8.0, 'L0_attn_b_dt': 64.0, 'L0_attn_A_log': 22.222}
    for name, (base, spread) in spreads.items():
        noise = np.random.default_rng([zlib.crc32(name.encode()), seed]).standard_normal(out[name].shape)
        drawn = base * np.exp(spread * noise) if base else spread * noise
        out[name] = jnp.asarray(drawn.astype(out[name].dtype))
    for name, factor in factors.items():
        out[name] = (out[name] * factor).astype(out[name].dtype)
    return out
```

```python
from contextlib import ExitStack

import concourse.bass as bass
from concourse import mybir

F32 = mybir.dt.float32
I32 = mybir.dt.int32
U32 = mybir.dt.uint32
ALU = mybir.AluOpType
ACT = mybir.ActivationFunctionType
AX = mybir.AxisListType

P = 128
SEQS = 32
GB = 4
GT = GB * P
GROUPS = SEQS // GB
TOKENS = SEQS * P
D = 256
KD = D // P
DI = 512
KI = DI // P
NS = 16
RANK = 64
CS = 512
KC = CS // P
HEADS = 8
HD = D // HEADS
HC = P // HD
E = 8
FF = 512
KF = FF // P
TILES = TOKENS // P + E - 1
SLOTS_DRAM = TILES * P
DT_MIN, DT_MAX = 0.001, 0.1
EPS = 1e-5
MASKED = -1e30
ATT_SCALE = 1.0 / float(HD) ** 0.5
C_ROW, B_ROW, R_ROW = 0, 32, 64

SCAN_SLOTS = NS * KI
SLOTS = SCAN_SLOTS + KI
OTHER_BANKS = 4

PE_POST = {("z", 0): 0, ("y", 0): 0, ("z", 1): 1, ("y", 1): 1, ("z", 2): 2, ("y", 2): 2, ("z", 3): 3, ("y", 3): 3,
           ("k", 0): 5, ("k", 1): 6, ("o", 0): 7, ("o", 1): 8, ("v", 0): 9, ("v", 1): 10,
           ("t2", 0): 14, ("t2", 1): 15, ("q", 0): 17, ("q", 1): 18,
           **{("s", m): 19 + 2 * m for m in range(HEADS)},
           **{("a", m): 23 + 2 * m for m in range(HEADS)},
           ("av", 0): 31, ("av", 1): 39, ("ut", 0): 40, ("ut", 1): 41, ("xo", 0): 43, ("xo", 1): 44,
           ("t3", 0): 49, ("t3", 1): 50, ("lg", 0): 52,
           **{("g", c): 53 + 2 * c for c in range(KF)}, **{("u", c): 53 + 2 * c for c in range(KF)},
           ("dn", 0): 62, ("dn", 1): 63}
PE_PRE = {("t1", 0): 12, ("t1", 1): 13, ("xb", 0): 20, ("xb", 1): 24, ("xb", 2): 28, ("xb", 3): 32,
          ("xd", 0): 45, ("ct", 0): 48, ("dt", 0): 47, ("dt", 1): 49, ("dt", 2): 51, ("dt", 3): 53}
ACT_POST = {("z", 0): 0, ("z", 1): 1, ("z", 2): 2, ("z", 3): 3, ("k", 0): 6, ("k", 1): 7, ("v", 0): 10, ("v", 1): 11,
            ("t2", 0): 15, ("t2", 1): 16,
            **{("s", m): 20 + 2 * m for m in range(HEADS)},
            **{("a", m): 24 + 2 * m for m in range(HEADS)},
            ("ut", 0): 41, ("ut", 1): 42, ("t3", 0): 50, ("t3", 1): 51, ("lg", 0): 54,
            **{("g", c): 54 + 2 * c for c in range(KF)}}
ACT_PRE = {("t1", 0): 13, ("t1", 1): 14, ("xb", 0): 21, ("xb", 1): 25, ("xb", 2): 29, ("xb", 3): 33,
           ("th", 0): 23, ("th", 1): 27, ("th", 2): 31, ("th", 3): 35,
           ("xd", 0): 46, ("dt", 0): 48, ("dt", 1): 50, ("dt", 2): 52, ("dt", 3): 54}
DVE_POST = {("z", 0): 1, ("z", 1): 2, ("z", 2): 3, ("z", 3): 4, ("o", 0): 8, ("o", 1): 9, ("ln2", 0): 10,
            ("mb", 0): 1, ("q", 0): 18, ("q", 1): 19,
            **{("s", m): 20 + 2 * m for m in range(HEADS)},
            ("r", 0): 29, ("r", 1): 37, ("av", 0): 32, ("av", 1): 39, ("xo", 0): 44, ("xo", 1): 45, ("ln3", 0): 46,
            ("lg", 0): 53, **{("g", c): 55 + 2 * c for c in range(KF)},
            ("dn", 0): 63, ("dn", 1): 64}
DVE_PRE = {("ln1", 0): 5, ("cv", 0): 22, ("cv", 1): 26, ("cv", 2): 30, ("cv", 3): 34,
           ("xc", 0): 24, ("xc", 1): 28, ("xc", 2): 32, ("xc", 3): 36, ("ct", 0): 49,
           ("dt", 0): 49, ("dt", 1): 51, ("dt", 2): 53, ("dt", 3): 55}
POOL_POST = {("cm", 0): 1, ("ln2", 0): 11, ("ln3", 0): 47, ("xs", 0): 56}
POOL_PRE = {("ln1", 0): 6, ("dx", 0): 50, ("dx", 1): 52, ("dx", 2): 54, ("dx", 3): 56}
SP_POST = {("oh", 0): 55, ("xs", 0): 58, ("base", 0): 66}
SP_PRE = {("B", 0): 48}


def steps_at(slot, *tables):
    return [step for table in tables for step, at in table.items() if at == slot]


class Memory:
    pass


def phase_a_memory(nc, ctx, m):
    def sb(name, shape, dtype=F32):
        return ctx.enter_context(nc.sbuf_tensor(name, shape, dtype))

    m.w_in = sb("w_in", [P, KD, 2 * DI])
    m.w_x = sb("w_x", [P, KI, P])
    m.w_dt = sb("w_dt", [P, DI])
    m.b_src = m.w_dt[0:1, 0:2 * D]
    m.b_xo, m.ones = m.w_dt[32:33, 0:D], m.w_dt[32:33, D:D + P]
    m.w_out = sb("w_out", [P, KI, D])
    m.w_src = sb("w_src", [P, KC, 2 * D])
    m.w_tgt = sb("w_tgt", [P, KD, D])
    m.w_xo = sb("w_xo", [P, 2 * KD, D])
    m.sh_gate = sb("sh_gate", [P, KD, FF])
    m.sh_up = sb("sh_up", [P, KD, FF])
    m.sh_down = sb("sh_down", [P, KF, D])
    m.gate_w = sb("gate_w", [P, KD, E])
    m.a_neg = sb("a_neg", [P, KI, NS])
    m.conv_w = sb("conv_w", [P, KI, 4])
    m.conv_b = sb("conv_b", [P, KI])
    m.dt_bias = sb("dt_bias", [P, KI])
    m.d_half = sb("d_half", [P, KI])
    m.b_tgt = sb("b_tgt", [P, KD])
    m.ident = sb("ident", [P, P])
    m.first = sb("first", [P, E])
    m.first_i = sb("first_i", [P, E], I32)
    m.minus_half = sb("minus_half", [P, GB])
    m.xn1T = [sb(f"xn1T{i}", [P, KD, GT]) for i in range(2)]
    m.xc2 = [sb(f"xc2_{i}", [P, KI, GT]) for i in range(2)]
    m.dt = [sb(f"dt{i}", [P, KI, GT]) for i in range(2)]
    m.dtx = [sb(f"dtx{i}", [P, KI, GT]) for i in range(2)]
    m.c_tok = [sb(f"c_tok{i}", [P, GB, NS]) for i in range(2)]
    m.acc = sb("acc", [P, GB, DI])
    m.bb = sb("bb", [P, 4, GT])
    m.u = sb("u", [P, 2, KI, GT])
    m.h = sb("h", [P, 2, KI, GT])
    m.xin = sb("xin", [P, GB, D])
    m.xb = sb("xb", [P, GT])
    m.cv = sb("cv", [P, GT])
    m.th = sb("th", [P, 2, GT])
    m.xdT = sb("xdT", [P, GT])
    m.x1 = sb("x1", [P, GB, D])
    m.xn = sb("xn", [P, GB, D])
    m.xnT = sb("xnT", [P, KD, GT])
    m.ctx_at = sb("ctx_at", [P, KC, GT])
    m.kv_act = sb("kv_act", [P, 4, GT])
    m.q_up = sb("q_up", [P, KD, GT])
    m.sc = sb("sc", [P, 2, GT])
    m.upd = sb("upd", [P, GB, D])
    m.mask_all = sb("mask_all", [P, GT])
    m.mask_neg = sb("mask_neg", [P, GT])
    m.small = {}
    for name, w in (("st1", 24), ("st2", 24), ("st3", 24), ("mv1", 8), ("mv2", 8), ("mv3", 8), ("rs1", 4), ("rs2", 4),
                    ("rs3", 4), ("nmax", 32), ("sum", 32), ("rec", 32), ("mx", 4), ("eq", 32), ("m8", 4), ("oh", 32),
                    ("top", 4), ("score", 4)):
        m.small[name] = sb("s_" + name, [P, w])


def setup(nc, m, a, sems):
    with nc.Block() as block:
        @block.sync
        def _(sp):
            def load(dst, src):
                sp.dma_start(dst, src).then_inc(sems["w"], 16)
                load.n += 16
            load.n = 0
            load(m.w_in[:], a["w_in"].rearrange("(k p) n -> p k n", p=P))
            sp.wait_ge(sems["w_clear"], 1)
            wx = a["w_x"].rearrange("(k p) n -> p k n", p=P)
            load(m.w_x[:, :, R_ROW:R_ROW + RANK], wx[:, :, 0:RANK])
            load(m.w_x[:, :, B_ROW:B_ROW + NS], wx[:, :, RANK:RANK + NS])
            load(m.w_x[:, :, C_ROW:C_ROW + NS], wx[:, :, RANK + NS:RANK + 2 * NS])
            load(m.w_dt[R_ROW:R_ROW + RANK, :], a["w_dt"])
            load(m.w_out[:], a["w_out"].rearrange("(k p) n -> p k n", p=P))
            load(m.w_src[:], a["w_srcT"].rearrange("(k p) n -> p k n", p=P))
            load(m.w_tgt[:], a["w_tgtT"].rearrange("(k p) n -> p k n", p=P))
            load(m.w_xo[:], a["w_xoT"].rearrange("(k p) n -> p k n", p=P))
            load(m.sh_gate[:], a["sh_gate"].rearrange("(k p) n -> p k n", p=P))
            load(m.sh_up[:], a["sh_up"].rearrange("(k p) n -> p k n", p=P))
            load(m.sh_down[:], a["sh_down"].rearrange("(k p) n -> p k n", p=P))
            load(m.gate_w[:], a["gate_w"].rearrange("(k p) n -> p k n", p=P))
            load(m.a_neg[:], a["a_log"].rearrange("(k p) n -> p k n", p=P))
            load(m.conv_w[:], a["conv_w"].rearrange("(k p) n -> p k n", p=P))
            load(m.conv_b[:], a["conv_b"])
            load(m.dt_bias[:], a["b_dt"])
            load(m.d_half[:], a["d_param"])
            load(m.b_tgt[:], a["b_tgt"])
            load(m.b_src, a["b_src"])
            load(m.b_xo, a["b_xo"])
            sp.wait_ge(sems["zero"], 1)
            for t in range(TILES):
                load(a["x_slots"][t * P:(t + 1) * P, :], m.xin[:, 0, :])
            sp.wait_ge(sems["w"], load.n)
            sp.sem_inc(sems["w_loaded"], 1)

        @block.gpsimd
        def _(pool):
            nc.gpsimd.memset(m.xin[:, 0, :], 0.0).then_inc(sems["zero"], 1)
            nc.gpsimd.memset(m.ident[:], 0.0).then_inc(sems["id"], 1)
            pool.wait_ge(sems["id"], 1)
            nc.gpsimd.affine_select(out=m.ident[:], in_=m.ident[:], compare_op=ALU.not_equal, fill=1.0, base=0,
                                    pattern=[[-1, P]], channel_multiplier=1).then_inc(sems["id"], 1)
            nc.gpsimd.iota(m.first_i[:], [[-1, E]], base=E, channel_multiplier=0).then_inc(sems["iota"], 1)

        @block.scalar
        def _(act):
            act.wait_ge(sems["w_loaded"], 1)
            nc.scalar.activation(m.a_neg[:], m.a_neg[:], ACT.Exp).then_inc(sems["a_exp"], 1)

        @block.vector
        def _(dve):
            nc.vector.memset(m.w_x[:], 0.0).then_inc(sems["w_clear"], 1)
            nc.vector.memset(m.ones, 1.0)
            nc.vector.memset(m.minus_half[:], -0.5)
            for bank in m.dA:
                nc.vector.memset(bank.rearrange("p (b t) -> p b t", b=GB)[:, :, 0:1], 0.0)
            dve.wait_ge(sems["iota"], 1)
            nc.vector.tensor_copy(m.first[:], m.first_i[:])
            dve.wait_ge(sems["w_loaded"], 1)
            for t, f in ((m.w_out[:], 0.5), (m.sh_down[:], 0.5), (m.dt_bias[:], 0.5), (m.d_half[:], 0.5),
                         (m.w_x[:, :, C_ROW:C_ROW + NS], 0.5), (m.w_x[:, :, B_ROW:B_ROW + NS], 0.25),
                         (m.w_x[:, :, R_ROW:R_ROW + RANK], 0.5)):
                nc.vector.tensor_scalar(t, t, f, None, ALU.mult)
            dve.wait_ge(sems["a_exp"], 1)
            nc.vector.tensor_scalar(m.a_neg[:], m.a_neg[:], -1.0, None, ALU.mult)


def iteration(nc, m, a, S, scan=None, post=None, pre=None, parity=0):
    do_scan, do_post, do_pre = scan is not None, post is not None, pre is not None
    other = 1 - parity
    tables = lambda p, q: ([p] if do_post else []) + ([q] if do_pre else [])
    order = [step for slot in range(SLOTS) for step in steps_at(slot, *tables(PE_POST, PE_PRE))]
    number = {step: i for i, step in enumerate(order)}
    last_slot = SLOTS if do_scan else SCAN_SLOTS + KI

    def bank(name, k=0):
        return m.other[number[name, k] % OTHER_BANKS]

    def wait_bank_free(pe, name, k):
        i = number[name, k]
        if i >= OTHER_BANKS:
            pe.wait_ge(S[f"bank_free{i % OTHER_BANKS}"], i // OTHER_BANKS)

    def wait_bank_full(eng, name, k=0):
        eng.wait_ge(S["bank_full"], number[name, k] + 1)

    def wait_bank_read(eng, name, k=0):
        eng.wait_ge(S[f"bank_free{number[name, k] % OTHER_BANKS}"], number[name, k] // OTHER_BANKS + 1)

    def bank_free(name, k=0):
        return S[f"bank_free{number[name, k] % OTHER_BANKS}"]

    k_ap, v_ap = m.kv_act[:, 0:2, :], m.kv_act[:, 2:4, :].rearrange("p a (b f) -> p (a b) f", f=D)

    with nc.Block() as block:
        @block.sync
        def _(sp):
            if do_pre:
                sp.dma_start(m.xin[:], a["x"][bass.ts(pre, GT)].rearrange("(b p) c -> p b c", p=P)).then_inc(S["x_in"], 16)
            if do_scan:
                for n in range(4):
                    sp.dma_start(m.bb[:, n, :], a["b_rows"][n:n + 1, parity * GT:(parity + 1) * GT].broadcast_to([P, GT])
                                 ).then_inc(S[f"bb{n}"], 16)
            if do_post:
                sp.dma_start(m.x1[:], a["x"][bass.ts(post, GT)].rearrange("(b p) c -> p b c", p=P)).then_inc(S["x_res"], 16)
                sp.dma_start(m.mask_all[:], a["mask"][0:1, bass.ts(post, GT)].broadcast_to([P, GT])).then_inc(S["mask_in"], 16)
                sp.dma_start(m.ctx_at[:], a["ctxT"][:, bass.ts(post, GT)].rearrange("(k p) t -> p k t", p=P)
                             ).then_inc(S["ctx_in"], 16)
            for slot in range(last_slot):
                n = slot // KI + 4
                if do_scan and slot % KI == 0 and n < NS:
                    sp.wait_ge(S["u_ready"], n - 4 + 1)
                    sp.dma_start(m.bb[:, n % 4, :], a["b_rows"][n:n + 1, parity * GT:(parity + 1) * GT].broadcast_to([P, GT])
                                 ).then_inc(S[f"bb{n % 4}"], 16)
                for name, k in steps_at(slot, *tables(SP_POST, SP_PRE)):
                    if name == "B":
                        wait_bank_read(sp, "xd")
                        sp.dma_start(a["b_rows"][:, other * GT:(other + 1) * GT], m.xdT[B_ROW:B_ROW + NS, :]
                                     ).then_inc(S["stored"], 16)
                    elif name == "oh":
                        sp.wait_ge(S["onehot"], 1)
                        sp.dma_start(a["onehot"][bass.ts(post, P), :], m.small["oh"][:]).then_inc(S["stored"], 16)
                    elif name == "xs":
                        sp.wait_ge(S["xs_ready"], 1)
                        sp.dma_start(a["xs"][bass.ts(post, GT)].rearrange("(b p) c -> p b c", p=P), m.xn[:]
                                     ).then_inc(S["stored"], 16)
                    elif name == "base":
                        wait_bank_read(sp, "dn", 0)
                        wait_bank_read(sp, "dn", 1)
                        sp.dma_start(a["base"][bass.ts(post, GT)].rearrange("(b p) c -> p b c", p=P), m.x1[:]
                                     ).then_inc(S["stored"], 16)
            sp.wait_ge(S["stored"], 16 * (3 * do_post + do_pre))

        @block.tensor
        def _(pe):
            def mm(out, lhsT, rhs, first, last):
                return nc.tensor.matmul(out, lhsT, rhs, start=first, stop=last)

            def transposes(name, k, src):
                for b in range(GB):
                    ins = nc.tensor.transpose(bank(name, k)[:, b * P:(b + 1) * P], src(b), m.ident[:])
                ins.then_inc(S["bank_full"], 1)

            def step(name, k):
                wait_bank_free(pe, name, k)
                out = bank(name, k)
                if name == "z":
                    for kk in range(KD):
                        ins = mm(out[:], m.w_in[:, kk, DI + k * P:DI + (k + 1) * P], m.xn1T[other][:, kk, :],
                                 kk == 0, kk == KD - 1)
                    ins.then_inc(S["bank_full"], 1)
                elif name == "y":
                    transposes(name, k, lambda b: m.acc[:, b, k * P:(k + 1) * P])
                elif name == "k":
                    pe.wait_ge(S["ctx_masked"], 1)
                    pe.wait_ge(S["mask_in"], 16)
                    for kk in range(KC):
                        mm(out[:], m.w_src[:, kk, k * P:(k + 1) * P], m.ctx_at[:, kk, :], kk == 0, False)
                    mm(out[:], m.b_src[:, k * P:(k + 1) * P], m.mask_all[0:1, :], False, True).then_inc(S["bank_full"], 1)
                elif name == "v":
                    for i in range(2):
                        b = 2 * k + i
                        o = out[:, i * D:(i + 1) * D]
                        for kk in range(KC):
                            mm(o, m.ctx_at[:, kk, b * P:(b + 1) * P], m.w_src[:, kk, D:2 * D], kk == 0, False)
                        ins = mm(o, m.mask_all[0:1, b * P:(b + 1) * P], m.b_src[:, D:2 * D], False, True)
                    ins.then_inc(S["bank_full"], 1)
                elif name == "o":
                    pe.wait_ge(S["y_gated"], KI)
                    for i in range(2):
                        b = 2 * k + i
                        for kk in range(KI):
                            ins = mm(out[:, i * D:(i + 1) * D], m.xc2[other][:, kk, b * P:(b + 1) * P], m.w_out[:, kk, :],
                                     kk == 0, kk == KI - 1)
                    ins.then_inc(S["bank_full"], 1)
                elif name == "t2":
                    pe.wait_ge(S["ln2_ready"], GB)
                    transposes(name, k, lambda b: m.xn[:, b, k * P:(k + 1) * P])
                elif name == "q":
                    for kk in range(KD):
                        wait_bank_read(pe, "t2", kk)
                    for kk in range(KD):
                        ins = mm(out[:], m.w_tgt[:, kk, k * P:(k + 1) * P], m.xnT[:, kk, :], kk == 0, kk == KD - 1)
                    ins.then_inc(S["bank_full"], 1)
                elif name == "s":
                    c, j = k // HC, k % HC
                    wait_bank_read(pe, "q", c)
                    wait_bank_read(pe, "k", c)
                    rows = slice(HD * j, HD * (j + 1))
                    for b in range(GB):
                        ins = mm(out[:, b * P:(b + 1) * P], m.q_up[rows, c, b * P:(b + 1) * P],
                                 k_ap[rows, c, b * P:(b + 1) * P], True, True)
                    ins.then_inc(S["bank_full"], 1)
                elif name == "a":
                    pe.wait_ge(S["att_exp"], GB * (k + 1))
                    transposes(name, k, lambda b: m.sc[:, k % 2, b * P:(b + 1) * P])
                elif name == "av":
                    for j in range(HC):
                        wait_bank_read(pe, "a", HC * k + j)
                    wait_bank_read(pe, "v", 0)
                    wait_bank_read(pe, "v", 1)
                    for b in range(GB):
                        for j in range(HC):
                            f = b * P + j * HD
                            ins = mm(out[:, f:f + HD], m.ctx_at[:, j, b * P:(b + 1) * P],
                                     v_ap[:, b, k * P + j * HD:k * P + (j + 1) * HD], True, True)
                    ins.then_inc(S["bank_full"], 1)
                elif name == "ut":
                    wait_bank_read(pe, "av", k)
                    transposes(name, k, lambda b: m.upd[:, b, k * P:(k + 1) * P])
                elif name == "xo":
                    for kk in range(KD):
                        wait_bank_read(pe, "ut", kk)
                    for i in range(2):
                        b = 2 * k + i
                        o = out[:, i * D:(i + 1) * D]
                        for kk in range(KD):
                            mm(o, m.xnT[:, kk, b * P:(b + 1) * P], m.w_xo[:, kk, :], kk == 0, False)
                        for kk in range(KD):
                            mm(o, m.q_up[:, kk, b * P:(b + 1) * P], m.w_xo[:, KD + kk, :], False, False)
                        ins = mm(o, m.ones, m.b_xo, False, True)
                    ins.then_inc(S["bank_full"], 1)
                elif name == "t3":
                    pe.wait_ge(S["ln3_ready"], GB)
                    transposes(name, k, lambda b: m.xn[:, b, k * P:(k + 1) * P])
                elif name == "lg":
                    for kk in range(KD):
                        wait_bank_read(pe, "t3", kk)
                    for b in range(GB):
                        for kk in range(KD):
                            ins = mm(out[:, b * E:(b + 1) * E], m.xnT[:, kk, b * P:(b + 1) * P], m.gate_w[:, kk, :],
                                     kk == 0, kk == KD - 1)
                    ins.then_inc(S["bank_full"], 1)
                elif name in ("g", "u"):
                    w = m.sh_gate if name == "g" else m.sh_up
                    for kk in range(KD):
                        ins = mm(out[:], w[:, kk, k * P:(k + 1) * P], m.xnT[:, kk, :], kk == 0, kk == KD - 1)
                    ins.then_inc(S["bank_full"], 1)
                elif name == "dn":
                    for kk in range(KF):
                        wait_bank_read(pe, "u", kk)
                    for i in range(2):
                        b = 2 * k + i
                        for kk in range(KF):
                            ins = mm(out[:, i * D:(i + 1) * D], m.kv_act[:, kk, b * P:(b + 1) * P], m.sh_down[:, kk, :],
                                     kk == 0, kk == KF - 1)
                    ins.then_inc(S["bank_full"], 1)
                elif name == "t1":
                    pe.wait_ge(S["ln1_ready"], GB)
                    transposes(name, k, lambda b: m.xin[:, b, k * P:(k + 1) * P])
                elif name == "xb":
                    for kk in range(KD):
                        wait_bank_read(pe, "t1", kk)
                    for kk in range(KD):
                        ins = mm(out[:], m.w_in[:, kk, k * P:(k + 1) * P], m.xn1T[other][:, kk, :], kk == 0, kk == KD - 1)
                    ins.then_inc(S["bank_full"], 1)
                elif name == "xd":
                    pe.wait_ge(S["xc2_ready"], KI)
                    for kk in range(KI):
                        ins = mm(out[:], m.w_x[:, kk, :], m.xc2[other][:, kk, :], kk == 0, kk == KI - 1)
                    ins.then_inc(S["bank_full"], 1)
                elif name == "ct":
                    wait_bank_read(pe, "xd")
                    for b in range(GB):
                        ins = nc.tensor.transpose(out[:, b * NS:(b + 1) * NS], m.xdT[C_ROW:C_ROW + NS, b * P:(b + 1) * P],
                                                  m.ident[0:NS, 0:NS])
                    ins.then_inc(S["bank_full"], 1)
                elif name == "dt":
                    wait_bank_read(pe, "xd")
                    mm(out[:], m.w_dt[R_ROW:R_ROW + RANK, k * P:(k + 1) * P], m.xdT[R_ROW:R_ROW + RANK, :],
                       True, True).then_inc(S["bank_full"], 1)

            for slot in range(last_slot):
                if do_scan and slot >= KI:
                    n, b = slot // KI - 1, slot % KI
                    pe.wait_ge(S["h_ready"], KI * (n + 1))
                    i = slot - KI
                    if i >= 2:
                        pe.wait_ge(S["acc_done"], i - 1)
                    for c in range(KI):
                        ins = nc.tensor.transpose(m.hT[i % 2][:, c * P:(c + 1) * P], m.h[:, n % 2, c, b * P:(b + 1) * P],
                                                  m.ident[:])
                    ins.then_inc(S["hT_ready"], 1)
                for name, k in steps_at(slot, *tables(PE_POST, PE_PRE)):
                    step(name, k)

        @block.scalar
        def _(act):
            def copy(out, in_):
                return nc.scalar.activation(out, in_, ACT.Copy)

            def decay(i):
                n, c = i // KI, i % KI
                if i >= 2:
                    act.wait_ge(S["h_ready"], i - 1)
                nc.scalar.activation(m.dA[i % 2].rearrange("p (b t) -> p b t", b=GB)[:, :, 1:P],
                                     m.dt[parity][:, c, :].rearrange("p (b t) -> p b t", b=GB)[:, :, 1:P],
                                     ACT.Exp, scale=m.a_neg[:, c, n:n + 1]).then_inc(S["dA_ready"], 1)

            def step(name, k):
                if name == "z":
                    wait_bank_full(act, "z", k)
                    if k >= 2:
                        act.wait_ge(S["y_gated"], k - 1)
                    nc.scalar.activation(m.th[:, k % 2, :], bank("z", k)[:], ACT.Tanh, scale=0.5).then_inc(S["z_tanh"], 1)
                elif name == "k":
                    wait_bank_full(act, "k", k)
                    copy(k_ap[:, k, :], bank("k", k)[:]).then_inc(bank_free("k", k), 1)
                elif name == "v":
                    wait_bank_full(act, "v", k)
                    copy(v_ap[:, 2 * k:2 * k + 2, :], bank("v", k)[:].rearrange("p (b f) -> p b f", f=D)
                         ).then_inc(bank_free("v", k), 1)
                elif name in ("t1", "t2", "t3", "ut", "a", "xd"):
                    wait_bank_full(act, name, k)
                    if name == "t1":
                        if do_post:
                            wait_bank_full(act, "z", KI - 1)
                        dst = m.xn1T[other][:, k, :]
                    elif name == "t2":
                        dst = m.xnT[:, k, :]
                    elif name == "t3":
                        wait_bank_full(act, "xo", 1)
                        dst = m.xnT[:, k, :]
                    elif name == "ut":
                        wait_bank_full(act, "s", HEADS - 1)
                        dst = m.q_up[:, k, :]
                    elif name == "a":
                        wait_bank_full(act, "v", 1)
                        wait_bank_full(act, "k", 1)
                        if k >= HC:
                            wait_bank_full(act, "av", 0)
                        dst = m.ctx_at[:, k % HC, :]
                    else:
                        dst = m.xdT[:]
                    copy(dst, bank(name, k)[:]).then_inc(bank_free(name, k), 1)
                elif name == "s":
                    act.wait_ge(S["neg_max"], k + 1)
                    for b in range(GB):
                        nc.scalar.activation(m.sc[:, k % 2, b * P:(b + 1) * P], m.sc[:, k % 2, b * P:(b + 1) * P], ACT.Exp,
                                             bias=m.small["nmax"][:, k * GB + b:k * GB + b + 1],
                                             accum_out=m.small["sum"][:, k * GB + b:k * GB + b + 1]).then_inc(S["att_exp"], 1)
                elif name == "lg":
                    act.wait_ge(S["top_logit"], 1)
                    nc.scalar.activation(m.small["top"][:], m.small["mx"][:], ACT.Tanh, scale=0.5).then_inc(S["top_tanh"], 1)
                elif name == "g":
                    wait_bank_full(act, "g", k)
                    if k >= 2:
                        wait_bank_read(act, "g", k - 2)
                    nc.scalar.activation(m.sc[:, k % 2, :], bank("g", k)[:], ACT.Tanh, scale=0.5).then_inc(S["g_tanh"], 1)
                elif name == "xb":
                    wait_bank_full(act, "xb", k)
                    if k >= 1:
                        act.wait_ge(S["xc2_ready"], k)
                    nc.scalar.activation(m.cv[:], bank("xb", k)[:], ACT.Identity, bias=m.conv_b[:, k:k + 1],
                                         scale=m.conv_w[:, k, 3:4]).then_inc(S["tap3"], 1)
                    copy(m.xb[:], bank("xb", k)[:]).then_inc(bank_free("xb", k), 1)
                elif name == "th":
                    act.wait_ge(S["conv_done"], 3 * (k + 1))
                    if do_post:
                        act.wait_ge(S["y_gated"], KI)
                    nc.scalar.activation(m.th[:, k % 2, :], m.cv[:], ACT.Tanh, scale=0.5).then_inc(S["cv_tanh"], 1)
                elif name == "dt":
                    wait_bank_full(act, "dt", k)
                    nc.scalar.activation(m.dt[other][:, k, :], bank("dt", k)[:], ACT.Tanh, bias=m.dt_bias[:, k:k + 1],
                                         scale=0.5).then_inc(bank_free("dt", k), 1)

            if do_scan:
                decay(0)
            for slot in range(last_slot):
                if do_scan and slot + 1 < SCAN_SLOTS:
                    decay(slot + 1)
                for name, k in steps_at(slot, *tables(ACT_POST, ACT_PRE)):
                    step(name, k)

        @block.vector
        def _(dve):
            stt = nc.vector.scalar_tensor_tensor
            ts = nc.vector.tensor_scalar

            def norm_stats(which, src):
                st, mv = m.small[f"st{which}"], m.small[f"mv{which}"]
                for b in range(GB):
                    nc.vector.bn_stats(st[:, 6 * b:6 * b + 6], src[:, b, :]).then_inc(S[f"bn{which}"], 1)
                for b in range(GB):
                    dve.wait_ge(S[f"bn{which}"], b + 1)
                    nc.vector.bn_aggr(mv[:, 2 * b:2 * b + 2], st[:, 6 * b:6 * b + 6]).then_inc(S[f"mv{which}_ready"], 1)

            def step(name, k):
                if name == "mb":
                    dve.wait_ge(S["mask_in"], 16)
                    ts(m.mask_neg[:], m.mask_all[:], 0.0, MASKED, ALU.is_equal, ALU.mult).then_inc(S["mask_neg"], 1)
                elif name == "z":
                    dve.wait_ge(S["z_tanh"], k + 1)
                    stt(m.th[:, k % 2, :], m.th[:, k % 2, :], 1.0, bank("z", k)[:], ALU.add, ALU.mult
                        ).then_inc(bank_free("z", k), 1)
                    wait_bank_full(dve, "y", k)
                    xc2 = m.xc2[other][:, k, :]
                    stt(xc2, xc2, m.d_half[:, k:k + 1], bank("y", k)[:], ALU.mult, ALU.add).then_inc(bank_free("y", k), 1)
                    wait_bank_read(dve, "z", k)
                    wait_bank_read(dve, "y", k)
                    nc.vector.tensor_tensor(xc2, xc2, m.th[:, k % 2, :], ALU.mult).then_inc(S["y_gated"], 1)
                elif name in ("o", "xo", "dn"):
                    wait_bank_full(dve, name, k)
                    x = m.x1[:, 2 * k:2 * k + 2, :]
                    if name == "o":
                        dve.wait_ge(S["x_res"], 16)
                    else:
                        wait_bank_read(dve, "o" if name == "xo" else "xo", k)
                    nc.vector.tensor_tensor(x, x, bank(name, k)[:].rearrange("p (b f) -> p b f", f=D), ALU.add
                                            ).then_inc(bank_free(name, k), 1)
                elif name == "ln1":
                    dve.wait_ge(S["x_in"], 16)
                    norm_stats(1, m.xin)
                elif name == "ln2":
                    wait_bank_read(dve, "o", 0)
                    wait_bank_read(dve, "o", 1)
                    norm_stats(2, m.x1)
                elif name == "ln3":
                    wait_bank_read(dve, "xo", 0)
                    wait_bank_read(dve, "xo", 1)
                    norm_stats(3, m.x1)
                elif name == "q":
                    wait_bank_full(dve, "q", k)
                    dve.wait_ge(S["mask_in"], 16)
                    stt(m.q_up[:, k, :], bank("q", k)[:], m.b_tgt[:, k:k + 1], m.mask_all[:], ALU.add, ALU.mult
                        ).then_inc(bank_free("q", k), 1)
                elif name == "s":
                    wait_bank_full(dve, "s", k)
                    dve.wait_ge(S["mask_neg"], 1)
                    if k >= 2:
                        wait_bank_full(dve, "a", k - 2)
                    stt(m.sc[:, k % 2, :], bank("s", k)[:], ATT_SCALE, m.mask_neg[:], ALU.mult, ALU.add
                        ).then_inc(bank_free("s", k), 1)
                    wait_bank_read(dve, "s", k)
                    nc.vector.tensor_reduce(m.small["nmax"][:, GB * k:GB * (k + 1)],
                                            m.sc[:, k % 2, :].rearrange("p (b t) -> p b t", b=GB), AX.X, ALU.max,
                                            negate=True).then_inc(S["neg_max"], 1)
                elif name == "r":
                    dve.wait_ge(S["att_exp"], GB * HC * (k + 1))
                    w = HC * GB
                    nc.vector.reciprocal(m.small["rec"][:, w * k:w * (k + 1)], m.small["sum"][:, w * k:w * (k + 1)]
                                         ).then_inc(S["rec_ready"], 1)
                elif name == "av":
                    wait_bank_full(dve, "av", k)
                    dve.wait_ge(S["rec_ready"], k + 1)
                    w = HC * GB
                    rec = m.small["rec"][:, w * k:w * (k + 1)].rearrange("p (j b) -> p b j", b=GB)
                    nc.vector.tensor_tensor(m.upd[:, :, k * P:(k + 1) * P].rearrange("p b (j f) -> p b j f", f=HD),
                                            bank("av", k)[:].rearrange("p (b j f) -> p b j f", b=GB, f=HD),
                                            rec.unsqueeze(3).broadcast_to([P, GB, HC, HD]), ALU.mult
                                            ).then_inc(bank_free("av", k), 1)
                elif name == "lg":
                    wait_bank_full(dve, "lg")
                    lg = bank("lg")[:, 0:GB * E].rearrange("p (b e) -> p b e", e=E)
                    v3 = lambda t: m.small[t][:].rearrange("p (b e) -> p b e", e=E)
                    row = lambda t: m.small[t][:].unsqueeze(2).broadcast_to([P, GB, E])
                    first = m.first[:].unsqueeze(1).broadcast_to([P, GB, E])
                    nc.vector.tensor_reduce(m.small["mx"][:], lg, AX.X, ALU.max).then_inc(S["top_logit"], 1)
                    dve.wait_ge(S["top_logit"], 1)
                    nc.vector.tensor_tensor(v3("eq"), lg, row("mx"), ALU.is_equal).then_inc(bank_free("lg"), 1)
                    wait_bank_read(dve, "lg")
                    nc.vector.tensor_tensor(v3("eq"), v3("eq"), first, ALU.mult).then_inc(S["route"], 1)
                    dve.wait_ge(S["route"], 1)
                    nc.vector.tensor_reduce(m.small["m8"][:], v3("eq"), AX.X, ALU.max).then_inc(S["route"], 1)
                    dve.wait_ge(S["route"], 2)
                    nc.vector.tensor_tensor(v3("oh"), first, row("m8"), ALU.is_equal).then_inc(S["onehot"], 1)
                elif name == "g":
                    dve.wait_ge(S["g_tanh"], k + 1)
                    if k == 0:
                        wait_bank_full(dve, "av", 1)
                    x = m.kv_act[:, k, :]
                    stt(x, m.sc[:, k % 2, :], 1.0, bank("g", k)[:], ALU.add, ALU.mult).then_inc(bank_free("g", k), 1)
                    wait_bank_read(dve, "g", k)
                    wait_bank_full(dve, "u", k)
                    nc.vector.tensor_tensor(x, x, bank("u", k)[:], ALU.mult).then_inc(bank_free("u", k), 1)
                elif name == "cv":
                    wait_bank_read(dve, "xb", k)
                    dve.wait_ge(S["tap3"], k + 1)
                    cv = m.cv[:].rearrange("p (b t) -> p b t", b=GB)
                    xb = m.xb[:].rearrange("p (b t) -> p b t", b=GB)
                    for j in range(1, 4):
                        if j > 1:
                            dve.wait_ge(S["conv_done"], 3 * k + j - 1)
                        stt(cv[:, :, j:P], xb[:, :, 0:P - j], m.conv_w[:, k, 3 - j:4 - j], cv[:, :, j:P], ALU.mult, ALU.add
                            ).then_inc(S["conv_done"], 1)
                elif name == "xc":
                    dve.wait_ge(S["cv_tanh"], k + 1)
                    if do_post:
                        wait_bank_full(dve, "o", 1)
                    stt(m.xc2[other][:, k, :], m.th[:, k % 2, :], 1.0, m.cv[:], ALU.add, ALU.mult
                        ).then_inc(S["xc2_ready"], 1)
                elif name == "ct":
                    wait_bank_full(dve, "ct")
                    nc.vector.tensor_copy(m.c_tok[other][:].rearrange("p b n -> p (b n)"), bank("ct")[:, 0:GB * NS]
                                          ).then_inc(bank_free("ct"), 1)
                elif name == "dt":
                    wait_bank_read(dve, "dt", k)
                    d = m.dt[other][:, k, :]
                    half = 0.5 * (DT_MAX - DT_MIN)
                    ts(d, d, half, half + DT_MIN, ALU.mult, ALU.add).then_inc(S["dt_lin"], 1)
                    dve.wait_ge(S["dt_lin"], k + 1)
                    ts(d, d, 1e-4, None, ALU.max).then_inc(S["dt_ready"], 1)

            for slot in range(last_slot):
                if do_scan and slot < SCAN_SLOTS:
                    n, c = slot // KI, slot % KI
                    dve.wait_ge(S["dA_ready"], slot + 1)
                    dve.wait_ge(S["u_ready"], n + 1)
                    if n >= 2:
                        dve.wait_ge(S["hT_ready"], KI * (n - 1))
                    nc.vector.tensor_tensor_scan(m.h[:, n % 2, c, :], m.dA[slot % 2][:], m.u[:, n % 2, c, :], 0.0,
                                                 ALU.mult, ALU.add).then_inc(S["h_ready"], 1)
                if do_scan and slot >= KI:
                    i = slot - KI
                    n, b = i // KI, i % KI
                    dve.wait_ge(S["hT_ready"], i + 1)
                    cn = m.c_tok[parity][:, b, n:n + 1]
                    if n == 0:
                        if do_post:
                            wait_bank_full(dve, "y", KI - 1)
                        ts(m.acc[:, b, :], m.hT[i % 2][:], cn, None, ALU.mult).then_inc(S["acc_done"], 1)
                    else:
                        dve.wait_ge(S["acc_done"], i - KI + 1)
                        stt(m.acc[:, b, :], m.hT[i % 2][:], cn, m.acc[:, b, :], ALU.mult, ALU.add
                            ).then_inc(S["acc_done"], 1)
                for name, k in steps_at(slot, *tables(DVE_POST, DVE_PRE)):
                    step(name, k)

        @block.gpsimd
        def _(pool):
            tt, ts = nc.gpsimd.tensor_tensor, nc.gpsimd.tensor_scalar

            def drive(n):
                pool.wait_ge(S[f"bb{n % 4}"], 16 * (n // 4 + 1))
                if n >= 2:
                    pool.wait_ge(S["h_ready"], KI * (n - 1))
                tt(m.u[:, n % 2, :, :], m.dtx[parity][:], m.bb[:, n % 4, :].unsqueeze(1).broadcast_to([P, KI, GT]),
                   ALU.mult).then_inc(S["u_ready"], 1)

            def normalise(which, src, dst):
                mv, rs = m.small[f"mv{which}"], m.small[f"rs{which}"]
                pool.wait_ge(S[f"mv{which}_ready"], GB)
                ts(rs[:], mv[:].rearrange("p (b v) -> p b v", v=2)[:, :, 1], EPS, None, ALU.add).then_inc(S[f"rs{which}"], 1)
                pool.wait_ge(S[f"rs{which}"], 1)
                tt(rs[:], rs[:], m.minus_half[:], ALU.pow).then_inc(S[f"rs{which}"], 1)
                pool.wait_ge(S[f"rs{which}"], 2)
                for b in range(GB):
                    ts(dst[:, b, :], src[:, b, :], mv[:, 2 * b:2 * b + 1], rs[:, b:b + 1], ALU.subtract, ALU.mult
                       ).then_inc(S[f"ln{which}_ready"], 1)

            def step(name, k):
                if name == "cm":
                    pool.wait_ge(S["ctx_in"], 16)
                    pool.wait_ge(S["mask_in"], 16)
                    tt(m.ctx_at[:], m.ctx_at[:], m.mask_all[:].unsqueeze(1).broadcast_to([P, KC, GT]), ALU.mult
                       ).then_inc(S["ctx_masked"], 1)
                elif name == "ln1":
                    normalise(1, m.xin, m.xin)
                elif name == "ln2":
                    normalise(2, m.x1, m.xn)
                elif name == "ln3":
                    normalise(3, m.x1, m.xn)
                elif name == "xs":
                    pool.wait_ge(S["top_tanh"], 1)
                    ts(m.small["score"][:], m.small["top"][:], 0.5, 0.5, ALU.mult, ALU.add).then_inc(S["score"], 1)
                    pool.wait_ge(S["score"], 1)
                    wait_bank_full(pool, "t3", 1)
                    tt(m.xn[:], m.xn[:], m.small["score"][:].unsqueeze(2).broadcast_to([P, GB, D]), ALU.mult
                       ).then_inc(S["xs_ready"], 1)
                elif name == "dx":
                    pool.wait_ge(S["dt_ready"], k + 1)
                    tt(m.dtx[other][:, k, :], m.dt[other][:, k, :], m.xc2[other][:, k, :], ALU.mult).then_inc(S["dtx_ready"], 1)

            if do_scan:
                drive(0)
            for slot in range(last_slot):
                if do_scan and slot % KI == 0 and slot // KI + 1 < NS:
                    drive(slot // KI + 1)
                for name, k in steps_at(slot, *tables(POOL_POST, POOL_PRE)):
                    step(name, k)

    with nc.Block() as block:
        @block.gpsimd
        def _(pool):
            for s in S.values():
                pool.sem_clear(s)


A_SEMS = ("acc_done", "att_exp", "bank_free0", "bank_free1", "bank_free2", "bank_free3", "bank_full", "bb0", "bb1",
          "bb2", "bb3", "bn1", "bn2", "bn3", "conv_done", "ctx_in", "ctx_masked", "cv_tanh", "dA_ready", "dt_lin",
          "dt_ready", "dtx_ready", "g_tanh", "hT_ready", "h_ready", "ln1_ready", "ln2_ready", "ln3_ready", "mask_in",
          "mask_neg", "mv1_ready", "mv2_ready", "mv3_ready", "neg_max", "onehot", "rec_ready", "route", "rs1", "rs2",
          "rs3", "score", "stored", "tap3", "top_logit", "top_tanh", "u_ready", "x_in", "x_res", "xc2_ready",
          "xs_ready", "y_gated", "z_tanh")


def phase_a(nc, a):
    with ExitStack() as ctx:
        m = Memory()
        phase_a_memory(nc, ctx, m)
        banks = [ctx.enter_context(nc.psum_tensor(f"bank{i}", [P, GT], F32)) for i in range(8)]
        m.dA, m.hT, m.other = banks[0:2], banks[2:4], banks[4:8]
        ws = {n: ctx.enter_context(nc.semaphore("s_" + n)) for n in ("w", "w_clear", "w_loaded", "id", "iota", "a_exp", "zero")}
        S = {n: ctx.enter_context(nc.semaphore("s_" + n)) for n in A_SEMS}
        setup(nc, m, a, ws)
        iteration(nc, m, a, S, pre=0, parity=1)
        iteration(nc, m, a, S, scan=0, pre=1, parity=0)
        with nc.Fori(0, GROUPS // 2 - 1) as j:
            iteration(nc, m, a, S, scan=2 * j + 1, post=2 * j, pre=2 * j + 2, parity=1)
            iteration(nc, m, a, S, scan=2 * j + 2, post=2 * j + 1, pre=2 * j + 3, parity=0)
        iteration(nc, m, a, S, scan=GROUPS - 1, post=GROUPS - 2, parity=1)
        iteration(nc, m, a, S, post=GROUPS - 1, parity=0)


def phase_b_to_d(nc, a):
    sorted_tiles = SEQS
    with ExitStack() as ctx:
        def sb(name, shape, dtype=F32):
            return ctx.enter_context(nc.sbuf_tensor(name, shape, dtype))

        def sem(name):
            return ctx.enter_context(nc.semaphore(name))

        w_gate = sb("e_gate", [P, E * KD * FF])
        w_up = sb("e_up", [P, E * KD * FF])
        w_down = sb("e_down", [P, E * KF * D])
        tok = sb("tok", [P, SEQS, D])
        base = sb("e_base", [P, SEQS // 2, D])
        oh = sb("oh_all", [P, SEQS, E])
        before = sb("before", [P, P])
        ones = sb("e_ones", [P, P])
        ident = sb("e_ident", [P, P])
        incl = sb("incl", [P, SEQS, E])
        rank = sb("rank", [P, SEQS, E])
        steps_i = sb("steps_i", [P, SEQS], I32)
        steps = sb("steps", [P, SEQS])
        tile_i = sb("tile_i", [P, TILES], I32)
        tile_f = sb("tile_f", [P, TILES])
        more = sb("more", [P, E, SEQS])
        past = sb("past", [P, TILES, E])
        need = sb("need", [P, E])
        ends = sb("ends", [P, E])
        starts = sb("starts", [P, E])
        pos_f = sb("pos_f", [P, SEQS])
        pos = sb("pos", [P, SEQS], U32)
        owner_f = sb("owner_f", [P, TILES])
        owner = sb("owner", [P, TILES], I32)
        x = sb("e_x", [P, 3, D])
        xT = sb("e_xT", [P, 2, KD, P])
        act_t = sb("e_act", [P, 2, FF])
        th = sb("e_th", [P, 2, FF])
        actT = sb("e_actT", [P, 2, KF, P])
        y = sb("e_y", [P, 2, D])
        psum = [ctx.enter_context(nc.psum_tensor(f"e_bank{i}", [P, FF], F32)) for i in range(8)]
        s_wg, s_oh, s_tok, s_const, s_iota, s_pe, s_seq, s_pos, s_owner, s_scat = (
            sem("t_" + n) for n in ("weights", "onehot", "tokens", "const", "iota", "counts", "chain", "pos", "owner",
                                    "scattered"))

        with nc.Block() as block:
            @block.sync
            def _(sp):
                sp.dma_start(oh[:].rearrange("p (g b) e -> p g (b e)", g=GROUPS),
                             a["onehot"].rearrange("(g p) c -> p g c", p=P)).then_inc(s_oh, 16)
                sp.dma_start(tok[:], a["xs"].rearrange("(s p) c -> p s c", p=P)).then_inc(s_tok, 16)
                for dst, src, kk in ((w_gate, a["rt_gate"], KD), (w_up, a["rt_up"], KD), (w_down, a["rt_down"], KF)):
                    sp.dma_start(dst[:].rearrange("p (k n) -> p k n", k=E * kk),
                                 src.rearrange("e (k p) n -> p (e k) n", p=P)).then_inc(s_wg, 16)

            @block.gpsimd
            def _(pool):
                gp = nc.gpsimd
                gp.memset(ident[:], 0.0).then_inc(s_iota, 1)
                gp.memset(before[:], 1.0).then_inc(s_iota, 1)
                gp.iota(steps_i[:], [[P, SEQS]], base=0, channel_multiplier=0).then_inc(s_iota, 1)
                gp.iota(tile_i[:], [[1, TILES]], base=0, channel_multiplier=0).then_inc(s_iota, 1)
                pool.wait_ge(s_iota, 4)
                gp.affine_select(out=ident[:], in_=ident[:], compare_op=ALU.not_equal, fill=1.0, base=0,
                                 pattern=[[-1, P]], channel_multiplier=1).then_inc(s_const, 1)
                gp.affine_select(out=before[:], in_=before[:], compare_op=ALU.is_gt, fill=0.0, base=0,
                                 pattern=[[1, P]], channel_multiplier=-1).then_inc(s_const, 1)
                pool.wait_ge(s_pos, 1)
                pool.wait_ge(s_tok, 16)
                for t in range(SEQS):
                    gp.indirect_dma_start(a["x_slots"], bass.IndirectOffsetOnAxis(ap=pos[:, t:t + 1], axis=0),
                                          tok[:, t, :], None).then_inc(s_scat, 16)
                pool.wait_ge(s_scat, 16 * SEQS)
                pool.wait_ge(s_wg, 48)

            @block.tensor
            def _(pe):
                pe.wait_ge(s_oh, 16)
                pe.wait_ge(s_const, 2)
                pe.wait_ge(s_seq, 1)
                flat = oh[:].rearrange("p s e -> p (s e)")
                nc.tensor.matmul(psum[0][:, 0:SEQS * E], before[:], flat, start=True, stop=True)
                nc.tensor.matmul(psum[1][:, 0:SEQS * E], ones[:], flat, start=True, stop=True).then_inc(s_pe, 1)

            @block.vector
            def _(dve):
                chain = [0]

                def link(ins):
                    chain[0] += 1
                    ins.then_inc(s_seq, 1)
                    dve.wait_ge(s_seq, chain[0])

                v = nc.vector
                link(v.memset(ones[:], 1.0))
                dve.wait_ge(s_iota, 4)
                link(v.tensor_copy(steps[:], steps_i[:]))
                link(v.tensor_copy(tile_f[:], tile_i[:]))
                dve.wait_ge(s_pe, 1)
                in_tile = psum[0][:, 0:SEQS * E].rearrange("p (s e) -> p s e", e=E)
                counts = psum[1][:, 0:SEQS * E].rearrange("p (s e) -> p s e", e=E)
                for e in range(E):
                    ins = v.tensor_tensor_scan(incl[:, :, e], ones[:, 0:SEQS], counts[:, :, e], 0.0, ALU.mult, ALU.add)
                link(ins)
                total = incl[:, SEQS - 1, :]
                link(v.tensor_tensor(more[:], total.unsqueeze(2).broadcast_to([P, E, SEQS]),
                                     steps[:].unsqueeze(1).broadcast_to([P, E, SEQS]), ALU.is_gt))
                link(v.tensor_reduce(need[:], more[:], AX.X, ALU.add))
                link(v.tensor_tensor_scan(ends[:], ones[:, 0:E], need[:], 0.0, ALU.mult, ALU.add))
                link(v.tensor_tensor(starts[:], ends[:], need[:], ALU.subtract))
                link(v.tensor_scalar(starts[:], starts[:], float(P), None, ALU.mult))
                link(v.tensor_tensor(rank[:], incl[:], counts, ALU.subtract))
                link(v.tensor_tensor(rank[:], rank[:], in_tile, ALU.add))
                link(v.tensor_tensor(rank[:], rank[:], starts[:].unsqueeze(1).broadcast_to([P, SEQS, E]), ALU.add))
                link(v.tensor_tensor(rank[:], rank[:], oh[:], ALU.mult))
                link(v.tensor_reduce(pos_f[:], rank[:], AX.X, ALU.add))
                v.tensor_copy(pos[:], pos_f[:]).then_inc(s_pos, 1)
                link(v.tensor_tensor(past[:], ends[:].unsqueeze(1).broadcast_to([P, TILES, E]),
                                     tile_f[:].unsqueeze(2).broadcast_to([P, TILES, E]), ALU.is_le))
                link(v.tensor_reduce(owner_f[:], past[:], AX.X, ALU.add))
                link(v.tensor_scalar(owner_f[:], owner_f[:], float(E - 1), None, ALU.min))
                v.tensor_copy(owner[:], owner_f[:]).then_inc(s_owner, 1)

        S = {n: sem("c_" + n) for n in ("x0", "x1", "x2", "xT_full", "xT_read", "gu_full", "tanh", "g_read", "u_read",
                                        "aT_full", "aT_read", "y_full", "y_read", "stored0", "stored1")}
        xT_bank, y_bank = psum[0], psum[1]
        g_bank, u_bank, aT_bank = psum[2:4], psum[4:6], psum[6:8]
        with nc.Fori(0, TILES // TPB) as it:
            with nc.Block() as block:
                @block.sync
                def _(sp):
                    def load(j):
                        sp.dma_start(x[:, j % 3, :], a["x_slots"][bass.ts(it * TPB + j, P), :]).then_inc(S[f"x{j % 3}"], 16)

                    for j in range(3):
                        load(j)
                    for j in range(TPB):
                        if j + 3 < TPB:
                            sp.wait_ge(S["xT_full"], j + 1)
                            load(j + 3)
                        sp.wait_ge(S["y_read"], j + 1)
                        sp.dma_start(a["y_slots"][bass.ts(it * TPB + j, P), :], y[:, j % 2, :]).then_inc(S[f"stored{j % 2}"], 16)
                    for i in range(2):
                        sp.wait_ge(S[f"stored{i}"], 16 * ((TPB + 1 - i) // 2))

                @block.tensor
                def _(pe):
                    def transpose_x(j):
                        pe.wait_ge(S[f"x{j % 3}"], 16 * (j // 3 + 1))
                        if j >= 1:
                            pe.wait_ge(S["xT_read"], j)
                        for k in range(KD):
                            ins = nc.tensor.transpose(xT_bank[:, k * P:(k + 1) * P], x[:, j % 3, k * P:(k + 1) * P], ident[:])
                        ins.then_inc(S["xT_full"], 1)

                    def gate_up(j):
                        e = nc.tensor.value_load(owner[0:1, bass.ds(it * TPB + j, 1)], min_val=0, max_val=E - 1)
                        pe.wait_ge(S["xT_read"], j + 1)
                        if j >= 2:
                            pe.wait_ge(S["u_read"], j - 1)
                        for out, w in ((g_bank[j % 2], w_gate), (u_bank[j % 2], w_up)):
                            for k in range(KD):
                                ins = nc.tensor.matmul(out[:], xT[:, j % 2, k, :], w[:, bass.ds(e * (KD * FF) + k * FF, FF)],
                                                       start=(k == 0), stop=(k == KD - 1))
                        ins.then_inc(S["gu_full"], 1)
                        return e

                    def transpose_act(j):
                        pe.wait_ge(S["u_read"], j + 1)
                        if j >= 2:
                            pe.wait_ge(S["aT_read"], j - 1)
                        for k in range(KF):
                            ins = nc.tensor.transpose(aT_bank[j % 2][:, k * P:(k + 1) * P], act_t[:, j % 2, k * P:(k + 1) * P],
                                                      ident[:])
                        ins.then_inc(S["aT_full"], 1)

                    def down(j, e):
                        pe.wait_ge(S["aT_read"], j + 1)
                        if j >= 1:
                            pe.wait_ge(S["y_read"], j)
                        for k in range(KF):
                            ins = nc.tensor.matmul(y_bank[:, 0:D], actT[:, j % 2, k, :], w_down[:, bass.ds(e * (KF * D) + k * D, D)],
                                                   start=(k == 0), stop=(k == KF - 1))
                        ins.then_inc(S["y_full"], 1)

                    transpose_x(0)
                    e_before = None
                    for j in range(TPB + 1):
                        if j + 1 < TPB:
                            transpose_x(j + 1)
                        if j < TPB:
                            e_now = gate_up(j)
                        if j >= 1:
                            transpose_act(j - 1)
                            down(j - 1, e_before)
                        e_before = e_now

                @block.scalar
                def _(act):
                    def copy_xT(j):
                        act.wait_ge(S["xT_full"], j + 1)
                        if j >= 2:
                            act.wait_ge(S["gu_full"], j - 1)
                        nc.scalar.activation(xT[:, j % 2].rearrange("p k t -> p (k t)"), xT_bank[:, 0:D], ACT.Copy
                                             ).then_inc(S["xT_read"], 1)

                    copy_xT(0)
                    for j in range(TPB + 1):
                        if j + 1 < TPB:
                            copy_xT(j + 1)
                        if j >= 1:
                            act.wait_ge(S["aT_full"], j)
                            if j >= 3:
                                act.wait_ge(S["y_full"], j - 2)
                            nc.scalar.activation(actT[:, (j - 1) % 2].rearrange("p k t -> p (k t)"), aT_bank[(j - 1) % 2][:],
                                                 ACT.Copy).then_inc(S["aT_read"], 1)
                        if j < TPB:
                            act.wait_ge(S["gu_full"], j + 1)
                            nc.scalar.activation(th[:, j % 2, :], g_bank[j % 2][:], ACT.Tanh, scale=0.5
                                                 ).then_inc(S["tanh"], 1)

                @block.vector
                def _(dve):
                    for j in range(TPB + 1):
                        if j < TPB:
                            dve.wait_ge(S["tanh"], j + 1)
                            if j >= 2:
                                dve.wait_ge(S["aT_full"], j - 1)
                            t = act_t[:, j % 2, :]
                            nc.vector.scalar_tensor_tensor(t, th[:, j % 2, :], 1.0, g_bank[j % 2][:], ALU.add, ALU.mult
                                                           ).then_inc(S["g_read"], 1)
                            dve.wait_ge(S["g_read"], j + 1)
                            nc.vector.tensor_tensor(t, t, u_bank[j % 2][:], ALU.mult).then_inc(S["u_read"], 1)
                        if j >= 1:
                            dve.wait_ge(S["y_full"], j)
                            if j >= 3:
                                dve.wait_ge(S[f"stored{(j - 1) % 2}"], 16 * ((j - 1) // 2))
                            nc.vector.tensor_scalar(y[:, (j - 1) % 2, :], y_bank[:, 0:D], 0.5, None, ALU.mult
                                                    ).then_inc(S["y_read"], 1)

            with nc.Block() as block:
                @block.gpsimd
                def _(pool):
                    for s in S.values():
                        pool.sem_clear(s)

        s_base, s_gath, s_sum, s_out = (sem("d_" + n) for n in ("base", "gathered", "sum", "out"))
        g_sems = [sem(f"d_got{q}") for q in range(SEQS // GB)]
        with nc.Block() as block:
            @block.gpsimd
            def _(pool):
                for t in range(SEQS):
                    nc.gpsimd.indirect_dma_start(tok[:, t, :], None, a["y_slots"],
                                                 bass.IndirectOffsetOnAxis(ap=pos[:, t:t + 1], axis=0)
                                                 ).then_inc(g_sems[t // GB], 16)

            @block.sync
            def _(sp):
                half = SEQS // 2
                base_rows = a["base"].rearrange("(s p) c -> p s c", p=P)
                out_rows = a["out"].rearrange("(s p) c -> p s c", p=P)
                sp.dma_start(base[:], base_rows[:, 0:half, :]).then_inc(s_base, 16)
                for q in range(SEQS // GB):
                    if q == half // GB:
                        sp.wait_ge(s_sum, half // GB)
                        sp.dma_start(base[:], base_rows[:, half:SEQS, :]).then_inc(s_base, 16)
                    sp.wait_ge(s_sum, q + 1)
                    sp.dma_start(out_rows[:, q * GB:(q + 1) * GB, :], tok[:, q * GB:(q + 1) * GB, :]).then_inc(s_out, 16)
                sp.wait_ge(s_out, 16 * (SEQS // GB))

            @block.vector
            def _(dve):
                for q in range(SEQS // GB):
                    dve.wait_ge(g_sems[q], 16 * GB)
                    dve.wait_ge(s_base, 16 * (1 + q // (SEQS // GB // 2)))
                    b0 = q * GB % (SEQS // 2)
                    t = tok[:, q * GB:(q + 1) * GB, :]
                    nc.vector.tensor_tensor(t, t, base[:, b0:b0 + GB, :], ALU.add).then_inc(s_sum, 1)


TPB = 13
assert TILES % TPB == 0

IN_SHAPES = {"x": (TOKENS, D), "ctxT": (CS, TOKENS), "mask": (1, TOKENS), "w_in": (D, 2 * DI), "conv_w": (DI, 4),
             "conv_b": (P, KI), "w_x": (DI, RANK + 2 * NS), "w_dt": (RANK, DI), "b_dt": (P, KI), "a_log": (DI, NS),
             "d_param": (P, KI), "w_out": (DI, D), "w_srcT": (CS, 2 * D), "b_src": (1, 2 * D), "w_tgtT": (D, D),
             "b_tgt": (P, KD), "w_xoT": (2 * D, D), "b_xo": (1, D), "gate_w": (D, E), "sh_gate": (D, FF),
             "sh_up": (D, FF), "sh_down": (FF, D), "rt_gate": (E, D, FF), "rt_up": (E, D, FF), "rt_down": (E, FF, D)}


def decoder_layer(nc, a):
    a["b_rows"] = nc.dram_tensor("b_rows", (NS, 2 * GT), F32).ap()
    a["onehot"] = nc.dram_tensor("onehot", (GROUPS * P, GB * E), F32).ap()
    a["xs"] = nc.dram_tensor("xs", (TOKENS, D), F32).ap()
    a["base"] = nc.dram_tensor("base", (TOKENS, D), F32).ap()
    a["x_slots"] = nc.dram_tensor("x_slots", (SLOTS_DRAM, D), F32).ap()
    a["y_slots"] = nc.dram_tensor("y_slots", (SLOTS_DRAM, D), F32).ap()
    phase_a(nc, a)
    phase_b_to_d(nc, a)


def kernel(**inputs):
    import numpy as np
    import concourse.bacc as bacc
    from concourse.bass_utils import run_bass_kernel_spmd

    g = {n: np.asarray(v) for n, v in inputs.items()}
    columns = lambda v: v.reshape(-1, P).T
    host = {"x": g["x"].reshape(TOKENS, D), "ctxT": g["ctx_2048"].reshape(TOKENS, CS).T,
            "mask": g["mask_BxS2_fk1"].reshape(1, TOKENS), "w_in": g["L0_attn_W_in"],
            "conv_w": g["L0_attn_conv_w"].reshape(DI, 4), "conv_b": columns(g["L0_attn_conv_b"]),
            "w_x": g["L0_attn_W_x"], "w_dt": g["L0_attn_W_dt"], "b_dt": columns(g["L0_attn_b_dt"]),
            "a_log": g["L0_attn_A_log"], "d_param": columns(g["L0_attn_D_param"]), "w_out": g["L0_attn_W_out"],
            "w_srcT": g["L0_xattn_W_src"].T, "b_src": g["L0_xattn_b_src"].reshape(1, -1), "w_tgtT": g["L0_xattn_W_tgt"].T,
            "b_tgt": columns(g["L0_xattn_b_tgt"]), "w_xoT": g["L0_xattn_W_out"].T,
            "b_xo": g["L0_xattn_b_out"].reshape(1, -1), "gate_w": g["L0_ffn_gate_w"], "sh_gate": g["L0_ffn_sh_gate"],
            "sh_up": g["L0_ffn_sh_up"], "sh_down": g["L0_ffn_sh_down"], "rt_gate": g["L0_ffn_rt_gate"],
            "rt_up": g["L0_ffn_rt_up"], "rt_down": g["L0_ffn_rt_down"]}
    nc = bacc.Bacc("TRN2", target_bir_lowering=False, num_devices=1)
    arrays, a = {}, {}
    for name, shape in IN_SHAPES.items():
        arrays["in_" + name] = np.ascontiguousarray(host[name])
        a[name] = nc.dram_tensor("in_" + name, shape, F32, kind="ExternalInput").ap()
    a["out"] = nc.dram_tensor("out", (TOKENS, D), F32, kind="ExternalOutput").ap()
    decoder_layer(nc, a)
    r = run_bass_kernel_spmd(nc, [arrays], core_ids=[0])
    return r.results[0]["out"].reshape(SEQS, P, D)
```

```python
from contextlib import ExitStack

import concourse.bass as bass
from concourse import mybir

F32 = mybir.dt.float32
I32 = mybir.dt.int32
U32 = mybir.dt.uint32
ALU = mybir.AluOpType
ACT = mybir.ActivationFunctionType
AX = mybir.AxisListType

P = 128
SEQS = 32
GB = 4
GT = GB * P
GROUPS = SEQS // GB
TOKENS = SEQS * P
D = 256
KD = D // P
DI = 512
KI = DI // P
NS = 16
RANK = 64
CS = 512
KC = CS // P
HEADS = 8
HD = D // HEADS
HC = P // HD
E = 8
FF = 512
KF = FF // P
TILES = TOKENS // P + E - 1
DT_MIN, DT_MAX = 0.001, 0.1
EPS = 1e-5
MASKED = -1e30
ATT_SCALE = 1.0 / float(HD) ** 0.5
C_ROW, B_ROW, R_ROW = 0, 32, 64

SCAN_SLOTS = NS * KI
DECAY_BANKS, HT_BANKS, OTHER_BANKS = 2, 3, 3
U_RING = 4
H_RING = 3
HT_LAG = 6
U_AHEAD = 4
ATT_RING = 2
ACC_LAG = 8
SLOTS = SCAN_SLOTS + ACC_LAG

PE_POST = {("z", 0): 2, ("y", 0): 2, ("z", 1): 2, ("y", 1): 2, ("z", 2): 3, ("y", 2): 3, ("z", 3): 5,
           ("y", 3): 4, ("k", 0): 6, ("k", 1): 8, ("o", 0): 8, ("o", 1): 9, ("v", 0): 11, ("v", 1): 12,
           ("t2", 0): 16, ("t2", 1): 18, ("q", 0): 19, ("q", 1): 20, ("s", 0): 21, ("s", 1): 23,
           ("s", 2): 25, ("s", 3): 27, ("s", 4): 29, ("s", 5): 30, ("s", 6): 33, ("s", 7): 35,
           ("a", 0): 24, ("a", 1): 26, ("a", 2): 27, ("a", 3): 30, ("a", 4): 32, ("a", 5): 34,
           ("a", 6): 36, ("a", 7): 39, ("av", 0): 32, ("av", 1): 40, ("ut", 0): 39, ("ut", 1): 44,
           ("xo", 0): 45, ("xo", 1): 45, ("t3", 0): 50, ("t3", 1): 51, ("lg", 0): 53, ("g", 0): 54,
           ("g", 1): 55, ("g", 2): 59, ("g", 3): 60, ("u", 0): 54, ("u", 1): 58, ("u", 2): 60,
           ("u", 3): 60, ("dn", 0): 62, ("dn", 1): 63}
PE_PRE = {("t1", 0): 9, ("t1", 1): 12, ("xb", 0): 16, ("xb", 1): 20, ("xb", 2): 23, ("xb", 3): 31,
          ("xd", 0): 36, ("ct", 0): 43, ("dt", 0): 44, ("dt", 1): 46, ("dt", 2): 49, ("dt", 3): 52}
ACT_POST = {("z", 0): 3, ("z", 1): 3, ("z", 2): 3, ("z", 3): 4, ("k", 0): 7, ("k", 1): 11, ("v", 0): 11,
            ("v", 1): 15, ("n2", 0): 13, ("t2", 0): 17, ("t2", 1): 19, ("s", 0): 22, ("s", 1): 25,
            ("s", 2): 27, ("s", 3): 28, ("s", 4): 30, ("s", 5): 32, ("s", 6): 35, ("s", 7): 38,
            ("a", 0): 24, ("a", 1): 26, ("a", 2): 28, ("a", 3): 31, ("a", 4): 33, ("a", 5): 35,
            ("a", 6): 36, ("a", 7): 39, ("ut", 0): 39, ("ut", 1): 45, ("n3", 0): 49, ("t3", 0): 51,
            ("t3", 1): 51, ("lg", 0): 54, ("g", 0): 55, ("g", 1): 58, ("g", 2): 59, ("g", 3): 64}
ACT_PRE = {("n1", 0): 10, ("t1", 0): 11, ("t1", 1): 15, ("xb", 0): 17, ("xb", 1): 21, ("xb", 2): 25,
           ("xb", 3): 31, ("th", 0): 19, ("th", 1): 23, ("th", 2): 29, ("th", 3): 34, ("xd", 0): 39,
           ("dt", 0): 45, ("dt", 1): 48, ("dt", 2): 50, ("dt", 3): 52}
DVE_POST = {("z", 0): 3, ("z", 1): 3, ("z", 2): 4, ("z", 3): 5, ("o", 0): 9, ("o", 1): 12,
            ("ln2", 0): 12, ("mb", 0): 9, ("q", 0): 20, ("q", 1): 21, ("s", 0): 22, ("s", 1): 23,
            ("s", 2): 26, ("s", 3): 28, ("s", 4): 30, ("s", 5): 30, ("s", 6): 34, ("s", 7): 37,
            ("r", 0): 29, ("r", 1): 38, ("av", 0): 33, ("av", 1): 42, ("xo", 0): 47, ("xo", 1): 47,
            ("ln3", 0): 47, ("lg", 0): 54, ("g", 0): 55, ("g", 1): 59, ("g", 2): 61, ("g", 3): 61,
            ("dn", 0): 64, ("dn", 1): 65}
DVE_PRE = {("ln1", 0): 2, ("cv", 0): 18, ("cv", 1): 22, ("cv", 2): 28, ("cv", 3): 32, ("xc", 0): 20,
           ("xc", 1): 23, ("xc", 2): 29, ("xc", 3): 35, ("ct", 0): 43, ("dt", 0): 44, ("dt", 1): 51,
           ("dt", 2): 52, ("dt", 3): 53}
POOL_POST = {("yz", 0): 4, ("yz", 1): 4, ("yz", 2): 5, ("yz", 3): 6, ("cm", 0): 3, ("ln2", 0): 10,
             ("ln3", 0): 46, ("xs", 0): 63}
POOL_PRE = {("ln1", 0): 1, ("dx", 0): 50, ("dx", 1): 51, ("dx", 2): 51, ("dx", 3): 52}
SP_POST = {("oh", 0): 62, ("xs", 0): 50, ("base", 0): 64}
SP_PRE = {("B", 0): 38, ("bb", 0): 49, ("bb", 1): 51, ("bb", 2): 53, ("bb", 3): 56}


def last_user(place, ring):
    return max(i for i in range(SCAN_SLOTS) if i % ring == place)


def steps_at(slot, *tables):
    return [step for table in tables for step, at in table.items() if at == slot]


class Memory:
    pass


EXPERT_WORDS = E * (2 * KD * FF + KF * D)


def phase_a_memory(nc, ctx, m, shared):
    at = [0]

    def carve(*shape):
        words = 1
        for n in shape:
            words *= n
        piece = shared[:, at[0]:at[0] + words]
        at[0] += words
        assert at[0] <= EXPERT_WORDS
        if len(shape) == 1:
            return piece
        names = "abc"[:len(shape)]
        return piece.rearrange(f"p ({' '.join(names)}) -> p {' '.join(names)}", **dict(zip(names[1:], shape[1:])))

    def sb(name, shape, dtype=F32):
        return ctx.enter_context(nc.sbuf_tensor(name, shape, dtype))

    m.w_in = sb("w_in", [P, KD, 2 * DI])
    m.w_x = carve(KI, P)
    m.w_dt = sb("w_dt", [P, DI])
    m.b_src = m.w_dt[0:1, 0:2 * D]
    m.b_xo, m.ones = m.w_dt[32:33, 0:D], m.w_dt[32:33, D:D + P]
    m.w_out = sb("w_out", [P, KI, D])
    m.w_src = sb("w_src", [P, KC, 2 * D])
    m.w_tgt = sb("w_tgt", [P, KD, D])
    m.w_xo = sb("w_xo", [P, 2 * KD, D])
    m.sh_gate = sb("sh_gate", [P, KD, FF])
    m.sh_up = sb("sh_up", [P, KD, FF])
    m.sh_down = sb("sh_down", [P, KF, D])
    m.gate_w = sb("gate_w", [P, KD, E])
    m.a_neg = sb("a_neg", [P, KI, NS])
    m.conv_w = sb("conv_w", [P, KI, 4])
    m.conv_b = sb("conv_b", [P, KI])
    m.dt_bias = sb("dt_bias", [P, KI])
    m.d_half = sb("d_half", [P, KI])
    m.b_tgt = sb("b_tgt", [P, KD])
    m.ident = sb("ident", [P, P])
    m.first = sb("first", [P, E])
    m.first_i = sb("first_i", [P, E], I32)
    m.minus_half = sb("minus_half", [P, GB])
    m.xn1T = [carve(KD, GT), sb("xn1T1", [P, KD, GT])]
    m.xc2 = [carve(KI, GT), sb("xc2_1", [P, KI, GT])]
    m.dt = [carve(KI, GT) for i in range(2)]
    m.dtx = [carve(KI, GT) for i in range(2)]
    m.c_tok = [sb(f"c_tok{i}", [P, GB, NS]) for i in range(2)]
    m.acc = sb("acc", [P, GB, DI])
    m.bb = carve(4, GT)
    m.u = carve(U_RING, GT)
    m.h = carve(H_RING, KI, GT)
    m.xin = carve(GB, D)
    m.xb = carve(GT)
    m.cv = carve(GT)
    m.th = sb("th", [P, 2, GT])
    m.xdT = carve(GT)
    m.x1 = sb("x1", [P, GB, D])
    m.xn = sb("xn", [P, GB, D])
    m.xnT = sb("xnT", [P, KD, GT])
    m.ctx_at = sb("ctx_at", [P, KC, GT])
    m.kv_act = sb("kv_act", [P, 4, GT])
    m.q_up = sb("q_up", [P, KD, GT])
    m.sc = sb("sc", [P, ATT_RING, GT])
    m.upd = sb("upd", [P, GB, D])
    m.mask_all = sb("mask_all", [P, GT])
    m.mask_neg = sb("mask_neg", [P, GT])
    m.small = {}
    for name, w in (("st1", 24), ("st2", 24), ("st3", 24), ("mv1", 8), ("mv2", 8), ("mv3", 8), ("rs1", 4), ("rs2", 4),
                    ("rs3", 4), ("nb1", 4), ("nb2", 4), ("nb3", 4), ("nmax", 32), ("sum", 32), ("rec", 32), ("mx", 4), ("eq", 32), ("m8", 4), ("oh", 32),
                    ("top", 4), ("score", 4)):
        m.small[name] = sb("s_" + name, [P, w])


def split_banks(m, banks):
    m.dA, m.hT = banks[0:DECAY_BANKS], banks[DECAY_BANKS:DECAY_BANKS + HT_BANKS]
    m.other = banks[DECAY_BANKS + HT_BANKS:DECAY_BANKS + HT_BANKS + OTHER_BANKS]


def setup(nc, m, a, sems):
    with nc.Block() as block:
        @block.sync
        def _(sp):
            def load(dst, src):
                sp.dma_start(dst, src).then_inc(sems["w"], 16)
                load.n += 16
            load.n = 0
            load(m.w_in[:], a["w_in"].rearrange("(k p) n -> p k n", p=P))
            sp.wait_ge(sems["w_clear"], 1)
            wx = a["w_x"].rearrange("(k p) n -> p k n", p=P)
            load(m.w_x[:, :, R_ROW:R_ROW + RANK], wx[:, :, 0:RANK])
            load(m.w_x[:, :, B_ROW:B_ROW + NS], wx[:, :, RANK:RANK + NS])
            load(m.w_x[:, :, C_ROW:C_ROW + NS], wx[:, :, RANK + NS:RANK + 2 * NS])
            load(m.w_dt[R_ROW:R_ROW + RANK, :], a["w_dt"])
            load(m.a_neg[:], a["a_log"].rearrange("(k p) n -> p k n", p=P))
            load(m.conv_w[:], a["conv_w"].rearrange("(k p) n -> p k n", p=P))
            load(m.conv_b[:], a["conv_b"])
            load(m.dt_bias[:], a["b_dt"])
            load(m.d_half[:], a["d_param"])
            load(m.b_tgt[:], a["b_tgt"])
            load(m.b_src, a["b_src"])
            load(m.b_xo, a["b_xo"])
            sp.wait_ge(sems["w"], load.n)
            sp.sem_inc(sems["w_loaded"], 1)

        @block.gpsimd
        def _(pool):
            nc.gpsimd.memset(m.x1[:, 0, :], 0.0).then_inc(sems["zero"], 1)
            nc.gpsimd.memset(m.ident[:], 0.0).then_inc(sems["id"], 1)
            pool.wait_ge(sems["id"], 1)
            nc.gpsimd.affine_select(out=m.ident[:], in_=m.ident[:], compare_op=ALU.not_equal, fill=1.0, base=0,
                                    pattern=[[-1, P]], channel_multiplier=1).then_inc(sems["id"], 1)
            nc.gpsimd.iota(m.first_i[:], [[-1, E]], base=E, channel_multiplier=0).then_inc(sems["iota"], 1)

        @block.scalar
        def _(act):
            act.wait_ge(sems["w_loaded"], 1)
            nc.scalar.activation(m.a_neg[:], m.a_neg[:], ACT.Exp).then_inc(sems["a_exp"], 1)

        @block.vector
        def _(dve):
            nc.vector.memset(m.w_x[:], 0.0).then_inc(sems["w_clear"], 1)
            nc.vector.memset(m.ones, 1.0)
            nc.vector.memset(m.minus_half[:], -0.5)
            for bank in m.dA:
                nc.vector.memset(bank.rearrange("p (b t) -> p b t", b=GB)[:, :, 0:1], 0.0)
            dve.wait_ge(sems["iota"], 1)
            nc.vector.tensor_copy(m.first[:], m.first_i[:])
            dve.wait_ge(sems["w_loaded"], 1)
            for t, f in ((m.dt_bias[:], 0.5), (m.d_half[:], 0.5),
                         (m.w_x[:, :, C_ROW:C_ROW + NS], 0.5), (m.w_x[:, :, B_ROW:B_ROW + NS], 0.25),
                         (m.w_x[:, :, R_ROW:R_ROW + RANK], 0.5)):
                nc.vector.tensor_scalar(t, t, f, None, ALU.mult)
            dve.wait_ge(sems["a_exp"], 1)
            nc.vector.tensor_scalar(m.a_neg[:], m.a_neg[:], -1.0, None, ALU.mult)


def late_loads(m, a):
    whole = lambda t: t.rearrange("(k p) n -> p k n", p=P)
    loads = [(m.w_out[:], whole(a["w_out"])), (m.w_src[:], whole(a["w_srcT"])), (m.w_tgt[:], whole(a["w_tgtT"])),
             (m.w_xo[:], whole(a["w_xoT"])), (m.sh_gate[:], whole(a["sh_gate"])), (m.sh_up[:], whole(a["sh_up"])),
             (m.sh_down[:], whole(a["sh_down"])), (m.gate_w[:], whole(a["gate_w"]))]
    return loads + [(a[name][TOKENS:TOKENS + P, :], m.x1[:, 0, :]) for name in ("xs", "out")]


def halve_late(nc, m):
    with nc.Block() as block:
        @block.vector
        def _(dve):
            for t in (m.w_out[:], m.sh_down[:]):
                nc.vector.tensor_scalar(t, t, 0.5, None, ALU.mult)


def iteration(nc, m, a, S, scan=None, post=None, pre=None, parity=0, loads=()):
    do_scan, do_post, do_pre = scan is not None, post is not None, pre is not None
    other = 1 - parity
    tables = lambda p, q: ([p] if do_post else []) + ([q] if do_pre else [])
    order = [step for slot in range(SLOTS) for step in steps_at(slot, *tables(PE_POST, PE_PRE))]
    number = {step: i for i, step in enumerate(order)}
    banks = m.other + ([] if do_scan else m.hT) + ([] if do_scan or do_pre else m.dA)
    n_banks = len(banks)
    last_slot = SLOTS

    def bank(name, k=0):
        return banks[number[name, k] % n_banks]

    def wait_bank_free(pe, name, k):
        i = number[name, k]
        if i >= n_banks:
            pe.wait_ge(S[f"bank_free{i % n_banks}"], i // n_banks)

    def wait_bank_full(eng, name, k=0):
        eng.wait_ge(S["bank_full"], number[name, k] + 1)

    def wait_bank_read(eng, name, k=0):
        eng.wait_ge(S[f"bank_free{number[name, k] % n_banks}"], number[name, k] // n_banks + 1)

    def bank_free(name, k=0):
        return S[f"bank_free{number[name, k] % n_banks}"]

    k_ap, v_ap = m.kv_act[:, 0:2, :], m.kv_act[:, 2:4, :].rearrange("p a (b f) -> p (a b) f", f=D)

    with nc.Block() as block:
        @block.sync
        def _(sp):
            if do_pre:
                sp.dma_start(m.xin[:], a["x"][bass.ts(pre, GT)].rearrange("(b p) c -> p b c", p=P)).then_inc(S["x_in"], 16)
            if do_post:
                sp.dma_start(m.x1[:], a["x"][bass.ts(post, GT)].rearrange("(b p) c -> p b c", p=P)).then_inc(S["x_res"], 16)
                sp.dma_start(m.mask_all[:], a["mask"][0:1, bass.ts(post, GT)].broadcast_to([P, GT])).then_inc(S["mask_in"], 16)
                sp.dma_start(m.ctx_at[:], a["ctxT"][:, bass.ts(post, GT)].rearrange("(k p) t -> p k t", p=P)
                             ).then_inc(S["ctx_in"], 16)
            for dst, src in loads:
                sp.dma_start(dst, src).then_inc(S["loaded"], 16)
            for slot in range(last_slot):
                n = slot // KI + 4
                if do_scan and slot % KI == 0 and n < NS:
                    if KI * (n - 3) > U_AHEAD:
                        sp.wait_ge(S["u_ready"], KI * (n - 3) - U_AHEAD)
                    sp.dma_start(m.bb[:, n % 4, :], a["b_rows"][n:n + 1, parity * GT:(parity + 1) * GT].broadcast_to([P, GT])
                                 ).then_inc(S[f"bb{n % 4}"], 16)
                for name, k in steps_at(slot, *tables(SP_POST, SP_PRE)):
                    if name == "B":
                        wait_bank_read(sp, "xd")
                        sp.dma_start(a["b_rows"][:, other * GT:(other + 1) * GT], m.xdT[B_ROW:B_ROW + NS, :]
                                     ).then_inc(S["b_stored"], 16)
                    elif name == "bb":
                        sp.wait_ge(S["b_stored"], 16)
                        if do_scan:
                            sp.wait_ge(S["u_ready"], KI * (NS - 3 + k) - U_AHEAD)
                        sp.dma_start(m.bb[:, k, :], a["b_rows"][k:k + 1, other * GT:(other + 1) * GT].broadcast_to([P, GT])
                                     ).then_inc(S["bb_ahead"], 16)
                    elif name == "oh":
                        sp.wait_ge(S["onehot"], 1)
                        sp.dma_start(a["onehot"][bass.ts(post, P), :], m.small["oh"][:]).then_inc(S["stored"], 16)
                    elif name == "xs":
                        sp.wait_ge(S["xs_ready"], 1)
                        sp.dma_start(a["xs"][bass.ts(post, GT)].rearrange("(b p) c -> p b c", p=P), m.xn[:]
                                     ).then_inc(S["stored"], 16)
                    elif name == "base":
                        wait_bank_read(sp, "dn", 0)
                        wait_bank_read(sp, "dn", 1)
                        sp.dma_start(a["out"][bass.ts(post, GT)].rearrange("(b p) c -> p b c", p=P), m.x1[:]
                                     ).then_inc(S["stored"], 16)
            if do_post:
                sp.wait_ge(S["stored"], 16 * 3)
            if do_pre:
                sp.wait_ge(S["bb_ahead"], 16 * 4)
            if loads:
                sp.wait_ge(S["loaded"], 16 * len(loads))

        @block.tensor
        def _(pe):
            def mm(out, lhsT, rhs, first, last):
                return nc.tensor.matmul(out, lhsT, rhs, start=first, stop=last)

            def transposes(name, k, src):
                for b in range(GB):
                    ins = nc.tensor.transpose(bank(name, k)[:, b * P:(b + 1) * P], src(b), m.ident[:])
                ins.then_inc(S["bank_full"], 1)

            def step(name, k):
                wait_bank_free(pe, name, k)
                out = bank(name, k)
                if name == "z":
                    for kk in range(KD):
                        ins = mm(out[:], m.w_in[:, kk, DI + k * P:DI + (k + 1) * P], m.xn1T[other][:, kk, :],
                                 kk == 0, kk == KD - 1)
                    ins.then_inc(S["bank_full"], 1)
                elif name == "y":
                    transposes(name, k, lambda b: m.acc[:, b, k * P:(k + 1) * P])
                elif name == "k":
                    pe.wait_ge(S["ctx_masked"], 1)
                    pe.wait_ge(S["mask_in"], 16)
                    for kk in range(KC):
                        mm(out[:], m.w_src[:, kk, k * P:(k + 1) * P], m.ctx_at[:, kk, :], kk == 0, False)
                    mm(out[:], m.b_src[:, k * P:(k + 1) * P], m.mask_all[0:1, :], False, True).then_inc(S["bank_full"], 1)
                elif name == "v":
                    for i in range(2):
                        b = 2 * k + i
                        o = out[:, i * D:(i + 1) * D]
                        for kk in range(KC):
                            mm(o, m.ctx_at[:, kk, b * P:(b + 1) * P], m.w_src[:, kk, D:2 * D], kk == 0, False)
                        ins = mm(o, m.mask_all[0:1, b * P:(b + 1) * P], m.b_src[:, D:2 * D], False, True)
                    ins.then_inc(S["bank_full"], 1)
                elif name == "o":
                    pe.wait_ge(S["y_gated"], KI)
                    for i in range(2):
                        b = 2 * k + i
                        for kk in range(KI):
                            ins = mm(out[:, i * D:(i + 1) * D], m.xc2[other][:, kk, b * P:(b + 1) * P], m.w_out[:, kk, :],
                                     kk == 0, kk == KI - 1)
                    ins.then_inc(S["bank_full"], 1)
                elif name == "t2":
                    pe.wait_ge(S["ln2_ready"], GB)
                    transposes(name, k, lambda b: m.xn[:, b, k * P:(k + 1) * P])
                elif name == "q":
                    for kk in range(KD):
                        wait_bank_read(pe, "t2", kk)
                    for kk in range(KD):
                        ins = mm(out[:], m.w_tgt[:, kk, k * P:(k + 1) * P], m.xnT[:, kk, :], kk == 0, kk == KD - 1)
                    ins.then_inc(S["bank_full"], 1)
                elif name == "s":
                    c, j = k // HC, k % HC
                    wait_bank_read(pe, "q", c)
                    wait_bank_read(pe, "k", c)
                    rows = slice(HD * j, HD * (j + 1))
                    for b in range(GB):
                        ins = mm(out[:, b * P:(b + 1) * P], m.q_up[rows, c, b * P:(b + 1) * P],
                                 k_ap[rows, c, b * P:(b + 1) * P], True, True)
                    ins.then_inc(S["bank_full"], 1)
                elif name == "a":
                    pe.wait_ge(S["att_exp"], GB * (k + 1))
                    transposes(name, k, lambda b: m.sc[:, k % ATT_RING, b * P:(b + 1) * P])
                elif name == "av":
                    for j in range(HC):
                        wait_bank_read(pe, "a", HC * k + j)
                    wait_bank_read(pe, "v", 0)
                    wait_bank_read(pe, "v", 1)
                    for b in range(GB):
                        for j in range(HC):
                            f = b * P + j * HD
                            ins = mm(out[:, f:f + HD], m.ctx_at[:, j, b * P:(b + 1) * P],
                                     v_ap[:, b, k * P + j * HD:k * P + (j + 1) * HD], True, True)
                    ins.then_inc(S["bank_full"], 1)
                elif name == "ut":
                    wait_bank_read(pe, "av", k)
                    transposes(name, k, lambda b: m.upd[:, b, k * P:(k + 1) * P])
                elif name == "xo":
                    for kk in range(KD):
                        wait_bank_read(pe, "ut", kk)
                    for i in range(2):
                        b = 2 * k + i
                        o = out[:, i * D:(i + 1) * D]
                        for kk in range(KD):
                            mm(o, m.xnT[:, kk, b * P:(b + 1) * P], m.w_xo[:, kk, :], kk == 0, False)
                        for kk in range(KD):
                            mm(o, m.q_up[:, kk, b * P:(b + 1) * P], m.w_xo[:, KD + kk, :], False, False)
                        ins = mm(o, m.ones, m.b_xo, False, True)
                    ins.then_inc(S["bank_full"], 1)
                elif name == "t3":
                    pe.wait_ge(S["ln3_ready"], GB)
                    transposes(name, k, lambda b: m.xn[:, b, k * P:(k + 1) * P])
                elif name == "lg":
                    for kk in range(KD):
                        wait_bank_read(pe, "t3", kk)
                    for b in range(GB):
                        for kk in range(KD):
                            ins = mm(out[:, b * E:(b + 1) * E], m.xnT[:, kk, b * P:(b + 1) * P], m.gate_w[:, kk, :],
                                     kk == 0, kk == KD - 1)
                    ins.then_inc(S["bank_full"], 1)
                elif name in ("g", "u"):
                    w = m.sh_gate if name == "g" else m.sh_up
                    for kk in range(KD):
                        ins = mm(out[:], w[:, kk, k * P:(k + 1) * P], m.xnT[:, kk, :], kk == 0, kk == KD - 1)
                    ins.then_inc(S["bank_full"], 1)
                elif name == "dn":
                    for kk in range(KF):
                        wait_bank_read(pe, "u", kk)
                    for i in range(2):
                        b = 2 * k + i
                        for kk in range(KF):
                            ins = mm(out[:, i * D:(i + 1) * D], m.kv_act[:, kk, b * P:(b + 1) * P], m.sh_down[:, kk, :],
                                     kk == 0, kk == KF - 1)
                    ins.then_inc(S["bank_full"], 1)
                elif name == "t1":
                    pe.wait_ge(S["ln1_ready"], GB)
                    transposes(name, k, lambda b: m.xin[:, b, k * P:(k + 1) * P])
                elif name == "xb":
                    for kk in range(KD):
                        wait_bank_read(pe, "t1", kk)
                    for kk in range(KD):
                        ins = mm(out[:], m.w_in[:, kk, k * P:(k + 1) * P], m.xn1T[other][:, kk, :], kk == 0, kk == KD - 1)
                    ins.then_inc(S["bank_full"], 1)
                elif name == "xd":
                    pe.wait_ge(S["xc2_ready"], KI)
                    for kk in range(KI):
                        ins = mm(out[:], m.w_x[:, kk, :], m.xc2[other][:, kk, :], kk == 0, kk == KI - 1)
                    ins.then_inc(S["bank_full"], 1)
                elif name == "ct":
                    wait_bank_read(pe, "xd")
                    for b in range(GB):
                        ins = nc.tensor.transpose(out[:, b * NS:(b + 1) * NS], m.xdT[C_ROW:C_ROW + NS, b * P:(b + 1) * P],
                                                  m.ident[0:NS, 0:NS])
                    ins.then_inc(S["bank_full"], 1)
                elif name == "dt":
                    wait_bank_read(pe, "xd")
                    mm(out[:], m.w_dt[R_ROW:R_ROW + RANK, k * P:(k + 1) * P], m.xdT[R_ROW:R_ROW + RANK, :],
                       True, True).then_inc(S["bank_full"], 1)

            for slot in range(last_slot):
                if do_scan and HT_LAG <= slot < HT_LAG + SCAN_SLOTS:
                    i = slot - HT_LAG
                    n, b = i // KI, i % KI
                    pe.wait_ge(S["h_ready"], KI * (n + 1))
                    if i >= HT_BANKS:
                        pe.wait_ge(S["acc_done"], i - HT_BANKS + 1)
                    for c in range(KI):
                        ins = nc.tensor.transpose(m.hT[i % HT_BANKS][:, c * P:(c + 1) * P], m.h[:, n % H_RING, c, b * P:(b + 1) * P],
                                                  m.ident[:])
                    ins.then_inc(S["hT_ready"], 1)
                for name, k in steps_at(slot, *tables(PE_POST, PE_PRE)):
                    step(name, k)

        @block.scalar
        def _(act):
            def copy(out, in_):
                return nc.scalar.activation(out, in_, ACT.Copy)

            def decay(i, group_parity, ready):
                n, c = i // KI, i % KI
                nc.scalar.activation(m.dA[i % DECAY_BANKS].rearrange("p (b t) -> p b t", b=GB)[:, :, 1:P],
                                     m.dt[group_parity][:, c, :].rearrange("p (b t) -> p b t", b=GB)[:, :, 1:P],
                                     ACT.Exp, scale=m.a_neg[:, c, n:n + 1]).then_inc(S[ready], 1)

            def step(name, k):
                if name == "z":
                    wait_bank_full(act, "z", k)
                    if k >= 2:
                        act.wait_ge(S["y_gated"], k - 1)
                    nc.scalar.activation(m.th[:, k % 2, :], bank("z", k)[:], ACT.Tanh, scale=0.5).then_inc(S["z_tanh"], 1)
                elif name == "k":
                    wait_bank_full(act, "k", k)
                    copy(k_ap[:, k, :], bank("k", k)[:]).then_inc(bank_free("k", k), 1)
                elif name == "v":
                    wait_bank_full(act, "v", k)
                    copy(v_ap[:, 2 * k:2 * k + 2, :], bank("v", k)[:].rearrange("p (b f) -> p b f", f=D)
                         ).then_inc(bank_free("v", k), 1)
                elif name in ("t1", "t2", "t3", "ut", "a", "xd"):
                    wait_bank_full(act, name, k)
                    if name == "t1":
                        if do_post:
                            wait_bank_full(act, "z", KI - 1)
                        dst = m.xn1T[other][:, k, :]
                    elif name == "t2":
                        dst = m.xnT[:, k, :]
                    elif name == "t3":
                        wait_bank_full(act, "xo", 1)
                        dst = m.xnT[:, k, :]
                    elif name == "ut":
                        wait_bank_full(act, "s", HEADS - 1)
                        dst = m.q_up[:, k, :]
                    elif name == "a":
                        wait_bank_full(act, "v", 1)
                        wait_bank_full(act, "k", 1)
                        if k >= HC:
                            wait_bank_full(act, "av", 0)
                        dst = m.ctx_at[:, k % HC, :]
                    else:
                        dst = m.xdT[:]
                    copy(dst, bank(name, k)[:]).then_inc(bank_free(name, k), 1)
                elif name == "s":
                    act.wait_ge(S["neg_max"], k + 1)
                    for b in range(GB):
                        nc.scalar.activation(m.sc[:, k % ATT_RING, b * P:(b + 1) * P], m.sc[:, k % ATT_RING, b * P:(b + 1) * P], ACT.Exp,
                                             bias=m.small["nmax"][:, k * GB + b:k * GB + b + 1],
                                             accum_out=m.small["sum"][:, k * GB + b:k * GB + b + 1]).then_inc(S["att_exp"], 1)
                elif name in ("n1", "n2", "n3"):
                    which = int(name[1])
                    act.wait_ge(S[f"rs{which}"], 4)
                    src, dst = (m.xin, m.xin) if which == 1 else (m.x1, m.xn)
                    if which == 3:
                        wait_bank_full(act, "t2", 1)
                    for b in range(GB):
                        nc.scalar.activation(dst[:, b, :], src[:, b, :], ACT.Identity, bias=m.small[f"nb{which}"][:, b:b + 1],
                                             scale=m.small[f"rs{which}"][:, b:b + 1]).then_inc(S[f"ln{which}_ready"], 1)
                elif name == "lg":
                    act.wait_ge(S["top_logit"], 1)
                    nc.scalar.activation(m.small["top"][:], m.small["mx"][:], ACT.Tanh, scale=0.5).then_inc(S["top_tanh"], 1)
                elif name == "g":
                    wait_bank_full(act, "g", k)
                    if k >= ATT_RING:
                        wait_bank_read(act, "g", k - ATT_RING)
                    nc.scalar.activation(m.sc[:, k % ATT_RING, :], bank("g", k)[:], ACT.Tanh, scale=0.5).then_inc(S["g_tanh"], 1)
                elif name == "xb":
                    wait_bank_full(act, "xb", k)
                    if k >= 1:
                        act.wait_ge(S["xc2_ready"], k)
                    nc.scalar.activation(m.cv[:], bank("xb", k)[:], ACT.Identity, bias=m.conv_b[:, k:k + 1],
                                         scale=m.conv_w[:, k, 3:4]).then_inc(S["tap3"], 1)
                    copy(m.xb[:], bank("xb", k)[:]).then_inc(bank_free("xb", k), 1)
                elif name == "th":
                    act.wait_ge(S["conv_done"], 3 * (k + 1))
                    if do_post:
                        act.wait_ge(S["y_gated"], KI)
                    nc.scalar.activation(m.th[:, k % 2, :], m.cv[:], ACT.Tanh, scale=0.5).then_inc(S["cv_tanh"], 1)
                elif name == "dt":
                    wait_bank_full(act, "dt", k)
                    nc.scalar.activation(m.dt[other][:, k, :], bank("dt", k)[:], ACT.Tanh, bias=m.dt_bias[:, k:k + 1],
                                         scale=0.5).then_inc(bank_free("dt", k), 1)

            for slot in range(last_slot):
                i = slot + DECAY_BANKS - 1
                if do_scan and DECAY_BANKS <= i < SCAN_SLOTS:
                    act.wait_ge(S["h_ready"], slot)
                    decay(i, parity, "dA_ready")
                for name, k in steps_at(slot, *tables(ACT_POST, ACT_PRE)):
                    step(name, k)

            if do_pre:
                for i in range(DECAY_BANKS):
                    act.wait_ge(S["dt_ready"], i + 1)
                    if do_scan:
                        act.wait_ge(S["h_ready"], last_user(i, DECAY_BANKS) + 1)
                    decay(i, other, "dA_ahead")

        @block.vector
        def _(dve):
            stt = nc.vector.scalar_tensor_tensor
            ts = nc.vector.tensor_scalar

            def norm_stats(which, src):
                st, mv = m.small[f"st{which}"], m.small[f"mv{which}"]
                for b in range(GB):
                    nc.vector.bn_stats(st[:, 6 * b:6 * b + 6], src[:, b, :]).then_inc(S[f"bn{which}"], 1)
                for b in range(GB):
                    dve.wait_ge(S[f"bn{which}"], b + 1)
                    nc.vector.bn_aggr(mv[:, 2 * b:2 * b + 2], st[:, 6 * b:6 * b + 6]).then_inc(S[f"mv{which}_ready"], 1)

            def step(name, k):
                if name == "mb":
                    dve.wait_ge(S["mask_in"], 16)
                    ts(m.mask_neg[:], m.mask_all[:], 0.0, MASKED, ALU.is_equal, ALU.mult).then_inc(S["mask_neg"], 1)
                elif name == "z":
                    dve.wait_ge(S["z_tanh"], k + 1)
                    stt(m.th[:, k % 2, :], m.th[:, k % 2, :], 1.0, bank("z", k)[:], ALU.add, ALU.mult
                        ).then_inc(bank_free("z", k), 1)
                    wait_bank_full(dve, "y", k)
                    xc2 = m.xc2[other][:, k, :]
                    stt(xc2, xc2, m.d_half[:, k:k + 1], bank("y", k)[:], ALU.mult, ALU.add).then_inc(bank_free("y", k), 1)
                elif name in ("o", "xo", "dn"):
                    wait_bank_full(dve, name, k)
                    x = m.x1[:, 2 * k:2 * k + 2, :]
                    if name == "o":
                        dve.wait_ge(S["x_res"], 16)
                    else:
                        wait_bank_read(dve, "o" if name == "xo" else "xo", k)
                    nc.vector.tensor_tensor(x, x, bank(name, k)[:].rearrange("p (b f) -> p b f", f=D), ALU.add
                                            ).then_inc(bank_free(name, k), 1)
                elif name == "ln1":
                    dve.wait_ge(S["x_in"], 16)
                    norm_stats(1, m.xin)
                elif name == "ln2":
                    wait_bank_read(dve, "o", 0)
                    wait_bank_read(dve, "o", 1)
                    norm_stats(2, m.x1)
                elif name == "ln3":
                    wait_bank_read(dve, "xo", 0)
                    wait_bank_read(dve, "xo", 1)
                    norm_stats(3, m.x1)
                elif name == "q":
                    wait_bank_full(dve, "q", k)
                    dve.wait_ge(S["mask_in"], 16)
                    stt(m.q_up[:, k, :], bank("q", k)[:], m.b_tgt[:, k:k + 1], m.mask_all[:], ALU.add, ALU.mult
                        ).then_inc(bank_free("q", k), 1)
                elif name == "s":
                    wait_bank_full(dve, "s", k)
                    dve.wait_ge(S["mask_neg"], 1)
                    if k >= ATT_RING:
                        wait_bank_full(dve, "a", k - ATT_RING)
                    stt(m.sc[:, k % ATT_RING, :], bank("s", k)[:], ATT_SCALE, m.mask_neg[:], ALU.mult, ALU.add
                        ).then_inc(bank_free("s", k), 1)
                    wait_bank_read(dve, "s", k)
                    nc.vector.tensor_reduce(m.small["nmax"][:, GB * k:GB * (k + 1)],
                                            m.sc[:, k % ATT_RING, :].rearrange("p (b t) -> p b t", b=GB), AX.X, ALU.max,
                                            negate=True).then_inc(S["neg_max"], 1)
                elif name == "r":
                    dve.wait_ge(S["att_exp"], GB * HC * (k + 1))
                    w = HC * GB
                    nc.vector.reciprocal(m.small["rec"][:, w * k:w * (k + 1)], m.small["sum"][:, w * k:w * (k + 1)]
                                         ).then_inc(S["rec_ready"], 1)
                elif name == "av":
                    wait_bank_full(dve, "av", k)
                    dve.wait_ge(S["rec_ready"], k + 1)
                    w = HC * GB
                    rec = m.small["rec"][:, w * k:w * (k + 1)].rearrange("p (j b) -> p b j", b=GB)
                    nc.vector.tensor_tensor(m.upd[:, :, k * P:(k + 1) * P].rearrange("p b (j f) -> p b j f", f=HD),
                                            bank("av", k)[:].rearrange("p (b j f) -> p b j f", b=GB, f=HD),
                                            rec.unsqueeze(3).broadcast_to([P, GB, HC, HD]), ALU.mult
                                            ).then_inc(bank_free("av", k), 1)
                elif name == "lg":
                    wait_bank_full(dve, "lg")
                    lg = bank("lg")[:, 0:GB * E].rearrange("p (b e) -> p b e", e=E)
                    v3 = lambda t: m.small[t][:].rearrange("p (b e) -> p b e", e=E)
                    row = lambda t: m.small[t][:].unsqueeze(2).broadcast_to([P, GB, E])
                    first = m.first[:].unsqueeze(1).broadcast_to([P, GB, E])
                    nc.vector.tensor_reduce(m.small["mx"][:], lg, AX.X, ALU.max).then_inc(S["top_logit"], 1)
                    dve.wait_ge(S["top_logit"], 1)
                    nc.vector.tensor_tensor(v3("eq"), lg, row("mx"), ALU.is_equal).then_inc(bank_free("lg"), 1)
                    wait_bank_read(dve, "lg")
                    nc.vector.tensor_tensor(v3("eq"), v3("eq"), first, ALU.mult).then_inc(S["route"], 1)
                    dve.wait_ge(S["route"], 1)
                    nc.vector.tensor_reduce(m.small["m8"][:], v3("eq"), AX.X, ALU.max).then_inc(S["route"], 1)
                    dve.wait_ge(S["route"], 2)
                    nc.vector.tensor_tensor(v3("oh"), first, row("m8"), ALU.is_equal).then_inc(S["onehot"], 1)
                elif name == "g":
                    dve.wait_ge(S["g_tanh"], k + 1)
                    if k == 0:
                        wait_bank_full(dve, "av", 1)
                    x = m.kv_act[:, k, :]
                    stt(x, m.sc[:, k % ATT_RING, :], 1.0, bank("g", k)[:], ALU.add, ALU.mult).then_inc(bank_free("g", k), 1)
                    wait_bank_read(dve, "g", k)
                    wait_bank_full(dve, "u", k)
                    nc.vector.tensor_tensor(x, x, bank("u", k)[:], ALU.mult).then_inc(bank_free("u", k), 1)
                elif name == "cv":
                    wait_bank_read(dve, "xb", k)
                    dve.wait_ge(S["tap3"], k + 1)
                    cv = m.cv[:].rearrange("p (b t) -> p b t", b=GB)
                    xb = m.xb[:].rearrange("p (b t) -> p b t", b=GB)
                    for j in range(1, 4):
                        if j > 1:
                            dve.wait_ge(S["conv_done"], 3 * k + j - 1)
                        stt(cv[:, :, j:P], xb[:, :, 0:P - j], m.conv_w[:, k, 3 - j:4 - j], cv[:, :, j:P], ALU.mult, ALU.add
                            ).then_inc(S["conv_done"], 1)
                elif name == "xc":
                    dve.wait_ge(S["cv_tanh"], k + 1)
                    if do_post:
                        wait_bank_full(dve, "o", 1)
                    stt(m.xc2[other][:, k, :], m.th[:, k % 2, :], 1.0, m.cv[:], ALU.add, ALU.mult
                        ).then_inc(S["xc2_ready"], 1)
                elif name == "ct":
                    wait_bank_full(dve, "ct")
                    nc.vector.tensor_copy(m.c_tok[other][:].rearrange("p b n -> p (b n)"), bank("ct")[:, 0:GB * NS]
                                          ).then_inc(bank_free("ct"), 1)
                elif name == "dt":
                    wait_bank_read(dve, "dt", k)
                    d = m.dt[other][:, k, :]
                    half = 0.5 * (DT_MAX - DT_MIN)
                    ts(d, d, half, half + DT_MIN, ALU.mult, ALU.add).then_inc(S["dt_lin"], 1)
                    dve.wait_ge(S["dt_lin"], k + 1)
                    ts(d, d, 1e-4, None, ALU.max).then_inc(S["dt_ready"], 1)

            for slot in range(last_slot):
                if do_scan and slot < SCAN_SLOTS:
                    n, c = slot // KI, slot % KI
                    if slot >= DECAY_BANKS:
                        dve.wait_ge(S["dA_ready"], slot - DECAY_BANKS + 1)
                    if slot >= U_AHEAD:
                        dve.wait_ge(S["u_ready"], slot - U_AHEAD + 1)
                    if n >= H_RING:
                        dve.wait_ge(S["hT_ready"], KI * (n - H_RING + 1))
                    nc.vector.tensor_tensor_scan(m.h[:, n % H_RING, c, :], m.dA[slot % DECAY_BANKS][:], m.u[:, slot % U_RING, :], 0.0,
                                                 ALU.mult, ALU.add).then_inc(S["h_ready"], 1)
                if do_scan and slot >= ACC_LAG:
                    i = slot - ACC_LAG
                    n, b = i // KI, i % KI
                    dve.wait_ge(S["hT_ready"], i + 1)
                    cn = m.c_tok[parity][:, b, n:n + 1]
                    if n == 0:
                        if do_post:
                            wait_bank_full(dve, "y", KI - 1)
                        ts(m.acc[:, b, :], m.hT[i % HT_BANKS][:], cn, None, ALU.mult).then_inc(S["acc_done"], 1)
                    else:
                        dve.wait_ge(S["acc_done"], i - KI + 1)
                        stt(m.acc[:, b, :], m.hT[i % HT_BANKS][:], cn, m.acc[:, b, :], ALU.mult, ALU.add
                            ).then_inc(S["acc_done"], 1)
                for name, k in steps_at(slot, *tables(DVE_POST, DVE_PRE)):
                    step(name, k)

        @block.gpsimd
        def _(pool):
            tt, ts = nc.gpsimd.tensor_tensor, nc.gpsimd.tensor_scalar

            def drive(i, group_parity, ready):
                n, c = i // KI, i % KI
                tt(m.u[:, i % U_RING, :], m.dtx[group_parity][:, c, :], m.bb[:, n % 4, :], ALU.mult).then_inc(S[ready], 1)

            def norm_factors(which):
                mv, rs, nb = (m.small[f"{t}{which}"] for t in ("mv", "rs", "nb"))
                pool.wait_ge(S[f"mv{which}_ready"], GB)
                ts(rs[:], mv[:].rearrange("p (b v) -> p b v", v=2)[:, :, 1], EPS, None, ALU.add).then_inc(S[f"rs{which}"], 1)
                pool.wait_ge(S[f"rs{which}"], 1)
                tt(rs[:], rs[:], m.minus_half[:], ALU.pow).then_inc(S[f"rs{which}"], 1)
                pool.wait_ge(S[f"rs{which}"], 2)
                mean = mv[:].rearrange("p (b v) -> p b v", v=2)[:, :, 0]
                tt(nb[:], mean, rs[:], ALU.mult).then_inc(S[f"rs{which}"], 1)
                pool.wait_ge(S[f"rs{which}"], 3)
                ts(nb[:], nb[:], -1.0, None, ALU.mult).then_inc(S[f"rs{which}"], 1)

            def step(name, k):
                if name == "yz":
                    wait_bank_read(pool, "z", k)
                    wait_bank_read(pool, "y", k)
                    xc2 = m.xc2[other][:, k, :]
                    tt(xc2, xc2, m.th[:, k % 2, :], ALU.mult).then_inc(S["y_gated"], 1)
                elif name == "cm":
                    pool.wait_ge(S["ctx_in"], 16)
                    pool.wait_ge(S["mask_in"], 16)
                    tt(m.ctx_at[:], m.ctx_at[:], m.mask_all[:].unsqueeze(1).broadcast_to([P, KC, GT]), ALU.mult
                       ).then_inc(S["ctx_masked"], 1)
                elif name == "ln1":
                    norm_factors(1)
                elif name == "ln2":
                    norm_factors(2)
                elif name == "ln3":
                    norm_factors(3)
                elif name == "xs":
                    pool.wait_ge(S["top_tanh"], 1)
                    ts(m.small["score"][:], m.small["top"][:], 0.5, 0.5, ALU.mult, ALU.add).then_inc(S["score"], 1)
                    pool.wait_ge(S["score"], 1)
                    pool.wait_ge(S["ln3_ready"], GB)
                    wait_bank_full(pool, "t3", 1)
                    tt(m.xn[:], m.xn[:], m.small["score"][:].unsqueeze(2).broadcast_to([P, GB, D]), ALU.mult
                       ).then_inc(S["xs_ready"], 1)
                elif name == "dx":
                    pool.wait_ge(S["dt_ready"], k + 1)
                    tt(m.dtx[other][:, k, :], m.dt[other][:, k, :], m.xc2[other][:, k, :], ALU.mult).then_inc(S["dtx_ready"], 1)

            for slot in range(last_slot):
                i = slot + U_RING - 1
                if do_scan and U_AHEAD <= i < SCAN_SLOTS:
                    n = i // KI
                    if n >= 4:
                        pool.wait_ge(S[f"bb{n % 4}"], 16 * (n // 4))
                    if slot >= 1:
                        pool.wait_ge(S["h_ready"], slot)
                    drive(i, parity, "u_ready")
                for name, k in steps_at(slot, *tables(POOL_POST, POOL_PRE)):
                    step(name, k)

            if do_pre:
                pool.wait_ge(S["bb_ahead"], 16 * 4)
                for i in range(U_AHEAD):
                    pool.wait_ge(S["dtx_ready"], i % KI + 1)
                    if do_scan:
                        pool.wait_ge(S["h_ready"], last_user(i, U_RING) + 1)
                    drive(i, other, "u_ahead")

    with nc.Block() as block:
        @block.gpsimd
        def _(pool):
            for s in S.values():
                pool.sem_clear(s)


A_SEMS = ("acc_done", "att_exp", "b_stored", "bank_free0", "bank_free1", "bank_free2", "bank_free3", "bank_free4", "bank_free5", "bank_free6", "bank_free7", "bank_full",
          "bb0", "bb1", "bb2", "bb3", "bb_ahead", "bn1", "bn2", "bn3", "conv_done", "ctx_in", "ctx_masked",
          "cv_tanh", "dA_ahead", "dA_ready", "dt_lin", "dt_ready", "dtx_ready", "g_tanh", "hT_ready", "h_ready", "ln1_ready",
          "ln2_ready", "ln3_ready", "loaded", "mask_in", "mask_neg", "mv1_ready", "mv2_ready", "mv3_ready",
          "neg_max", "onehot", "rec_ready", "route", "rs1", "rs2", "rs3", "score", "stored", "tap3", "top_logit",
          "top_tanh", "u_ahead", "u_ready", "x_in", "x_res", "xc2_ready", "xs_ready", "y_gated", "z_tanh")


def expert_weights(shared):
    gu, d = E * KD * FF, E * KF * D
    return shared[:, 0:gu], shared[:, gu:2 * gu], shared[:, 2 * gu:2 * gu + d]


def phase_a(nc, a, shared):
    with ExitStack() as ctx:
        m = Memory()
        phase_a_memory(nc, ctx, m, shared)
        banks = [ctx.enter_context(nc.psum_tensor(f"bank{i}", [P, GT], F32)) for i in range(8)]
        split_banks(m, banks)
        ws = {n: ctx.enter_context(nc.semaphore("s_" + n)) for n in ("w", "w_clear", "w_loaded", "id", "iota", "a_exp", "zero")}
        S = {n: ctx.enter_context(nc.semaphore("s_" + n)) for n in A_SEMS}
        setup(nc, m, a, ws)
        iteration(nc, m, a, S, pre=0, parity=1, loads=late_loads(m, a))
        halve_late(nc, m)
        iteration(nc, m, a, S, scan=0, pre=1, parity=0)
        with nc.Fori(0, GROUPS // 2 - 1) as j:
            iteration(nc, m, a, S, scan=2 * j + 1, post=2 * j, pre=2 * j + 2, parity=1)
            iteration(nc, m, a, S, scan=2 * j + 2, post=2 * j + 1, pre=2 * j + 3, parity=0)
        iteration(nc, m, a, S, scan=GROUPS - 1, post=GROUPS - 2, parity=1)
        rt = lambda t, k: (t.rearrange("p (k n) -> p k n", k=E * k))
        iteration(nc, m, a, S, post=GROUPS - 1, parity=0, loads=[
            (rt(w, k), a[name].rearrange("e (k p) n -> p (e k) n", p=P))
            for w, name, k in zip(expert_weights(shared), ("rt_gate", "rt_up", "rt_down"), (KD, KD, KF))])


def route_and_run_experts(nc, a, shared):
    with ExitStack() as ctx:
        def sb(name, shape, dtype=F32):
            return ctx.enter_context(nc.sbuf_tensor(name, shape, dtype))

        def sem(name):
            return ctx.enter_context(nc.semaphore(name))

        w_gate, w_up, w_down = expert_weights(shared)
        oh = sb("oh_all", [P, SEQS, E])
        before = sb("before", [P, P])
        ones = sb("e_ones", [P, P])
        ident = sb("e_ident", [P, P])
        incl = sb("incl", [P, SEQS, E])
        rank = sb("rank", [P, SEQS, E])
        row_i = sb("row_i", [P, P], I32)
        row = sb("row", [P, P])
        steps = sb("steps", [P, SEQS])
        token_i = sb("token_i", [P, SEQS + 1], I32)
        token = sb("token", [P, SEQS + 1])
        more = sb("more", [P, E, SEQS])
        past = sb("past", [P, TILES, E])
        need = sb("need", [P, E])
        ends = sb("ends", [P, E])
        starts = sb("starts", [P, E])
        pos_f = sb("pos_f", [P, SEQS])
        pos_i = sb("pos_i", [P, SEQS], I32)
        part_i = sb("part_i", [P, 2, SEQS], I32)
        part = sb("part", [P, 2, SEQS])
        at_lane = sb("at_lane", [P, SEQS, P])
        at_tile = sb("at_tile", [P, SEQS, 2, TILES])
        slot_f = sb("slot_f", [P, TILES])
        free = sb("free", [P, TILES])
        slot = sb("slot", [P, TILES], U32)
        slot_now = sb("slot_now", [P, TPB], U32)
        owner_f = sb("owner_f", [P, TILES])
        owner = sb("owner", [P, TILES], I32)
        x = sb("e_x", [P, X_RING, D])
        xT = sb("e_xT", [P, 2, KD, P])
        act_t = sb("e_act", [P, 2, FF])
        th = sb("e_th", [P, 2, FF])
        actT = sb("e_actT", [P, 2, KF, P])
        y = sb("e_y", [P, Y_RING, D])
        psum = [ctx.enter_context(nc.psum_tensor(f"e_bank{i}", [P, FF], F32)) for i in range(8)]
        s_oh, s_const, s_iota, s_ones, s_counts, s_seq, s_spread, s_slots = (
            sem("t_" + n) for n in ("onehot", "const", "iota", "ones", "counts", "chain", "spread", "slots"))

        with nc.Block() as block:
            @block.sync
            def _(sp):
                sp.dma_start(oh[:].rearrange("p (g b) e -> p g (b e)", g=GROUPS),
                             a["onehot"].rearrange("(g p) c -> p g c", p=P)).then_inc(s_oh, 16)

            @block.gpsimd
            def _(pool):
                gp = nc.gpsimd
                gp.memset(ident[:], 0.0).then_inc(s_iota, 1)
                gp.memset(before[:], 1.0).then_inc(s_iota, 1)
                gp.iota(row_i[:], [[1, P]], base=0, channel_multiplier=0).then_inc(s_iota, 1)
                gp.iota(token_i[:], [[P, SEQS + 1]], base=0, channel_multiplier=1).then_inc(s_iota, 1)
                pool.wait_ge(s_iota, 4)
                gp.affine_select(out=ident[:], in_=ident[:], compare_op=ALU.not_equal, fill=1.0, base=0,
                                 pattern=[[-1, P]], channel_multiplier=1).then_inc(s_const, 1)
                gp.affine_select(out=before[:], in_=before[:], compare_op=ALU.is_gt, fill=0.0, base=0,
                                 pattern=[[1, P]], channel_multiplier=-1).then_inc(s_const, 1)

            @block.tensor
            def _(pe):
                pe.wait_ge(s_oh, 16)
                pe.wait_ge(s_const, 2)
                pe.wait_ge(s_ones, 1)
                flat = oh[:].rearrange("p s e -> p (s e)")
                nc.tensor.matmul(psum[0][:, 0:SEQS * E], before[:], flat, start=True, stop=True)
                nc.tensor.matmul(psum[1][:, 0:SEQS * E], ones[:], flat, start=True, stop=True).then_inc(s_counts, 1)
                pe.wait_ge(s_spread, 3)
                for t in range(SEQS):
                    ins = nc.tensor.matmul(psum[2][:, 0:2 * TILES], at_lane[:, t, :],
                                           at_tile[:, t, :, :].rearrange("p a j -> p (a j)"),
                                           start=(t == 0), stop=(t == SEQS - 1))
                ins.then_inc(s_slots, 1)

            @block.vector
            def _(dve):
                chain = [0]

                def link(ins):
                    chain[0] += 1
                    ins.then_inc(s_seq, 1)
                    dve.wait_ge(s_seq, chain[0])

                v = nc.vector
                v.memset(ones[:], 1.0).then_inc(s_ones, 1)
                dve.wait_ge(s_iota, 4)
                link(v.tensor_copy(row[:], row_i[:]))
                link(v.tensor_copy(token[:], token_i[:]))
                link(v.tensor_scalar(steps[:], row[:, 0:SEQS], float(P), None, ALU.mult))
                dve.wait_ge(s_ones, 1)
                dve.wait_ge(s_counts, 1)
                in_tile = psum[0][:, 0:SEQS * E].rearrange("p (s e) -> p s e", e=E)
                counts = psum[1][:, 0:SEQS * E].rearrange("p (s e) -> p s e", e=E)
                for e in range(E):
                    ins = v.tensor_tensor_scan(incl[:, :, e], ones[:, 0:SEQS], counts[:, :, e], 0.0, ALU.mult, ALU.add)
                link(ins)
                total = incl[:, SEQS - 1, :]
                link(v.tensor_tensor(more[:], total.unsqueeze(2).broadcast_to([P, E, SEQS]),
                                     steps[:].unsqueeze(1).broadcast_to([P, E, SEQS]), ALU.is_gt))
                link(v.tensor_reduce(need[:], more[:], AX.X, ALU.add))
                link(v.tensor_tensor_scan(ends[:], ones[:, 0:E], need[:], 0.0, ALU.mult, ALU.add))
                link(v.tensor_tensor(starts[:], ends[:], need[:], ALU.subtract))
                link(v.tensor_scalar(starts[:], starts[:], float(P), None, ALU.mult))
                link(v.tensor_tensor(rank[:], incl[:], counts, ALU.subtract))
                link(v.tensor_tensor(rank[:], rank[:], in_tile, ALU.add))
                link(v.tensor_tensor(rank[:], rank[:], starts[:].unsqueeze(1).broadcast_to([P, SEQS, E]), ALU.add))
                dve.wait_ge(s_oh, 16)
                link(v.tensor_tensor(rank[:], rank[:], oh[:], ALU.mult))
                link(v.tensor_reduce(pos_f[:], rank[:], AX.X, ALU.add))
                link(v.tensor_copy(pos_i[:], pos_f[:]))
                link(v.tensor_single_scalar(part_i[:, 0, :], pos_i[:], P - 1, ALU.bitwise_and))
                link(v.tensor_single_scalar(part_i[:, 1, :], pos_i[:], P.bit_length() - 1, ALU.logical_shift_right))
                link(v.tensor_copy(part[:], part_i[:]))
                v.tensor_tensor(at_lane[:], part[:, 0, :].unsqueeze(2).broadcast_to([P, SEQS, P]),
                                row[:].unsqueeze(1).broadcast_to([P, SEQS, P]), ALU.is_equal).then_inc(s_spread, 1)
                v.tensor_tensor(at_tile[:, :, 1, :], part[:, 1, :].unsqueeze(2).broadcast_to([P, SEQS, TILES]),
                                row[:, 0:TILES].unsqueeze(1).broadcast_to([P, SEQS, TILES]), ALU.is_equal
                                ).then_inc(s_spread, 1)
                dve.wait_ge(s_spread, 2)
                v.tensor_tensor(at_tile[:, :, 0, :], at_tile[:, :, 1, :],
                                token[:, 0:SEQS].unsqueeze(2).broadcast_to([P, SEQS, TILES]), ALU.mult
                                ).then_inc(s_spread, 1)
                link(v.tensor_tensor(past[:], ends[:].unsqueeze(1).broadcast_to([P, TILES, E]),
                                     row[:, 0:TILES].unsqueeze(2).broadcast_to([P, TILES, E]), ALU.is_le))
                link(v.tensor_reduce(owner_f[:], past[:], AX.X, ALU.add))
                link(v.tensor_scalar(owner_f[:], owner_f[:], float(E - 1), None, ALU.min))
                v.tensor_copy(owner[:], owner_f[:])
                dve.wait_ge(s_slots, 1)
                link(v.tensor_scalar(free[:], psum[2][:, TILES:2 * TILES], -1.0, 1.0, ALU.mult, ALU.add))
                link(v.scalar_tensor_tensor(slot_f[:], free[:], token[:, SEQS:SEQS + 1], psum[2][:, 0:TILES],
                                            ALU.mult, ALU.add))
                v.tensor_copy(slot[:], slot_f[:])

        S = {n: sem("c_" + n) for n in [f"x{i}" for i in range(X_RING)] + [f"added{i}" for i in range(Y_RING)] + [
            "slot_now", "xT_full", "xT_read", "g_full", "u_full", "tanh", "g_read", "u_read", "aT_full", "aT_read", "y_full", "y_read"]}
        xT_bank, y_bank = psum[0], psum[1]
        g_bank, u_bank, aT_bank = psum[2:4], psum[4:6], psum[6:8]
        with nc.Fori(0, TILES // TPB) as it:
            with nc.Block() as block:
                @block.gpsimd
                def _(pool):
                    def column(j):
                        return slot_now[:, j:j + 1]

                    def gather(j):
                        nc.gpsimd.indirect_dma_start(x[:, j % X_RING, :], None, a["xs"],
                                                     bass.IndirectOffsetOnAxis(ap=column(j), axis=0)
                                                     ).then_inc(S[f"x{j % X_RING}"], 16)

                    nc.gpsimd.tensor_copy(slot_now[:], slot[:, bass.ds(it * TPB, TPB)]).then_inc(S["slot_now"], 1)
                    pool.wait_ge(S["slot_now"], 1)
                    for j in range(X_RING):
                        gather(j)
                    for j in range(TPB):
                        if j + X_RING < TPB:
                            pool.wait_ge(S["xT_full"], j + 1)
                            gather(j + X_RING)
                        pool.wait_ge(S["y_read"], j + 1)
                        if j >= 1:
                            pool.wait_ge(S[f"added{(j - 1) % Y_RING}"], 16 * ((j - 1) // Y_RING + 1))
                        nc.gpsimd.indirect_dma_start(a["out"], bass.IndirectOffsetOnAxis(ap=column(j), axis=0),
                                                     y[:, j % Y_RING, :], None, compute_op=ALU.add
                                                     ).then_inc(S[f"added{j % Y_RING}"], 16)
                    for i in range(Y_RING):
                        pool.wait_ge(S[f"added{i}"], 16 * ((TPB - 1 - i) // Y_RING + 1))

                @block.tensor
                def _(pe):
                    def transpose_x(j):
                        pe.wait_ge(S[f"x{j % X_RING}"], 16 * (j // X_RING + 1))
                        if j >= 1:
                            pe.wait_ge(S["xT_read"], j)
                        for k in range(KD):
                            ins = nc.tensor.transpose(xT_bank[:, k * P:(k + 1) * P], x[:, j % X_RING, k * P:(k + 1) * P], ident[:])
                        ins.then_inc(S["xT_full"], 1)

                    def transpose_act(j):
                        pe.wait_ge(S["u_read"], j + 1)
                        if j >= 2:
                            pe.wait_ge(S["aT_read"], j - 1)
                        for k in range(KF):
                            ins = nc.tensor.transpose(aT_bank[j % 2][:, k * P:(k + 1) * P], act_t[:, j % 2, k * P:(k + 1) * P],
                                                      ident[:])
                        ins.then_inc(S["aT_full"], 1)

                    def gate(j, e):
                        pe.wait_ge(S["xT_read"], j + 1)
                        if j >= 2:
                            pe.wait_ge(S["u_read"], j - 1)
                        for k in range(KD):
                            ins = nc.tensor.matmul(g_bank[j % 2][:], xT[:, j % 2, k, :],
                                                   w_gate[:, bass.ds(e * (KD * FF) + k * FF, FF)],
                                                   start=(k == 0), stop=(k == KD - 1))
                        ins.then_inc(S["g_full"], 1)

                    def up(j, e):
                        for k in range(KD):
                            ins = nc.tensor.matmul(u_bank[j % 2][:], xT[:, j % 2, k, :],
                                                   w_up[:, bass.ds(e * (KD * FF) + k * FF, FF)],
                                                   start=(k == 0), stop=(k == KD - 1))
                        ins.then_inc(S["u_full"], 1)

                    def down(j, e):
                        pe.wait_ge(S["aT_read"], j + 1)
                        if j >= 1:
                            pe.wait_ge(S["y_read"], j)
                        for k in range(KF):
                            ins = nc.tensor.matmul(y_bank[:, 0:D], actT[:, j % 2, k, :],
                                                   w_down[:, bass.ds(e * (KF * D) + k * D, D)],
                                                   start=(k == 0), stop=(k == KF - 1))
                        ins.then_inc(S["y_full"], 1)

                    transpose_x(0)
                    e_before = e_now = None
                    for j in range(TPB + 1):
                        if j + 1 < TPB:
                            transpose_x(j + 1)
                        if j < TPB:
                            e_now = nc.tensor.value_load(owner[0:1, bass.ds(it * TPB + j, 1)], min_val=0, max_val=E - 1)
                            gate(j, e_now)
                        if j >= 1:
                            transpose_act(j - 1)
                        if j < TPB:
                            up(j, e_now)
                        if j >= 1:
                            down(j - 1, e_before)
                        e_before = e_now

                @block.scalar
                def _(act):
                    def copy_xT(j):
                        act.wait_ge(S["xT_full"], j + 1)
                        if j >= 2:
                            act.wait_ge(S["u_full"], j - 1)
                        nc.scalar.activation(xT[:, j % 2].rearrange("p k t -> p (k t)"), xT_bank[:, 0:D], ACT.Copy
                                             ).then_inc(S["xT_read"], 1)

                    copy_xT(0)
                    for j in range(TPB + 1):
                        if j + 1 < TPB:
                            copy_xT(j + 1)
                        if j < TPB:
                            act.wait_ge(S["g_full"], j + 1)
                            if j >= 2:
                                act.wait_ge(S["g_read"], j - 1)
                            nc.scalar.activation(th[:, j % 2, :], g_bank[j % 2][:], ACT.Tanh, scale=0.5
                                                 ).then_inc(S["tanh"], 1)
                        if j >= 1:
                            act.wait_ge(S["aT_full"], j)
                            if j >= 3:
                                act.wait_ge(S["y_full"], j - 2)
                            nc.scalar.activation(actT[:, (j - 1) % 2].rearrange("p k t -> p (k t)"), aT_bank[(j - 1) % 2][:],
                                                 ACT.Copy).then_inc(S["aT_read"], 1)

                @block.vector
                def _(dve):
                    for j in range(TPB + 1):
                        if j < TPB:
                            dve.wait_ge(S["tanh"], j + 1)
                            if j >= 2:
                                dve.wait_ge(S["aT_full"], j - 1)
                            t = act_t[:, j % 2, :]
                            nc.vector.scalar_tensor_tensor(t, th[:, j % 2, :], 1.0, g_bank[j % 2][:], ALU.add, ALU.mult
                                                           ).then_inc(S["g_read"], 1)
                            dve.wait_ge(S["g_read"], j + 1)
                            dve.wait_ge(S["u_full"], j + 1)
                            nc.vector.tensor_tensor(t, t, u_bank[j % 2][:], ALU.mult).then_inc(S["u_read"], 1)
                        if j >= 1:
                            dve.wait_ge(S["y_full"], j)
                            i = j - 1
                            if i >= Y_RING:
                                dve.wait_ge(S[f"added{i % Y_RING}"], 16 * (i // Y_RING))
                            nc.vector.tensor_scalar(y[:, i % Y_RING, :], y_bank[:, 0:D], 0.5, None, ALU.mult
                                                    ).then_inc(S["y_read"], 1)

            with nc.Block() as block:
                @block.gpsimd
                def _(pool):
                    pool.dma_reset()
                    for s in S.values():
                        pool.sem_clear(s)


X_RING = Y_RING = 3
TPB = 13
assert TILES % TPB == 0

IN_SHAPES = {"x": (TOKENS, D), "ctxT": (CS, TOKENS), "mask": (1, TOKENS), "w_in": (D, 2 * DI), "conv_w": (DI, 4),
             "conv_b": (P, KI), "w_x": (DI, RANK + 2 * NS), "w_dt": (RANK, DI), "b_dt": (P, KI), "a_log": (DI, NS),
             "d_param": (P, KI), "w_out": (DI, D), "w_srcT": (CS, 2 * D), "b_src": (1, 2 * D), "w_tgtT": (D, D),
             "b_tgt": (P, KD), "w_xoT": (2 * D, D), "b_xo": (1, D), "gate_w": (D, E), "sh_gate": (D, FF),
             "sh_up": (D, FF), "sh_down": (FF, D), "rt_gate": (E, D, FF), "rt_up": (E, D, FF), "rt_down": (E, FF, D)}


def decoder_layer(nc, a):
    a["b_rows"] = nc.dram_tensor("b_rows", (NS, 2 * GT), F32).ap()
    a["onehot"] = nc.dram_tensor("onehot", (GROUPS * P, GB * E), F32).ap()
    a["xs"] = nc.dram_tensor("xs", (TOKENS + P, D), F32).ap()
    with nc.sbuf_tensor("shared", [P, EXPERT_WORDS], F32) as shared:
        phase_a(nc, a, shared)
        route_and_run_experts(nc, a, shared)


def kernel(**inputs):
    import numpy as np
    import concourse.bacc as bacc
    from concourse.bass_utils import run_bass_kernel_spmd

    g = {n: np.asarray(v) for n, v in inputs.items()}
    columns = lambda v: v.reshape(-1, P).T
    host = {"x": g["x"].reshape(TOKENS, D), "ctxT": g["ctx_2048"].reshape(TOKENS, CS).T,
            "mask": g["mask_BxS2_fk1"].reshape(1, TOKENS), "w_in": g["L0_attn_W_in"],
            "conv_w": g["L0_attn_conv_w"].reshape(DI, 4), "conv_b": columns(g["L0_attn_conv_b"]),
            "w_x": g["L0_attn_W_x"], "w_dt": g["L0_attn_W_dt"], "b_dt": columns(g["L0_attn_b_dt"]),
            "a_log": g["L0_attn_A_log"], "d_param": columns(g["L0_attn_D_param"]), "w_out": g["L0_attn_W_out"],
            "w_srcT": g["L0_xattn_W_src"].T, "b_src": g["L0_xattn_b_src"].reshape(1, -1), "w_tgtT": g["L0_xattn_W_tgt"].T,
            "b_tgt": columns(g["L0_xattn_b_tgt"]), "w_xoT": g["L0_xattn_W_out"].T,
            "b_xo": g["L0_xattn_b_out"].reshape(1, -1), "gate_w": g["L0_ffn_gate_w"], "sh_gate": g["L0_ffn_sh_gate"],
            "sh_up": g["L0_ffn_sh_up"], "sh_down": g["L0_ffn_sh_down"], "rt_gate": g["L0_ffn_rt_gate"],
            "rt_up": g["L0_ffn_rt_up"], "rt_down": g["L0_ffn_rt_down"]}
    nc = bacc.Bacc("TRN2", target_bir_lowering=False, num_devices=1)
    arrays, a = {}, {}
    for name, shape in IN_SHAPES.items():
        arrays["in_" + name] = np.ascontiguousarray(host[name])
        a[name] = nc.dram_tensor("in_" + name, shape, F32, kind="ExternalInput").ap()
    a["out"] = nc.dram_tensor("out", (TOKENS + P, D), F32, kind="ExternalOutput").ap()
    decoder_layer(nc, a)
    r = run_bass_kernel_spmd(nc, [arrays], core_ids=[0])
    return r.results[0]["out"][0:TOKENS].reshape(SEQS, P, D)
```

```python
from contextlib import ExitStack

import concourse.bass as bass
from concourse import mybir

F32 = mybir.dt.float32
I32 = mybir.dt.int32
U32 = mybir.dt.uint32
ALU = mybir.AluOpType
ACT = mybir.ActivationFunctionType
AX = mybir.AxisListType

P = 128
SEQS = 32
GB = 4
GT = GB * P
GROUPS = SEQS // GB
TOKENS = SEQS * P
D = 256
KD = D // P
DI = 512
KI = DI // P
NS = 16
RANK = 64
CS = 512
KC = CS // P
HEADS = 8
HD = D // HEADS
HC = P // HD
E = 8
FF = 512
KF = FF // P
TILES = TOKENS // P + E - 1
DT_MIN, DT_MAX = 0.001, 0.1
EPS = 1e-5
MASKED = -1e30
ATT_SCALE = 1.0 / float(HD) ** 0.5
C_ROW, B_ROW, R_ROW = 0, 32, 64

SCAN_SLOTS = NS * KI
HT_BANKS, OTHER_BANKS = 3, 5
DECAY_RING = 3
U_RING = 4
H_RING = 3
HT_LAG = 6
U_AHEAD = 4
B_RING = 4
ATT_RING = 2
ACC_LAG = 8
SLOTS = SCAN_SLOTS + ACC_LAG

PE_POST = {("z", 0): 2, ("y", 0): 0, ("z", 1): 2, ("y", 1): 2, ("z", 2): 4, ("y", 2): 2, ("z", 3): 5,
           ("y", 3): 3, ("k", 0): 5, ("k", 1): 6, ("o", 0): 8, ("o", 1): 10, ("v", 0): 12, ("v", 1): 12,
           ("t2", 0): 16, ("t2", 1): 17, ("q", 0): 18, ("q", 1): 20, ("s", 0): 20, ("s", 1): 20,
           ("s", 2): 25, ("s", 3): 26, ("s", 4): 29, ("s", 5): 30, ("s", 6): 34, ("s", 7): 36,
           ("a", 0): 23, ("a", 1): 25, ("a", 2): 27, ("a", 3): 30, ("a", 4): 32, ("a", 5): 34,
           ("a", 6): 36, ("a", 7): 40, ("av", 0): 32, ("av", 1): 41, ("ut", 0): 40, ("ut", 1): 43,
           ("xo", 0): 46, ("xo", 1): 46, ("t3", 0): 51, ("t3", 1): 51, ("lg", 0): 53, ("g", 0): 54,
           ("g", 1): 55, ("g", 2): 57, ("g", 3): 59, ("u", 0): 54, ("u", 1): 56, ("u", 2): 59,
           ("u", 3): 59, ("dn", 0): 61, ("dn", 1): 61}
PE_PRE = {("t1", 0): 9, ("t1", 1): 12, ("xb", 0): 16, ("xb", 1): 17, ("xb", 2): 23, ("xb", 3): 30,
          ("xd", 0): 37, ("ct", 0): 41, ("dt", 0): 47, ("dt", 1): 47, ("dt", 2): 50, ("dt", 3): 50}
ACT_POST = {("z", 0): 2, ("z", 1): 4, ("z", 2): 4, ("z", 3): 5, ("k", 0): 5, ("k", 1): 8, ("v", 0): 11,
            ("v", 1): 15, ("n2", 0): 11, ("t2", 0): 16, ("t2", 1): 18, ("s", 0): 21, ("s", 1): 24,
            ("s", 2): 27, ("s", 3): 28, ("s", 4): 30, ("s", 5): 32, ("s", 6): 36, ("s", 7): 38,
            ("a", 0): 24, ("a", 1): 25, ("a", 2): 27, ("a", 3): 31, ("a", 4): 33, ("a", 5): 35,
            ("a", 6): 36, ("a", 7): 40, ("ut", 0): 42, ("ut", 1): 44, ("n3", 0): 50, ("t3", 0): 52,
            ("t3", 1): 52, ("lg", 0): 54, ("g", 0): 55, ("g", 1): 58, ("g", 2): 58, ("g", 3): 63}
ACT_PRE = {("n1", 0): 8, ("t1", 0): 8, ("t1", 1): 14, ("xb", 0): 17, ("xb", 1): 20, ("xb", 2): 24,
           ("xb", 3): 31, ("th", 0): 19, ("th", 1): 23, ("th", 2): 29, ("th", 3): 33, ("xd", 0): 40,
           ("dt", 0): 48, ("dt", 1): 48, ("dt", 2): 50, ("dt", 3): 52}
DVE_POST = {("z", 0): 3, ("z", 1): 4, ("z", 2): 4, ("z", 3): 6, ("o", 0): 9, ("o", 1): 13,
            ("ln2", 0): 13, ("q", 0): 19, ("q", 1): 21, ("s", 0): 21, ("s", 1): 22, ("s", 2): 27,
            ("s", 3): 28, ("s", 4): 30, ("s", 5): 32, ("s", 6): 35, ("s", 7): 37, ("r", 0): 29,
            ("r", 1): 42, ("av", 0): 34, ("av", 1): 43, ("xo", 0): 48, ("xo", 1): 48, ("ln3", 0): 48,
            ("lg", 0): 54, ("g", 0): 55, ("g", 1): 59, ("g", 2): 60, ("g", 3): 60, ("dn", 0): 62,
            ("dn", 1): 63}
DVE_PRE = {("ln1", 0): 5, ("cv", 0): 18, ("cv", 1): 22, ("cv", 2): 28, ("cv", 3): 33, ("xc", 0): 21,
           ("xc", 1): 23, ("xc", 2): 32, ("xc", 3): 35, ("ct", 0): 44, ("dt", 0): 49, ("dt", 1): 50,
           ("dt", 2): 52, ("dt", 3): 53}
POOL_POST = {("yz", 0): 2, ("yz", 1): 2, ("yz", 2): 4, ("yz", 3): 6, ("ln2", 0): 11, ("ln3", 0): 49,
             ("xs", 0): 58}
POOL_PRE = {("ln1", 0): 6, ("dx", 0): 50, ("dx", 1): 53, ("dx", 2): 55, ("dx", 3): 62}
SP_POST = {("oh", 0): 58, ("xs", 0): 49, ("base", 0): 65}
SP_AHEAD = {("src", 0): 41}
POOL_AHEAD = {("cm", 0): 46}
DVE_AHEAD = {("mb", 0): 59}
SP_PRE = {("B", 0): 40, ("bb", 0): 50, ("bb", 1): 53, ("bb", 2): 54, ("bb", 3): 59}

PE_LAST = {("z", 0): 1, ("y", 0): 0, ("z", 1): 2, ("y", 1): 2, ("z", 2): 3, ("y", 2): 2, ("z", 3): 5,
           ("y", 3): 3, ("k", 0): 4, ("k", 1): 6, ("o", 0): 10, ("o", 1): 10, ("v", 0): 12, ("v", 1): 12,
           ("t2", 0): 16, ("t2", 1): 17, ("q", 0): 18, ("q", 1): 19, ("s", 0): 20, ("s", 1): 22,
           ("s", 2): 22, ("s", 3): 24, ("s", 4): 26, ("s", 5): 28, ("s", 6): 31, ("s", 7): 37,
           ("a", 0): 23, ("a", 1): 25, ("a", 2): 26, ("a", 3): 29, ("a", 4): 34, ("a", 5): 36,
           ("a", 6): 37, ("a", 7): 38, ("av", 0): 34, ("av", 1): 43, ("ut", 0): 39, ("ut", 1): 43,
           ("xo", 0): 45, ("xo", 1): 48, ("t3", 0): 53, ("t3", 1): 53, ("lg", 0): 58, ("g", 0): 55,
           ("g", 1): 56, ("g", 2): 60, ("g", 3): 60, ("u", 0): 55, ("u", 1): 59, ("u", 2): 60,
           ("u", 3): 60, ("dn", 0): 62, ("dn", 1): 62}
ACT_LAST = {("z", 0): 0, ("z", 1): 1, ("z", 2): 3, ("z", 3): 5, ("k", 0): 3, ("k", 1): 8, ("v", 0): 11,
            ("v", 1): 20, ("n2", 0): 11, ("t2", 0): 15, ("t2", 1): 16, ("s", 0): 21, ("s", 1): 24,
            ("s", 2): 24, ("s", 3): 25, ("s", 4): 27, ("s", 5): 34, ("s", 6): 36, ("s", 7): 39,
            ("a", 0): 24, ("a", 1): 25, ("a", 2): 26, ("a", 3): 32, ("a", 4): 37, ("a", 5): 38,
            ("a", 6): 38, ("a", 7): 39, ("ut", 0): 42, ("ut", 1): 44, ("n3", 0): 51, ("t3", 0): 54,
            ("t3", 1): 54, ("lg", 0): 58, ("g", 0): 56, ("g", 1): 61, ("g", 2): 61, ("g", 3): 64}
DVE_LAST = {("z", 0): 2, ("z", 1): 3, ("z", 2): 3, ("z", 3): 8, ("o", 0): 9, ("o", 1): 12,
            ("ln2", 0): 13, ("q", 0): 19, ("q", 1): 20, ("s", 0): 21, ("s", 1): 23, ("s", 2): 23,
            ("s", 3): 25, ("s", 4): 27, ("s", 5): 34, ("s", 6): 35, ("s", 7): 38, ("r", 0): 28,
            ("r", 1): 42, ("av", 0): 36, ("av", 1): 45, ("xo", 0): 47, ("xo", 1): 49, ("ln3", 0): 49,
            ("lg", 0): 60, ("g", 0): 56, ("g", 1): 60, ("g", 2): 61, ("g", 3): 61, ("dn", 0): 63,
            ("dn", 1): 64}
POOL_LAST = {("yz", 0): 2, ("yz", 1): 3, ("yz", 2): 6, ("yz", 3): 7, ("ln2", 0): 14, ("ln3", 0): 49,
             ("xs", 0): 59}
SP_LAST = {("oh", 0): 62, ("xs", 0): 55, ("base", 0): 70}


def last_user(place, ring):
    return max(i for i in range(SCAN_SLOTS) if i % ring == place)


def steps_at(slot, *tables):
    return [step for table in tables for step, at in table.items() if at == slot]


class Memory:
    pass


EXPERT_WORDS = E * (2 * KD * FF + KF * D)


def phase_a_memory(nc, ctx, m, shared):
    at = [0]

    def carve(*shape):
        words = 1
        for n in shape:
            words *= n
        piece = shared[:, at[0]:at[0] + words]
        at[0] += words
        assert at[0] <= EXPERT_WORDS
        if len(shape) == 1:
            return piece
        names = "abc"[:len(shape)]
        return piece.rearrange(f"p ({' '.join(names)}) -> p {' '.join(names)}", **dict(zip(names[1:], shape[1:])))

    def sb(name, shape, dtype=F32):
        return ctx.enter_context(nc.sbuf_tensor(name, shape, dtype))

    m.w_in = sb("w_in", [P, KD, 2 * DI])
    m.w_x = carve(KI, P)
    m.w_dt = sb("w_dt", [P, DI])
    m.b_src = m.w_dt[0:1, 0:2 * D]
    m.b_xo, m.ones = m.w_dt[32:33, 0:D], m.w_dt[32:33, D:D + P]
    m.w_out = sb("w_out", [P, KI, D])
    m.w_src = sb("w_src", [P, KC, 2 * D])
    m.w_tgt = sb("w_tgt", [P, KD, D])
    m.w_xo = sb("w_xo", [P, 2 * KD, D])
    m.sh_gate = sb("sh_gate", [P, KD, FF])
    m.sh_up = sb("sh_up", [P, KD, FF])
    m.sh_down = sb("sh_down", [P, KF, D])
    m.gate_w = sb("gate_w", [P, KD, E])
    m.a_neg = sb("a_neg", [P, KI, NS])
    m.conv_w = sb("conv_w", [P, KI, 4])
    m.conv_b = sb("conv_b", [P, KI])
    m.dt_bias = sb("dt_bias", [P, KI])
    m.d_quarter = sb("d_quarter", [P, KI])
    m.b_tgt = sb("b_tgt", [P, KD])
    m.ident = sb("ident", [P, P])
    m.first = sb("first", [P, E])
    m.first_i = sb("first_i", [P, E], I32)
    m.minus_half = sb("minus_half", [P, GB])
    m.xn1T = [carve(KD, GT), sb("xn1T1", [P, KD, GT])]
    m.xc2 = [carve(KI, GT), sb("xc2_1", [P, KI, GT])]
    m.dt = [carve(KI, GT) for i in range(2)]
    m.dtx = [carve(KI, GT) for i in range(2)]
    m.c_tok = [sb(f"c_tok{i}", [P, GB, NS]) for i in range(2)]
    m.acc = sb("acc", [P, GB, DI])
    m.bb = carve(B_RING, GT)
    m.u = carve(U_RING, GT)
    m.dA = [carve(GT)] + [sb(f"dA{i}", [P, GT])[:] for i in range(1, DECAY_RING)]
    m.h = carve(H_RING, KI, GT)
    m.xin = carve(GB, D)
    m.cv = carve(GT)
    m.th = sb("th", [P, 2, GT])
    m.xdT = m.xb = carve(GT)
    m.x1 = sb("x1", [P, GB, D])
    m.xn = m.upd = sb("xn", [P, GB, D])
    m.xnT = sb("xnT", [P, KD, GT])
    m.ctx_at = sb("ctx_at", [P, KC, GT])
    m.kv_act = sb("kv_act", [P, 4, GT])
    m.q_up = sb("q_up", [P, KD, GT])
    m.sc = sb("sc", [P, ATT_RING, GT])
    m.mask_all = sb("mask_all", [P, GT])
    m.mask_neg = sb("mask_neg", [P, GT])
    m.small = {}
    for name, w in (("st1", 24), ("st2", 24), ("st3", 24), ("mv1", 8), ("mv2", 8), ("mv3", 8), ("rs1", 4), ("rs2", 4),
                    ("rs3", 4), ("nb1", 4), ("nb2", 4), ("nb3", 4), ("nmax", 32), ("sum", 32), ("rec", 32), ("mx", 4), ("eq", 32), ("m8", 4), ("oh", 32),
                    ("top", 4), ("score", 4)):
        m.small[name] = sb("s_" + name, [P, w])


def split_banks(m, banks):
    m.hT, m.other = banks[0:HT_BANKS], banks[HT_BANKS:HT_BANKS + OTHER_BANKS]


def setup(nc, m, a, sems):
    with nc.Block() as block:
        @block.sync
        def _(sp):
            def load(dst, src):
                sp.dma_start(dst, src).then_inc(sems["w"], 16)
                load.n += 16
            load.n = 0
            load(m.w_in[:], a["w_in"].rearrange("(k p) n -> p k n", p=P))
            sp.wait_ge(sems["w_clear"], 1)
            wx = a["w_x"].rearrange("(k p) n -> p k n", p=P)
            load(m.w_x[:, :, R_ROW:R_ROW + RANK], wx[:, :, 0:RANK])
            load(m.w_x[:, :, B_ROW:B_ROW + NS], wx[:, :, RANK:RANK + NS])
            load(m.w_x[:, :, C_ROW:C_ROW + NS], wx[:, :, RANK + NS:RANK + 2 * NS])
            load(m.w_dt[R_ROW:R_ROW + RANK, :], a["w_dt"])
            load(m.a_neg[:], a["a_log"].rearrange("(k p) n -> p k n", p=P))
            load(m.conv_w[:], a["conv_w"].rearrange("(k p) n -> p k n", p=P))
            load(m.conv_b[:], a["conv_b"])
            load(m.dt_bias[:], a["b_dt"])
            load(m.d_quarter[:], a["d_param"])
            load(m.b_tgt[:], a["b_tgt"])
            load(m.b_src, a["b_src"])
            load(m.b_xo, a["b_xo"])
            sp.wait_ge(sems["w"], load.n)
            sp.sem_inc(sems["w_loaded"], 1)

        @block.gpsimd
        def _(pool):
            nc.gpsimd.memset(m.x1[:, 0, :], 0.0).then_inc(sems["zero"], 1)
            nc.gpsimd.memset(m.ident[:], 0.0).then_inc(sems["id"], 1)
            pool.wait_ge(sems["id"], 1)
            nc.gpsimd.affine_select(out=m.ident[:], in_=m.ident[:], compare_op=ALU.not_equal, fill=1.0, base=0,
                                    pattern=[[-1, P]], channel_multiplier=1).then_inc(sems["id"], 1)
            nc.gpsimd.iota(m.first_i[:], [[-1, E]], base=E, channel_multiplier=0).then_inc(sems["iota"], 1)

        @block.scalar
        def _(act):
            act.wait_ge(sems["w_loaded"], 1)
            nc.scalar.activation(m.a_neg[:], m.a_neg[:], ACT.Exp).then_inc(sems["a_exp"], 1)

        @block.vector
        def _(dve):
            nc.vector.memset(m.w_x[:], 0.0).then_inc(sems["w_clear"], 1)
            nc.vector.memset(m.ones, 1.0)
            nc.vector.memset(m.minus_half[:], -0.5)
            for chunk in m.dA:
                nc.vector.memset(chunk.rearrange("p (b t) -> p b t", b=GB)[:, :, 0:1], 0.0)
            dve.wait_ge(sems["iota"], 1)
            nc.vector.tensor_copy(m.first[:], m.first_i[:])
            dve.wait_ge(sems["w_loaded"], 1)
            for t, f in ((m.dt_bias[:], 0.5), (m.d_quarter[:], 0.25),
                         (m.w_x[:, :, C_ROW:C_ROW + NS], 0.25), (m.w_x[:, :, B_ROW:B_ROW + NS], 0.25),
                         (m.w_x[:, :, R_ROW:R_ROW + RANK], 0.5)):
                nc.vector.tensor_scalar(t, t, f, None, ALU.mult)
            dve.wait_ge(sems["a_exp"], 1)
            nc.vector.tensor_scalar(m.a_neg[:], m.a_neg[:], -1.0, None, ALU.mult)


def late_loads(m, a):
    whole = lambda t: t.rearrange("(k p) n -> p k n", p=P)
    loads = [(m.w_out[:], whole(a["w_out"])), (m.w_src[:], whole(a["w_srcT"])), (m.w_tgt[:], whole(a["w_tgtT"])),
             (m.w_xo[:], whole(a["w_xoT"])), (m.sh_gate[:], whole(a["sh_gate"])), (m.sh_up[:], whole(a["sh_up"])),
             (m.sh_down[:], whole(a["sh_down"])), (m.gate_w[:], whole(a["gate_w"]))]
    return loads + [(a[name][TOKENS:TOKENS + P, :], m.x1[:, 0, :]) for name in ("xs", "out")]


def iteration(nc, m, a, S, scan=None, post=None, pre=None, parity=0, loads=()):
    do_scan, do_post, do_pre = scan is not None, post is not None, pre is not None
    other = 1 - parity
    def tables(post_steps, last_steps, pre_steps, ahead_steps=None):
        return ([post_steps if do_pre else last_steps] if do_post else []) + ([pre_steps] if do_pre else []) + (
            [ahead_steps] if do_scan and ahead_steps else [])

    order = [step for slot in range(SLOTS) for step in steps_at(slot, *tables(PE_POST, PE_LAST, PE_PRE))]
    number = {step: i for i, step in enumerate(order)}
    banks = m.other + ([] if do_scan else m.hT)
    n_banks = len(banks)

    def bank(name, k=0):
        return banks[number[name, k] % n_banks]

    def wait_bank_free(pe, name, k):
        i = number[name, k]
        if i >= n_banks:
            pe.wait_ge(S[f"bank_free{i % n_banks}"], i // n_banks)

    def wait_bank_full(eng, name, k=0):
        eng.wait_ge(S["bank_full"], number[name, k] + 1)

    def wait_bank_read(eng, name, k=0):
        eng.wait_ge(S[f"bank_free{number[name, k] % n_banks}"], number[name, k] // n_banks + 1)

    def bank_free(name, k=0):
        return S[f"bank_free{number[name, k] % n_banks}"]

    k_ap, v_ap = m.kv_act[:, 0:2, :], m.kv_act[:, 2:4, :].rearrange("p a (b f) -> p (a b) f", f=D)

    with nc.Block() as block:
        @block.sync
        def _(sp):
            if do_pre:
                sp.dma_start(m.xin[:], a["x"][bass.ts(pre, GT)].rearrange("(b p) c -> p b c", p=P)).then_inc(S["x_in"], 16)
            if do_post:
                sp.dma_start(m.x1[:], a["x"][bass.ts(post, GT)].rearrange("(b p) c -> p b c", p=P)).then_inc(S["x_res"], 16)
            for dst, src in loads:
                sp.dma_start(dst, src).then_inc(S["loaded"], 16)
            for slot in range(SLOTS):
                n = slot // KI + B_RING
                if do_scan and slot % KI == 0 and n < NS:
                    if KI * (n - B_RING + 1) > U_AHEAD:
                        sp.wait_ge(S["u_ready"], KI * (n - B_RING + 1) - U_AHEAD)
                    sp.dma_start(m.bb[:, n % B_RING, :], a["b_rows"][n:n + 1, parity * GT:(parity + 1) * GT].broadcast_to([P, GT])
                                 ).then_inc(S[f"bb{n % B_RING}"], 16)
                for name, k in steps_at(slot, *tables(SP_POST, SP_LAST, SP_PRE, SP_AHEAD)):
                    if name == "src":
                        if do_post:
                            wait_bank_full(sp, "av", 1)
                        sp.dma_start(m.mask_all[:], a["mask"][0:1, bass.ts(scan, GT)].broadcast_to([P, GT])
                                     ).then_inc(S["mask_in"], 16)
                        sp.dma_start(m.ctx_at[:], a["ctxT"][:, bass.ts(scan, GT)].rearrange("(k p) t -> p k t", p=P)
                                     ).then_inc(S["ctx_in"], 16)
                    if name == "B":
                        wait_bank_read(sp, "xd")
                        sp.dma_start(a["b_rows"][:, other * GT:(other + 1) * GT], m.xdT[B_ROW:B_ROW + NS, :]
                                     ).then_inc(S["b_stored"], 16)
                    elif name == "bb":
                        sp.wait_ge(S["b_stored"], 16)
                        if do_scan:
                            sp.wait_ge(S["u_ready"], KI * (NS - B_RING + k + 1) - U_AHEAD)
                        sp.dma_start(m.bb[:, k, :], a["b_rows"][k:k + 1, other * GT:(other + 1) * GT].broadcast_to([P, GT])
                                     ).then_inc(S["bb_ahead"], 16)
                    elif name == "oh":
                        sp.wait_ge(S["onehot"], 1)
                        sp.dma_start(a["onehot"][bass.ts(post, P), :], m.small["oh"][:]).then_inc(S["stored"], 16)
                    elif name == "xs":
                        sp.wait_ge(S["xs_ready"], 1)
                        sp.dma_start(a["xs"][bass.ts(post, GT)].rearrange("(b p) c -> p b c", p=P), m.xn[:]
                                     ).then_inc(S["stored"], 16)
                    elif name == "base":
                        wait_bank_read(sp, "dn", 0)
                        wait_bank_read(sp, "dn", 1)
                        sp.dma_start(a["out"][bass.ts(post, GT)].rearrange("(b p) c -> p b c", p=P), m.x1[:]
                                     ).then_inc(S["stored"], 16)
            if do_post:
                sp.wait_ge(S["stored"], 16 * 3)
            if do_pre:
                sp.wait_ge(S["bb_ahead"], 16 * B_RING)
            if loads:
                sp.wait_ge(S["loaded"], 16 * len(loads))

        @block.tensor
        def _(pe):
            def mm(out, lhsT, rhs, first, last):
                return nc.tensor.matmul(out, lhsT, rhs, start=first, stop=last)

            def transposes(name, k, src):
                for b in range(GB):
                    ins = nc.tensor.transpose(bank(name, k)[:, b * P:(b + 1) * P], src(b), m.ident[:])
                ins.then_inc(S["bank_full"], 1)

            def step(name, k):
                wait_bank_free(pe, name, k)
                out = bank(name, k)
                if name == "z":
                    for kk in range(KD):
                        ins = mm(out[:], m.w_in[:, kk, DI + k * P:DI + (k + 1) * P], m.xn1T[other][:, kk, :],
                                 kk == 0, kk == KD - 1)
                    ins.then_inc(S["bank_full"], 1)
                elif name == "y":
                    transposes(name, k, lambda b: m.acc[:, b, k * P:(k + 1) * P])
                elif name == "k":
                    for kk in range(KC):
                        mm(out[:], m.w_src[:, kk, k * P:(k + 1) * P], m.ctx_at[:, kk, :], kk == 0, False)
                    mm(out[:], m.b_src[:, k * P:(k + 1) * P], m.mask_all[0:1, :], False, True).then_inc(S["bank_full"], 1)
                elif name == "v":
                    for i in range(2):
                        b = 2 * k + i
                        o = out[:, i * D:(i + 1) * D]
                        for kk in range(KC):
                            mm(o, m.ctx_at[:, kk, b * P:(b + 1) * P], m.w_src[:, kk, D:2 * D], kk == 0, False)
                        ins = mm(o, m.mask_all[0:1, b * P:(b + 1) * P], m.b_src[:, D:2 * D], False, True)
                    ins.then_inc(S["bank_full"], 1)
                elif name == "o":
                    pe.wait_ge(S["y_gated"], KI)
                    for i in range(2):
                        b = 2 * k + i
                        for kk in range(KI):
                            ins = mm(out[:, i * D:(i + 1) * D], m.xc2[other][:, kk, b * P:(b + 1) * P], m.w_out[:, kk, :],
                                     kk == 0, kk == KI - 1)
                    ins.then_inc(S["bank_full"], 1)
                elif name == "t2":
                    pe.wait_ge(S["ln2_ready"], GB)
                    transposes(name, k, lambda b: m.xn[:, b, k * P:(k + 1) * P])
                elif name == "q":
                    for kk in range(KD):
                        wait_bank_read(pe, "t2", kk)
                    for kk in range(KD):
                        ins = mm(out[:], m.w_tgt[:, kk, k * P:(k + 1) * P], m.xnT[:, kk, :], kk == 0, kk == KD - 1)
                    ins.then_inc(S["bank_full"], 1)
                elif name == "s":
                    c, j = k // HC, k % HC
                    wait_bank_read(pe, "q", c)
                    wait_bank_read(pe, "k", c)
                    rows = slice(HD * j, HD * (j + 1))
                    for b in range(GB):
                        ins = mm(out[:, b * P:(b + 1) * P], m.q_up[rows, c, b * P:(b + 1) * P],
                                 k_ap[rows, c, b * P:(b + 1) * P], True, True)
                    ins.then_inc(S["bank_full"], 1)
                elif name == "a":
                    pe.wait_ge(S["att_exp"], GB * (k + 1))
                    transposes(name, k, lambda b: m.sc[:, k % ATT_RING, b * P:(b + 1) * P])
                elif name == "av":
                    for j in range(HC):
                        wait_bank_read(pe, "a", HC * k + j)
                    wait_bank_read(pe, "v", 0)
                    wait_bank_read(pe, "v", 1)
                    for b in range(GB):
                        for j in range(HC):
                            f = b * P + j * HD
                            ins = mm(out[:, f:f + HD], m.ctx_at[:, j, b * P:(b + 1) * P],
                                     v_ap[:, b, k * P + j * HD:k * P + (j + 1) * HD], True, True)
                    ins.then_inc(S["bank_full"], 1)
                elif name == "ut":
                    wait_bank_read(pe, "av", k)
                    transposes(name, k, lambda b: m.upd[:, b, k * P:(k + 1) * P])
                elif name == "xo":
                    for kk in range(KD):
                        wait_bank_read(pe, "ut", kk)
                    for i in range(2):
                        b = 2 * k + i
                        o = out[:, i * D:(i + 1) * D]
                        for kk in range(KD):
                            mm(o, m.xnT[:, kk, b * P:(b + 1) * P], m.w_xo[:, kk, :], kk == 0, False)
                        for kk in range(KD):
                            mm(o, m.q_up[:, kk, b * P:(b + 1) * P], m.w_xo[:, KD + kk, :], False, False)
                        ins = mm(o, m.ones, m.b_xo, False, True)
                    ins.then_inc(S["bank_full"], 1)
                elif name == "t3":
                    pe.wait_ge(S["ln3_ready"], GB)
                    transposes(name, k, lambda b: m.xn[:, b, k * P:(k + 1) * P])
                elif name == "lg":
                    for kk in range(KD):
                        wait_bank_read(pe, "t3", kk)
                    for b in range(GB):
                        for kk in range(KD):
                            ins = mm(out[:, b * E:(b + 1) * E], m.xnT[:, kk, b * P:(b + 1) * P], m.gate_w[:, kk, :],
                                     kk == 0, kk == KD - 1)
                    ins.then_inc(S["bank_full"], 1)
                elif name in ("g", "u"):
                    w = m.sh_gate if name == "g" else m.sh_up
                    if k == 0:
                        for kk in range(KD):
                            wait_bank_read(pe, "t3", kk)
                    for kk in range(KD):
                        ins = mm(out[:], w[:, kk, k * P:(k + 1) * P], m.xnT[:, kk, :], kk == 0, kk == KD - 1)
                    ins.then_inc(S["bank_full"], 1)
                elif name == "dn":
                    for kk in range(KF):
                        wait_bank_read(pe, "u", kk)
                    for i in range(2):
                        b = 2 * k + i
                        for kk in range(KF):
                            ins = mm(out[:, i * D:(i + 1) * D], m.kv_act[:, kk, b * P:(b + 1) * P], m.sh_down[:, kk, :],
                                     kk == 0, kk == KF - 1)
                    ins.then_inc(S["bank_full"], 1)
                elif name == "t1":
                    pe.wait_ge(S["ln1_ready"], GB)
                    transposes(name, k, lambda b: m.xin[:, b, k * P:(k + 1) * P])
                elif name == "xb":
                    for kk in range(KD):
                        wait_bank_read(pe, "t1", kk)
                    for kk in range(KD):
                        ins = mm(out[:], m.w_in[:, kk, k * P:(k + 1) * P], m.xn1T[other][:, kk, :], kk == 0, kk == KD - 1)
                    ins.then_inc(S["bank_full"], 1)
                elif name == "xd":
                    pe.wait_ge(S["xc2_ready"], KI)
                    for kk in range(KI):
                        ins = mm(out[:], m.w_x[:, kk, :], m.xc2[other][:, kk, :], kk == 0, kk == KI - 1)
                    ins.then_inc(S["bank_full"], 1)
                elif name == "ct":
                    wait_bank_read(pe, "xd")
                    for b in range(GB):
                        ins = nc.tensor.transpose(out[:, b * NS:(b + 1) * NS], m.xdT[C_ROW:C_ROW + NS, b * P:(b + 1) * P],
                                                  m.ident[0:NS, 0:NS])
                    ins.then_inc(S["bank_full"], 1)
                elif name == "dt":
                    wait_bank_read(pe, "xd")
                    mm(out[:], m.w_dt[R_ROW:R_ROW + RANK, k * P:(k + 1) * P], m.xdT[R_ROW:R_ROW + RANK, :],
                       True, True).then_inc(S["bank_full"], 1)

            for slot in range(SLOTS):
                if do_scan and HT_LAG <= slot < HT_LAG + SCAN_SLOTS:
                    i = slot - HT_LAG
                    n, b = i // KI, i % KI
                    pe.wait_ge(S["h_ready"], KI * (n + 1))
                    if i >= HT_BANKS:
                        pe.wait_ge(S["acc_done"], i - HT_BANKS + 1)
                    for c in range(KI):
                        ins = nc.tensor.transpose(m.hT[i % HT_BANKS][:, c * P:(c + 1) * P], m.h[:, n % H_RING, c, b * P:(b + 1) * P],
                                                  m.ident[:])
                    ins.then_inc(S["hT_ready"], 1)
                for name, k in steps_at(slot, *tables(PE_POST, PE_LAST, PE_PRE)):
                    step(name, k)

        @block.scalar
        def _(act):
            def copy(out, in_):
                return nc.scalar.activation(out, in_, ACT.Copy)

            def decay(i, group_parity, ready):
                n, c = i // KI, i % KI
                nc.scalar.activation(m.dA[i % DECAY_RING].rearrange("p (b t) -> p b t", b=GB)[:, :, 1:P],
                                     m.dt[group_parity][:, c, :].rearrange("p (b t) -> p b t", b=GB)[:, :, 1:P],
                                     ACT.Exp, scale=m.a_neg[:, c, n:n + 1]).then_inc(S[ready], 1)

            def step(name, k):
                if name == "z":
                    wait_bank_full(act, "z", k)
                    if k >= 2:
                        act.wait_ge(S["y_gated"], k - 1)
                    nc.scalar.activation(m.th[:, k % 2, :], bank("z", k)[:], ACT.Tanh, scale=0.5).then_inc(S["z_tanh"], 1)
                elif name == "k":
                    wait_bank_full(act, "k", k)
                    copy(k_ap[:, k, :], bank("k", k)[:]).then_inc(bank_free("k", k), 1)
                elif name == "v":
                    wait_bank_full(act, "v", k)
                    copy(v_ap[:, 2 * k:2 * k + 2, :], bank("v", k)[:].rearrange("p (b f) -> p b f", f=D)
                         ).then_inc(bank_free("v", k), 1)
                elif name in ("t1", "t2", "t3", "ut", "a", "xd"):
                    wait_bank_full(act, name, k)
                    if name == "t1":
                        if do_post:
                            wait_bank_full(act, "z", KI - 1)
                        dst = m.xn1T[other][:, k, :]
                    elif name == "t2":
                        dst = m.xnT[:, k, :]
                    elif name == "t3":
                        wait_bank_full(act, "xo", 1)
                        dst = m.xnT[:, k, :]
                    elif name == "ut":
                        wait_bank_full(act, "s", HEADS - 1)
                        dst = m.q_up[:, k, :]
                    elif name == "a":
                        wait_bank_full(act, "v", 1)
                        wait_bank_full(act, "k", 1)
                        if k >= HC:
                            wait_bank_full(act, "av", 0)
                        dst = m.ctx_at[:, k % HC, :]
                    else:
                        dst = m.xdT[:]
                    copy(dst, bank(name, k)[:]).then_inc(bank_free(name, k), 1)
                elif name == "s":
                    act.wait_ge(S["neg_max"], k + 1)
                    for b in range(GB):
                        nc.scalar.activation(m.sc[:, k % ATT_RING, b * P:(b + 1) * P], m.sc[:, k % ATT_RING, b * P:(b + 1) * P], ACT.Exp,
                                             bias=m.small["nmax"][:, k * GB + b:k * GB + b + 1],
                                             accum_out=m.small["sum"][:, k * GB + b:k * GB + b + 1]).then_inc(S["att_exp"], 1)
                elif name in ("n1", "n2", "n3"):
                    which = int(name[1])
                    act.wait_ge(S[f"rs{which}"], 4)
                    src, dst = (m.xin, m.xin) if which == 1 else (m.x1, m.xn)
                    if which == 3:
                        wait_bank_full(act, "ut", 1)
                    for b in range(GB):
                        nc.scalar.activation(dst[:, b, :], src[:, b, :], ACT.Identity, bias=m.small[f"nb{which}"][:, b:b + 1],
                                             scale=m.small[f"rs{which}"][:, b:b + 1]).then_inc(S[f"ln{which}_ready"], 1)
                elif name == "lg":
                    act.wait_ge(S["top_logit"], 1)
                    nc.scalar.activation(m.small["top"][:], m.small["mx"][:], ACT.Tanh, scale=0.5).then_inc(S["top_tanh"], 1)
                elif name == "g":
                    wait_bank_full(act, "g", k)
                    if k >= ATT_RING:
                        wait_bank_read(act, "g", k - ATT_RING)
                    nc.scalar.activation(m.sc[:, k % ATT_RING, :], bank("g", k)[:], ACT.Tanh, scale=0.5).then_inc(S["g_tanh"], 1)
                elif name == "xb":
                    wait_bank_full(act, "xb", k)
                    if k >= 1:
                        act.wait_ge(S["xc2_ready"], k)
                    nc.scalar.activation(m.cv[:], bank("xb", k)[:], ACT.Identity, bias=m.conv_b[:, k:k + 1],
                                         scale=m.conv_w[:, k, 3:4]).then_inc(S["tap3"], 1)
                    copy(m.xb[:], bank("xb", k)[:]).then_inc(bank_free("xb", k), 1)
                elif name == "th":
                    act.wait_ge(S["conv_done"], 3 * (k + 1))
                    if do_post:
                        act.wait_ge(S["y_gated"], KI)
                    nc.scalar.activation(m.th[:, k % 2, :], m.cv[:], ACT.Tanh, scale=0.5).then_inc(S["cv_tanh"], 1)
                elif name == "dt":
                    wait_bank_full(act, "dt", k)
                    nc.scalar.activation(m.dt[other][:, k, :], bank("dt", k)[:], ACT.Tanh, bias=m.dt_bias[:, k:k + 1],
                                         scale=0.5).then_inc(bank_free("dt", k), 1)

            for slot in range(SLOTS):
                i = slot + DECAY_RING - 1
                if do_scan and DECAY_RING <= i < SCAN_SLOTS:
                    if slot >= 1:
                        act.wait_ge(S["h_ready"], slot)
                    decay(i, parity, "dA_ready")
                for name, k in steps_at(slot, *tables(ACT_POST, ACT_LAST, ACT_PRE)):
                    step(name, k)

            if do_pre:
                for i in range(DECAY_RING):
                    act.wait_ge(S["dt_ready"], i + 1)
                    if do_scan:
                        act.wait_ge(S["h_ready"], last_user(i, DECAY_RING) + 1)
                    decay(i, other, "dA_ahead")

        @block.vector
        def _(dve):
            stt = nc.vector.scalar_tensor_tensor
            ts = nc.vector.tensor_scalar

            def norm_stats(which, src):
                st, mv = m.small[f"st{which}"], m.small[f"mv{which}"]
                for b in range(GB):
                    nc.vector.bn_stats(st[:, 6 * b:6 * b + 6], src[:, b, :]).then_inc(S[f"bn{which}"], 1)
                for b in range(GB):
                    dve.wait_ge(S[f"bn{which}"], b + 1)
                    nc.vector.bn_aggr(mv[:, 2 * b:2 * b + 2], st[:, 6 * b:6 * b + 6]).then_inc(S[f"mv{which}_ready"], 1)

            def step(name, k):
                if name == "mb":
                    dve.wait_ge(S["mask_in"], 16)
                    if do_post:
                        wait_bank_read(dve, "s", HEADS - 1)
                    ts(m.mask_neg[:], m.mask_all[:], 0.0, MASKED, ALU.is_equal, ALU.mult)
                elif name == "z":
                    dve.wait_ge(S["z_tanh"], k + 1)
                    stt(m.th[:, k % 2, :], m.th[:, k % 2, :], 1.0, bank("z", k)[:], ALU.add, ALU.mult
                        ).then_inc(bank_free("z", k), 1)
                    wait_bank_full(dve, "y", k)
                    xc2 = m.xc2[other][:, k, :]
                    stt(xc2, xc2, m.d_quarter[:, k:k + 1], bank("y", k)[:], ALU.mult, ALU.add).then_inc(bank_free("y", k), 1)
                elif name in ("o", "xo", "dn"):
                    wait_bank_full(dve, name, k)
                    x = m.x1[:, 2 * k:2 * k + 2, :]
                    if name == "o":
                        dve.wait_ge(S["x_res"], 16)
                    else:
                        wait_bank_read(dve, "o" if name == "xo" else "xo", k)
                    new = bank(name, k)[:].rearrange("p (b f) -> p b f", f=D)
                    if name == "dn":
                        stt(x, new, 0.5, x, ALU.mult, ALU.add).then_inc(bank_free(name, k), 1)
                    else:
                        nc.vector.tensor_tensor(x, x, new, ALU.add).then_inc(bank_free(name, k), 1)
                elif name == "ln1":
                    dve.wait_ge(S["x_in"], 16)
                    norm_stats(1, m.xin)
                elif name == "ln2":
                    wait_bank_read(dve, "o", 0)
                    wait_bank_read(dve, "o", 1)
                    norm_stats(2, m.x1)
                elif name == "ln3":
                    wait_bank_read(dve, "xo", 0)
                    wait_bank_read(dve, "xo", 1)
                    norm_stats(3, m.x1)
                elif name == "q":
                    wait_bank_full(dve, "q", k)
                    stt(m.q_up[:, k, :], bank("q", k)[:], m.b_tgt[:, k:k + 1], m.mask_all[:], ALU.add, ALU.mult
                        ).then_inc(bank_free("q", k), 1)
                elif name == "s":
                    wait_bank_full(dve, "s", k)
                    if k >= ATT_RING:
                        wait_bank_full(dve, "a", k - ATT_RING)
                    stt(m.sc[:, k % ATT_RING, :], bank("s", k)[:], ATT_SCALE, m.mask_neg[:], ALU.mult, ALU.add
                        ).then_inc(bank_free("s", k), 1)
                    wait_bank_read(dve, "s", k)
                    nc.vector.tensor_reduce(m.small["nmax"][:, GB * k:GB * (k + 1)],
                                            m.sc[:, k % ATT_RING, :].rearrange("p (b t) -> p b t", b=GB), AX.X, ALU.max,
                                            negate=True).then_inc(S["neg_max"], 1)
                elif name == "r":
                    dve.wait_ge(S["att_exp"], GB * HC * (k + 1))
                    w = HC * GB
                    nc.vector.reciprocal(m.small["rec"][:, w * k:w * (k + 1)], m.small["sum"][:, w * k:w * (k + 1)]
                                         ).then_inc(S["rec_ready"], 1)
                elif name == "av":
                    wait_bank_full(dve, "av", k)
                    wait_bank_full(dve, "t2", 1)
                    dve.wait_ge(S["rec_ready"], k + 1)
                    w = HC * GB
                    rec = m.small["rec"][:, w * k:w * (k + 1)].rearrange("p (j b) -> p b j", b=GB)
                    nc.vector.tensor_tensor(m.upd[:, :, k * P:(k + 1) * P].rearrange("p b (j f) -> p b j f", f=HD),
                                            bank("av", k)[:].rearrange("p (b j f) -> p b j f", b=GB, f=HD),
                                            rec.unsqueeze(3).broadcast_to([P, GB, HC, HD]), ALU.mult
                                            ).then_inc(bank_free("av", k), 1)
                elif name == "lg":
                    wait_bank_full(dve, "lg")
                    lg = bank("lg")[:, 0:GB * E].rearrange("p (b e) -> p b e", e=E)
                    v3 = lambda t: m.small[t][:].rearrange("p (b e) -> p b e", e=E)
                    row = lambda t: m.small[t][:].unsqueeze(2).broadcast_to([P, GB, E])
                    first = m.first[:].unsqueeze(1).broadcast_to([P, GB, E])
                    nc.vector.tensor_reduce(m.small["mx"][:], lg, AX.X, ALU.max).then_inc(S["top_logit"], 1)
                    dve.wait_ge(S["top_logit"], 1)
                    nc.vector.tensor_tensor(v3("eq"), lg, row("mx"), ALU.is_equal).then_inc(bank_free("lg"), 1)
                    wait_bank_read(dve, "lg")
                    nc.vector.tensor_tensor(v3("eq"), v3("eq"), first, ALU.mult).then_inc(S["route"], 1)
                    dve.wait_ge(S["route"], 1)
                    nc.vector.tensor_reduce(m.small["m8"][:], v3("eq"), AX.X, ALU.max).then_inc(S["route"], 1)
                    dve.wait_ge(S["route"], 2)
                    nc.vector.tensor_tensor(v3("oh"), first, row("m8"), ALU.is_equal).then_inc(S["onehot"], 1)
                elif name == "g":
                    dve.wait_ge(S["g_tanh"], k + 1)
                    if k == 0:
                        wait_bank_full(dve, "av", 1)
                    x = m.kv_act[:, k, :]
                    stt(x, m.sc[:, k % ATT_RING, :], 1.0, bank("g", k)[:], ALU.add, ALU.mult).then_inc(bank_free("g", k), 1)
                    wait_bank_read(dve, "g", k)
                    wait_bank_full(dve, "u", k)
                    nc.vector.tensor_tensor(x, x, bank("u", k)[:], ALU.mult).then_inc(bank_free("u", k), 1)
                elif name == "cv":
                    wait_bank_read(dve, "xb", k)
                    dve.wait_ge(S["tap3"], k + 1)
                    cv = m.cv[:].rearrange("p (b t) -> p b t", b=GB)
                    xb = m.xb[:].rearrange("p (b t) -> p b t", b=GB)
                    for j in range(1, 4):
                        if j > 1:
                            dve.wait_ge(S["conv_done"], 3 * k + j - 1)
                        stt(cv[:, :, j:P], xb[:, :, 0:P - j], m.conv_w[:, k, 3 - j:4 - j], cv[:, :, j:P], ALU.mult, ALU.add
                            ).then_inc(S["conv_done"], 1)
                elif name == "xc":
                    dve.wait_ge(S["cv_tanh"], k + 1)
                    if do_post:
                        wait_bank_full(dve, "o", 1)
                    stt(m.xc2[other][:, k, :], m.th[:, k % 2, :], 1.0, m.cv[:], ALU.add, ALU.mult
                        ).then_inc(S["xc2_ready"], 1)
                elif name == "ct":
                    wait_bank_full(dve, "ct")
                    nc.vector.tensor_copy(m.c_tok[other][:].rearrange("p b n -> p (b n)"), bank("ct")[:, 0:GB * NS]
                                          ).then_inc(bank_free("ct"), 1)
                elif name == "dt":
                    wait_bank_read(dve, "dt", k)
                    d = m.dt[other][:, k, :]
                    half = 0.5 * (DT_MAX - DT_MIN)
                    ts(d, d, half, half + DT_MIN, ALU.mult, ALU.add).then_inc(S["dt_lin"], 1)
                    dve.wait_ge(S["dt_lin"], k + 1)
                    ts(d, d, 1e-4, None, ALU.max).then_inc(S["dt_ready"], 1)

            for slot in range(SLOTS):
                if do_scan and slot < SCAN_SLOTS:
                    n, c = slot // KI, slot % KI
                    if slot >= DECAY_RING:
                        dve.wait_ge(S["dA_ready"], slot - DECAY_RING + 1)
                    if slot >= U_AHEAD:
                        dve.wait_ge(S["u_ready"], slot - U_AHEAD + 1)
                    if n >= H_RING:
                        dve.wait_ge(S["hT_ready"], KI * (n - H_RING + 1))
                    nc.vector.tensor_tensor_scan(m.h[:, n % H_RING, c, :], m.dA[slot % DECAY_RING][:], m.u[:, slot % U_RING, :], 0.0,
                                                 ALU.mult, ALU.add).then_inc(S["h_ready"], 1)
                if do_scan and slot >= ACC_LAG:
                    i = slot - ACC_LAG
                    n, b = i // KI, i % KI
                    dve.wait_ge(S["hT_ready"], i + 1)
                    cn = m.c_tok[parity][:, b, n:n + 1]
                    if n == 0:
                        if do_post:
                            wait_bank_full(dve, "y", KI - 1)
                        ts(m.acc[:, b, :], m.hT[i % HT_BANKS][:], cn, None, ALU.mult).then_inc(S["acc_done"], 1)
                    else:
                        dve.wait_ge(S["acc_done"], i - KI + 1)
                        stt(m.acc[:, b, :], m.hT[i % HT_BANKS][:], cn, m.acc[:, b, :], ALU.mult, ALU.add
                            ).then_inc(S["acc_done"], 1)
                for name, k in steps_at(slot, *tables(DVE_POST, DVE_LAST, DVE_PRE, DVE_AHEAD)):
                    step(name, k)

        @block.gpsimd
        def _(pool):
            tt, ts = nc.gpsimd.tensor_tensor, nc.gpsimd.tensor_scalar

            def drive(i, group_parity, ready):
                n, c = i // KI, i % KI
                tt(m.u[:, i % U_RING, :], m.dtx[group_parity][:, c, :], m.bb[:, n % B_RING, :], ALU.mult).then_inc(S[ready], 1)

            def norm_factors(which):
                mv, rs, nb = (m.small[f"{t}{which}"] for t in ("mv", "rs", "nb"))
                pool.wait_ge(S[f"mv{which}_ready"], GB)
                ts(rs[:], mv[:].rearrange("p (b v) -> p b v", v=2)[:, :, 1], EPS, None, ALU.add).then_inc(S[f"rs{which}"], 1)
                pool.wait_ge(S[f"rs{which}"], 1)
                tt(rs[:], rs[:], m.minus_half[:], ALU.pow).then_inc(S[f"rs{which}"], 1)
                pool.wait_ge(S[f"rs{which}"], 2)
                mean = mv[:].rearrange("p (b v) -> p b v", v=2)[:, :, 0]
                tt(nb[:], mean, rs[:], ALU.mult).then_inc(S[f"rs{which}"], 1)
                pool.wait_ge(S[f"rs{which}"], 3)
                ts(nb[:], nb[:], -1.0, None, ALU.mult).then_inc(S[f"rs{which}"], 1)

            def step(name, k):
                if name == "yz":
                    wait_bank_read(pool, "z", k)
                    wait_bank_read(pool, "y", k)
                    xc2 = m.xc2[other][:, k, :]
                    tt(xc2, xc2, m.th[:, k % 2, :], ALU.mult).then_inc(S["y_gated"], 1)
                elif name == "cm":
                    pool.wait_ge(S["ctx_in"], 16)
                    pool.wait_ge(S["mask_in"], 16)
                    tt(m.ctx_at[:], m.ctx_at[:], m.mask_all[:].unsqueeze(1).broadcast_to([P, KC, GT]), ALU.mult)
                elif name == "ln1":
                    norm_factors(1)
                elif name == "ln2":
                    norm_factors(2)
                elif name == "ln3":
                    norm_factors(3)
                elif name == "xs":
                    pool.wait_ge(S["top_tanh"], 1)
                    ts(m.small["score"][:], m.small["top"][:], 0.5, 0.5, ALU.mult, ALU.add).then_inc(S["score"], 1)
                    pool.wait_ge(S["score"], 1)
                    pool.wait_ge(S["ln3_ready"], GB)
                    wait_bank_full(pool, "t3", 1)
                    tt(m.xn[:], m.xn[:], m.small["score"][:].unsqueeze(2).broadcast_to([P, GB, D]), ALU.mult
                       ).then_inc(S["xs_ready"], 1)
                elif name == "dx":
                    pool.wait_ge(S["dt_ready"], k + 1)
                    tt(m.dtx[other][:, k, :], m.dt[other][:, k, :], m.xc2[other][:, k, :], ALU.mult).then_inc(S["dtx_ready"], 1)

            for slot in range(SLOTS):
                i = slot + U_RING - 1
                if do_scan and U_AHEAD <= i < SCAN_SLOTS:
                    n = i // KI
                    if n >= B_RING:
                        pool.wait_ge(S[f"bb{n % B_RING}"], 16 * (n // B_RING))
                    if slot >= 1:
                        pool.wait_ge(S["h_ready"], slot)
                    drive(i, parity, "u_ready")
                for name, k in steps_at(slot, *tables(POOL_POST, POOL_LAST, POOL_PRE, POOL_AHEAD)):
                    step(name, k)

            if do_pre:
                pool.wait_ge(S["bb_ahead"], 16 * B_RING)
                for i in range(U_AHEAD):
                    pool.wait_ge(S["dtx_ready"], i % KI + 1)
                    if do_scan:
                        pool.wait_ge(S["h_ready"], last_user(i, U_RING) + 1)
                    drive(i, other, "u_ahead")

    with nc.Block() as block:
        @block.gpsimd
        def _(pool):
            for s in S.values():
                pool.sem_clear(s)


A_SEMS = ("acc_done", "att_exp", "b_stored", "bank_free0", "bank_free1", "bank_free2", "bank_free3", "bank_free4",
          "bank_free5", "bank_free6", "bank_free7", "bank_full", "bb0", "bb1", "bb2", "bb3", "bb_ahead", "bn1",
          "bn2", "bn3", "conv_done", "ctx_in", "cv_tanh", "dA_ahead", "dA_ready", "dt_lin", "dt_ready",
          "dtx_ready", "g_tanh", "hT_ready", "h_ready", "ln1_ready", "ln2_ready", "ln3_ready", "loaded",
          "mask_in", "mv1_ready", "mv2_ready", "mv3_ready", "neg_max", "onehot", "rec_ready", "route", "rs1",
          "rs2", "rs3", "score", "stored", "tap3", "top_logit", "top_tanh", "u_ahead", "u_ready", "x_in",
          "x_res", "xc2_ready", "xs_ready", "y_gated", "z_tanh")


def expert_weights(shared):
    gu, d = E * KD * FF, E * KF * D
    return shared[:, 0:gu], shared[:, gu:2 * gu], shared[:, 2 * gu:2 * gu + d]


def phase_a(nc, a, shared):
    with ExitStack() as ctx:
        m = Memory()
        phase_a_memory(nc, ctx, m, shared)
        banks = [ctx.enter_context(nc.psum_tensor(f"bank{i}", [P, GT], F32)) for i in range(8)]
        split_banks(m, banks)
        ws = {n: ctx.enter_context(nc.semaphore("s_" + n)) for n in ("w", "w_clear", "w_loaded", "id", "iota", "a_exp", "zero")}
        S = {n: ctx.enter_context(nc.semaphore("s_" + n)) for n in A_SEMS}
        setup(nc, m, a, ws)
        iteration(nc, m, a, S, pre=0, parity=1, loads=late_loads(m, a))
        iteration(nc, m, a, S, scan=0, pre=1, parity=0)
        with nc.Fori(0, GROUPS // 2 - 1) as j:
            iteration(nc, m, a, S, scan=2 * j + 1, post=2 * j, pre=2 * j + 2, parity=1)
            iteration(nc, m, a, S, scan=2 * j + 2, post=2 * j + 1, pre=2 * j + 3, parity=0)
        iteration(nc, m, a, S, scan=GROUPS - 1, post=GROUPS - 2, parity=1)
        rt = lambda t, k: (t.rearrange("p (k n) -> p k n", k=E * k))
        iteration(nc, m, a, S, post=GROUPS - 1, parity=0, loads=[
            (rt(w, k), a[name].rearrange("e (k p) n -> p (e k) n", p=P))
            for w, name, k in zip(expert_weights(shared), ("rt_gate", "rt_up", "rt_down"), (KD, KD, KF))])


def route_and_run_experts(nc, a, shared):
    with ExitStack() as ctx:
        def sb(name, shape, dtype=F32):
            return ctx.enter_context(nc.sbuf_tensor(name, shape, dtype))

        def sem(name):
            return ctx.enter_context(nc.semaphore(name))

        w_gate, w_up, w_down = expert_weights(shared)
        oh = sb("oh_all", [P, SEQS, E])
        before = sb("before", [P, P])
        ones = sb("e_ones", [P, P])
        ident = sb("e_ident", [P, P])
        incl = sb("incl", [P, SEQS, E])
        rank = sb("rank", [P, SEQS, E])
        row_i = sb("row_i", [P, P], I32)
        row = sb("row", [P, P])
        steps = sb("steps", [P, SEQS])
        token_i = sb("token_i", [P, SEQS + 1], I32)
        token = sb("token", [P, SEQS + 1])
        more = sb("more", [P, E, SEQS])
        past = sb("past", [P, TILES, E])
        need = sb("need", [P, E])
        ends = sb("ends", [P, E])
        starts = sb("starts", [P, E])
        pos_f = sb("pos_f", [P, SEQS])
        pos_i = sb("pos_i", [P, SEQS], I32)
        part_i = sb("part_i", [P, 2, SEQS], I32)
        part = sb("part", [P, 2, SEQS])
        at_lane = sb("at_lane", [P, SEQS, P])
        at_tile = sb("at_tile", [P, SEQS, 2, TILES])
        slot_f = sb("slot_f", [P, TILES])
        free = sb("free", [P, TILES])
        slot = sb("slot", [P, TILES + X_RING], U32)
        slot_now = sb("slot_now", [P, TPB + X_RING], U32)
        owner_f = sb("owner_f", [P, TILES])
        owner = sb("owner", [P, TILES], I32)
        x = sb("e_x", [P, X_RING, D])
        xT = sb("e_xT", [P, 2, KD, P])
        act_t = sb("e_act", [P, 2, FF])
        th = sb("e_th", [P, 2, FF])
        actT = sb("e_actT", [P, 2, KF, P])
        y = sb("e_y", [P, Y_RING, D])
        psum = [ctx.enter_context(nc.psum_tensor(f"e_bank{i}", [P, FF], F32)) for i in range(8)]
        s_oh, s_const, s_iota, s_ones, s_counts, s_seq, s_spread, s_slots, s_first = (
            sem("t_" + n) for n in ("onehot", "const", "iota", "ones", "counts", "chain", "spread", "slots", "first"))

        def gather(table, column, place, signal):
            nc.gpsimd.indirect_dma_start(x[:, place, :], None, a["xs"],
                                         bass.IndirectOffsetOnAxis(ap=table[:, column:column + 1], axis=0)
                                         ).then_inc(signal, 16)

        with nc.Block() as block:
            @block.sync
            def _(sp):
                sp.dma_start(oh[:].rearrange("p (g b) e -> p g (b e)", g=GROUPS),
                             a["onehot"].rearrange("(g p) c -> p g c", p=P)).then_inc(s_oh, 16)

            @block.gpsimd
            def _(pool):
                gp = nc.gpsimd
                gp.memset(ident[:], 0.0).then_inc(s_iota, 1)
                gp.memset(before[:], 1.0).then_inc(s_iota, 1)
                gp.iota(row_i[:], [[1, P]], base=0, channel_multiplier=0).then_inc(s_iota, 1)
                gp.iota(token_i[:], [[P, SEQS + 1]], base=0, channel_multiplier=1).then_inc(s_iota, 1)
                pool.wait_ge(s_iota, 4)
                gp.affine_select(out=ident[:], in_=ident[:], compare_op=ALU.not_equal, fill=1.0, base=0,
                                 pattern=[[-1, P]], channel_multiplier=1).then_inc(s_const, 1)
                gp.affine_select(out=before[:], in_=before[:], compare_op=ALU.is_gt, fill=0.0, base=0,
                                 pattern=[[1, P]], channel_multiplier=-1).then_inc(s_const, 1)
                pool.wait_ge(s_slots, 2)
                for j in range(X_RING):
                    gather(slot, j, j, s_first)
                pool.wait_ge(s_first, 16 * X_RING)

            @block.tensor
            def _(pe):
                pe.wait_ge(s_oh, 16)
                pe.wait_ge(s_const, 2)
                pe.wait_ge(s_ones, 1)
                flat = oh[:].rearrange("p s e -> p (s e)")
                nc.tensor.matmul(psum[0][:, 0:SEQS * E], before[:], flat, start=True, stop=True)
                nc.tensor.matmul(psum[1][:, 0:SEQS * E], ones[:], flat, start=True, stop=True).then_inc(s_counts, 1)
                pe.wait_ge(s_spread, 3)
                for t in range(SEQS):
                    ins = nc.tensor.matmul(psum[2][:, 0:2 * TILES], at_lane[:, t, :],
                                           at_tile[:, t, :, :].rearrange("p a j -> p (a j)"),
                                           start=(t == 0), stop=(t == SEQS - 1))
                ins.then_inc(s_slots, 1)

            @block.vector
            def _(dve):
                chain = [0]

                def link(ins):
                    chain[0] += 1
                    ins.then_inc(s_seq, 1)
                    dve.wait_ge(s_seq, chain[0])

                v = nc.vector
                v.memset(ones[:], 1.0).then_inc(s_ones, 1)
                dve.wait_ge(s_iota, 4)
                link(v.tensor_copy(row[:], row_i[:]))
                link(v.tensor_copy(token[:], token_i[:]))
                link(v.tensor_scalar(steps[:], row[:, 0:SEQS], float(P), None, ALU.mult))
                dve.wait_ge(s_ones, 1)
                dve.wait_ge(s_counts, 1)
                in_tile = psum[0][:, 0:SEQS * E].rearrange("p (s e) -> p s e", e=E)
                counts = psum[1][:, 0:SEQS * E].rearrange("p (s e) -> p s e", e=E)
                for e in range(E):
                    ins = v.tensor_tensor_scan(incl[:, :, e], ones[:, 0:SEQS], counts[:, :, e], 0.0, ALU.mult, ALU.add)
                link(ins)
                total = incl[:, SEQS - 1, :]
                link(v.tensor_tensor(more[:], total.unsqueeze(2).broadcast_to([P, E, SEQS]),
                                     steps[:].unsqueeze(1).broadcast_to([P, E, SEQS]), ALU.is_gt))
                link(v.tensor_reduce(need[:], more[:], AX.X, ALU.add))
                link(v.tensor_tensor_scan(ends[:], ones[:, 0:E], need[:], 0.0, ALU.mult, ALU.add))
                link(v.tensor_tensor(starts[:], ends[:], need[:], ALU.subtract))
                link(v.tensor_scalar(starts[:], starts[:], float(P), None, ALU.mult))
                link(v.tensor_tensor(rank[:], incl[:], counts, ALU.subtract))
                link(v.tensor_tensor(rank[:], rank[:], in_tile, ALU.add))
                link(v.tensor_tensor(rank[:], rank[:], starts[:].unsqueeze(1).broadcast_to([P, SEQS, E]), ALU.add))
                dve.wait_ge(s_oh, 16)
                link(v.tensor_tensor(rank[:], rank[:], oh[:], ALU.mult))
                link(v.tensor_reduce(pos_f[:], rank[:], AX.X, ALU.add))
                link(v.tensor_copy(pos_i[:], pos_f[:]))
                link(v.tensor_single_scalar(part_i[:, 0, :], pos_i[:], P - 1, ALU.bitwise_and))
                link(v.tensor_single_scalar(part_i[:, 1, :], pos_i[:], P.bit_length() - 1, ALU.logical_shift_right))
                link(v.tensor_copy(part[:], part_i[:]))
                v.tensor_tensor(at_lane[:], part[:, 0, :].unsqueeze(2).broadcast_to([P, SEQS, P]),
                                row[:].unsqueeze(1).broadcast_to([P, SEQS, P]), ALU.is_equal).then_inc(s_spread, 1)
                v.tensor_tensor(at_tile[:, :, 1, :], part[:, 1, :].unsqueeze(2).broadcast_to([P, SEQS, TILES]),
                                row[:, 0:TILES].unsqueeze(1).broadcast_to([P, SEQS, TILES]), ALU.is_equal
                                ).then_inc(s_spread, 1)
                dve.wait_ge(s_spread, 2)
                v.tensor_tensor(at_tile[:, :, 0, :], at_tile[:, :, 1, :],
                                token[:, 0:SEQS].unsqueeze(2).broadcast_to([P, SEQS, TILES]), ALU.mult
                                ).then_inc(s_spread, 1)
                link(v.tensor_tensor(past[:], ends[:].unsqueeze(1).broadcast_to([P, TILES, E]),
                                     row[:, 0:TILES].unsqueeze(2).broadcast_to([P, TILES, E]), ALU.is_le))
                link(v.tensor_reduce(owner_f[:], past[:], AX.X, ALU.add))
                link(v.tensor_scalar(owner_f[:], owner_f[:], float(E - 1), None, ALU.min))
                v.tensor_copy(owner[:], owner_f[:])
                dve.wait_ge(s_slots, 1)
                link(v.tensor_scalar(free[:], psum[2][:, TILES:2 * TILES], -1.0, 1.0, ALU.mult, ALU.add))
                link(v.scalar_tensor_tensor(slot_f[:], free[:], token[:, SEQS:SEQS + 1], psum[2][:, 0:TILES],
                                            ALU.mult, ALU.add))
                v.tensor_copy(slot[:, 0:TILES], slot_f[:]).then_inc(s_slots, 1)
                v.tensor_copy(slot[:, TILES:TILES + X_RING], token[:, SEQS:SEQS + 1].broadcast_to([P, X_RING]))

        S = {n: sem("c_" + n) for n in [f"x{i}" for i in range(X_RING)] + [f"added{i}" for i in range(Y_RING)] + [
            "slot_now", "x_ahead", "xT_full", "xT_read", "g_full", "u_full", "tanh", "g_read", "u_read", "aT_full", "aT_read", "y_full", "y_read"]}
        xT_bank, y_bank = psum[0], psum[1]
        g_bank, u_bank, aT_bank = psum[2:4], psum[4:6], psum[6:8]
        with nc.Fori(0, TILES // TPB) as it:
            with nc.Block() as block:
                @block.gpsimd
                def _(pool):
                    nc.gpsimd.tensor_copy(slot_now[:], slot[:, bass.ds(it * TPB, TPB + X_RING)]).then_inc(S["slot_now"], 1)
                    pool.wait_ge(S["slot_now"], 1)
                    for j in range(TPB):
                        pool.wait_ge(S["xT_full"], j + 1)
                        place = j % X_RING
                        if j + X_RING < TPB:
                            gather(slot_now, j + X_RING, place, S[f"x{place}"])
                        else:
                            gather(slot_now, TPB + place, place, S["x_ahead"])
                        pool.wait_ge(S["y_read"], j + 1)
                        if j >= 1:
                            pool.wait_ge(S[f"added{(j - 1) % Y_RING}"], 16 * ((j - 1) // Y_RING + 1))
                        nc.gpsimd.indirect_dma_start(a["out"], bass.IndirectOffsetOnAxis(ap=slot_now[:, j:j + 1], axis=0),
                                                     y[:, j % Y_RING, :], None, compute_op=ALU.add
                                                     ).then_inc(S[f"added{j % Y_RING}"], 16)
                    pool.wait_ge(S["x_ahead"], 16 * X_RING)
                    for i in range(Y_RING):
                        pool.wait_ge(S[f"added{i}"], 16 * ((TPB - 1 - i) // Y_RING + 1))

                @block.tensor
                def _(pe):
                    def transpose_x(j):
                        if j >= X_RING:
                            pe.wait_ge(S[f"x{j % X_RING}"], 16 * (j // X_RING))
                        if j >= 1:
                            pe.wait_ge(S["xT_read"], j)
                        for k in range(KD):
                            ins = nc.tensor.transpose(xT_bank[:, k * P:(k + 1) * P], x[:, j % X_RING, k * P:(k + 1) * P], ident[:])
                        ins.then_inc(S["xT_full"], 1)

                    def transpose_act(j):
                        pe.wait_ge(S["u_read"], j + 1)
                        if j >= 2:
                            pe.wait_ge(S["aT_read"], j - 1)
                        for k in range(KF):
                            ins = nc.tensor.transpose(aT_bank[j % 2][:, k * P:(k + 1) * P], act_t[:, j % 2, k * P:(k + 1) * P],
                                                      ident[:])
                        ins.then_inc(S["aT_full"], 1)

                    def gate(j, e):
                        pe.wait_ge(S["xT_read"], j + 1)
                        if j >= 2:
                            pe.wait_ge(S["u_read"], j - 1)
                        for k in range(KD):
                            ins = nc.tensor.matmul(g_bank[j % 2][:], xT[:, j % 2, k, :],
                                                   w_gate[:, bass.ds(e * (KD * FF) + k * FF, FF)],
                                                   start=(k == 0), stop=(k == KD - 1))
                        ins.then_inc(S["g_full"], 1)

                    def up(j, e):
                        for k in range(KD):
                            ins = nc.tensor.matmul(u_bank[j % 2][:], xT[:, j % 2, k, :],
                                                   w_up[:, bass.ds(e * (KD * FF) + k * FF, FF)],
                                                   start=(k == 0), stop=(k == KD - 1))
                        ins.then_inc(S["u_full"], 1)

                    def down(j, e):
                        pe.wait_ge(S["aT_read"], j + 1)
                        if j >= 1:
                            pe.wait_ge(S["y_read"], j)
                        for k in range(KF):
                            ins = nc.tensor.matmul(y_bank[:, 0:D], actT[:, j % 2, k, :],
                                                   w_down[:, bass.ds(e * (KF * D) + k * D, D)],
                                                   start=(k == 0), stop=(k == KF - 1))
                        ins.then_inc(S["y_full"], 1)

                    transpose_x(0)
                    e_before = e_now = None
                    for j in range(TPB + 1):
                        if j + 1 < TPB:
                            transpose_x(j + 1)
                        if j < TPB:
                            e_now = nc.tensor.value_load(owner[0:1, bass.ds(it * TPB + j, 1)], min_val=0, max_val=E - 1)
                            gate(j, e_now)
                        if j >= 1:
                            transpose_act(j - 1)
                        if j < TPB:
                            up(j, e_now)
                        if j >= 1:
                            down(j - 1, e_before)
                        e_before = e_now

                @block.scalar
                def _(act):
                    def copy_xT(j):
                        act.wait_ge(S["xT_full"], j + 1)
                        if j >= 2:
                            act.wait_ge(S["u_full"], j - 1)
                        nc.scalar.activation(xT[:, j % 2].rearrange("p k t -> p (k t)"), xT_bank[:, 0:D], ACT.Copy
                                             ).then_inc(S["xT_read"], 1)

                    copy_xT(0)
                    for j in range(TPB + 1):
                        if j + 1 < TPB:
                            copy_xT(j + 1)
                        if j < TPB:
                            act.wait_ge(S["g_full"], j + 1)
                            if j >= 2:
                                act.wait_ge(S["g_read"], j - 1)
                            nc.scalar.activation(th[:, j % 2, :], g_bank[j % 2][:], ACT.Tanh, scale=0.5
                                                 ).then_inc(S["tanh"], 1)
                        if j >= 1:
                            act.wait_ge(S["aT_full"], j)
                            if j >= 3:
                                act.wait_ge(S["y_full"], j - 2)
                            nc.scalar.activation(actT[:, (j - 1) % 2].rearrange("p k t -> p (k t)"), aT_bank[(j - 1) % 2][:],
                                                 ACT.Copy).then_inc(S["aT_read"], 1)

                @block.vector
                def _(dve):
                    for j in range(TPB + 1):
                        if j < TPB:
                            dve.wait_ge(S["tanh"], j + 1)
                            if j >= 2:
                                dve.wait_ge(S["aT_full"], j - 1)
                            t = act_t[:, j % 2, :]
                            nc.vector.scalar_tensor_tensor(t, th[:, j % 2, :], 1.0, g_bank[j % 2][:], ALU.add, ALU.mult
                                                           ).then_inc(S["g_read"], 1)
                            dve.wait_ge(S["g_read"], j + 1)
                            dve.wait_ge(S["u_full"], j + 1)
                            nc.vector.tensor_tensor(t, t, u_bank[j % 2][:], ALU.mult).then_inc(S["u_read"], 1)
                        if j >= 1:
                            dve.wait_ge(S["y_full"], j)
                            i = j - 1
                            if i >= Y_RING:
                                dve.wait_ge(S[f"added{i % Y_RING}"], 16 * (i // Y_RING))
                            nc.vector.tensor_scalar(y[:, i % Y_RING, :], y_bank[:, 0:D], 0.5, None, ALU.mult
                                                    ).then_inc(S["y_read"], 1)

            with nc.Block() as block:
                @block.gpsimd
                def _(pool):
                    pool.dma_reset()
                    for s in S.values():
                        pool.sem_clear(s)


X_RING = Y_RING = 3
TPB = 13
assert TILES % TPB == 0

IN_SHAPES = {"x": (TOKENS, D), "ctxT": (CS, TOKENS), "mask": (1, TOKENS), "w_in": (D, 2 * DI), "conv_w": (DI, 4),
             "conv_b": (P, KI), "w_x": (DI, RANK + 2 * NS), "w_dt": (RANK, DI), "b_dt": (P, KI), "a_log": (DI, NS),
             "d_param": (P, KI), "w_out": (DI, D), "w_srcT": (CS, 2 * D), "b_src": (1, 2 * D), "w_tgtT": (D, D),
             "b_tgt": (P, KD), "w_xoT": (2 * D, D), "b_xo": (1, D), "gate_w": (D, E), "sh_gate": (D, FF),
             "sh_up": (D, FF), "sh_down": (FF, D), "rt_gate": (E, D, FF), "rt_up": (E, D, FF), "rt_down": (E, FF, D)}


def decoder_layer(nc, a):
    a["b_rows"] = nc.dram_tensor("b_rows", (NS, 2 * GT), F32).ap()
    a["onehot"] = nc.dram_tensor("onehot", (GROUPS * P, GB * E), F32).ap()
    a["xs"] = nc.dram_tensor("xs", (TOKENS + P, D), F32).ap()
    with nc.sbuf_tensor("shared", [P, EXPERT_WORDS], F32) as shared:
        phase_a(nc, a, shared)
        route_and_run_experts(nc, a, shared)


def kernel(**inputs):
    import numpy as np
    import concourse.bacc as bacc
    from concourse.bass_utils import run_bass_kernel_spmd

    g = {n: np.asarray(v) for n, v in inputs.items()}
    columns = lambda v: v.reshape(-1, P).T
    host = {"x": g["x"].reshape(TOKENS, D), "ctxT": g["ctx_2048"].reshape(TOKENS, CS).T,
            "mask": g["mask_BxS2_fk1"].reshape(1, TOKENS), "w_in": g["L0_attn_W_in"],
            "conv_w": g["L0_attn_conv_w"].reshape(DI, 4), "conv_b": columns(g["L0_attn_conv_b"]),
            "w_x": g["L0_attn_W_x"], "w_dt": g["L0_attn_W_dt"], "b_dt": columns(g["L0_attn_b_dt"]),
            "a_log": g["L0_attn_A_log"], "d_param": columns(g["L0_attn_D_param"]), "w_out": g["L0_attn_W_out"],
            "w_srcT": g["L0_xattn_W_src"].T, "b_src": g["L0_xattn_b_src"].reshape(1, -1), "w_tgtT": g["L0_xattn_W_tgt"].T,
            "b_tgt": columns(g["L0_xattn_b_tgt"]), "w_xoT": g["L0_xattn_W_out"].T,
            "b_xo": g["L0_xattn_b_out"].reshape(1, -1), "gate_w": g["L0_ffn_gate_w"], "sh_gate": g["L0_ffn_sh_gate"],
            "sh_up": g["L0_ffn_sh_up"], "sh_down": g["L0_ffn_sh_down"], "rt_gate": g["L0_ffn_rt_gate"],
            "rt_up": g["L0_ffn_rt_up"], "rt_down": g["L0_ffn_rt_down"]}
    nc = bacc.Bacc("TRN2", target_bir_lowering=False, num_devices=1)
    arrays, a = {}, {}
    for name, shape in IN_SHAPES.items():
        arrays["in_" + name] = np.ascontiguousarray(host[name])
        a[name] = nc.dram_tensor("in_" + name, shape, F32, kind="ExternalInput").ap()
    a["out"] = nc.dram_tensor("out", (TOKENS + P, D), F32, kind="ExternalOutput").ap()
    decoder_layer(nc, a)
    r = run_bass_kernel_spmd(nc, [arrays], core_ids=[0])
    return r.results[0]["out"][0:TOKENS].reshape(SEQS, P, D)
```
